# Optimizing a Trainium2 kernel written in Bass

```python
import numpy as np
import jax
import jax.numpy as jnp

def _softmax(x, axis=-1):
    return jax.nn.softmax(x, axis=axis)

def _gelu(x):
    return jax.nn.gelu(x, approximate=True)

def _silu(x):
    return jax.nn.silu(x)

def _sigmoid(x):
    return jax.nn.sigmoid(x)

def _layernorm(x, axis=-1, eps=1e-05):
    m = jnp.mean(x, axis=axis, keepdims=True)
    v = jnp.var(x, axis=axis, keepdims=True)
    return (x - m) / jnp.sqrt(v + eps)

def _scatter_add(tgt, idx, src, axis=0):
    return tgt.at[idx].add(src)

def _segment_sum(src, seg, n):
    return jax.ops.segment_sum(src, seg, n)
kernel_name = 'mk_cond_seq_d2_seqx_r4_7568c9'

def setup_inputs(seed: int=0):
    np.random.seed(seed)
    _w = jnp.asarray

    def _rec_inputs():
        import jax
        import jax.numpy as jnp
        _rk = jax.random.key(seed)
        x = -0.0002928 + 1 * jax.random.normal(jax.random.fold_in(_rk, 1), (128, 64, 256), jnp.float32)
        _lenS = 64 - jax.random.randint(jax.random.fold_in(_rk, 7), (128,), 0, max(1, 64 // 4) + 1, jnp.int32)
        _lenS2 = 64 - jax.random.randint(jax.random.fold_in(_rk, 8), (128,), 0, max(1, 64 // 4) + 1, jnp.int32)
        cond_1024 = 0.0061147 + 1.02565 * jax.random.normal(jax.random.fold_in(_rk, 11), (128, 256), jnp.float32)
        return (x, cond_1024)
    x, cond_1024 = _rec_inputs()

    def _L0_cond_setup():
        import jax, jax.numpy as jnp
        import numpy as np
        EPS_LN = 1e-06
        EPS_NORM = 1e-12
        MAX_SCALE_MUL = float(np.log(100.0))
        H = 16

        def _ln(x):
            mu = jnp.mean(x, axis=-1, keepdims=True)
            var = jnp.mean((x - mu) ** 2, axis=-1, keepdims=True)
            return (x - mu) / jnp.sqrt(var + EPS_LN)

        def _l2norm(x):
            n = jnp.sqrt(jnp.sum(x * x, axis=-1, keepdims=True))
            return x / jnp.maximum(n, EPS_NORM)
        key = jax.random.key(seed)
        ks = jax.random.split(key, 12)
        B, L, C = (4, 256, 256)
        Ccond, Dff = (256, 1024)
        s = lambda fan: 1.0 / np.sqrt(fan)
        return {'x': jax.random.normal(ks[0], (B, L, C), jnp.float32), 'cond': jax.random.normal(ks[1], (B, Ccond), jnp.float32), 'mat_qkv_w': jax.random.normal(ks[2], (3 * C, C), jnp.float32) * s(C), 'q_bias': jnp.zeros((C,), jnp.float32), 'v_bias': jnp.zeros((C,), jnp.float32), 'scale_mul': jnp.full((1, H, 1, 1), np.log(4.0), jnp.float32), 'proj_w': jax.random.normal(ks[3], (C, C), jnp.float32) * s(C), 'proj_b': jnp.zeros((C,), jnp.float32), 'ada_w': jax.random.normal(ks[4], (6 * C, Ccond), jnp.float32) * s(Ccond), 'ada_b': jnp.zeros((6 * C,), jnp.float32), 'fc1_w': jax.random.normal(ks[5], (Dff, C), jnp.float32) * s(C), 'fc1_b': jnp.zeros((Dff,), jnp.float32), 'fc2_w': jax.random.normal(ks[6], (C, Dff), jnp.float32) * s(Dff), 'fc2_b': jnp.zeros((C,), jnp.float32)}
    _L0_cond_all = _L0_cond_setup()
    _L0_cond_in = {k: v for k, v in _L0_cond_all.items() if k in ('mat_qkv_w', 'q_bias', 'v_bias', 'scale_mul', 'proj_w', 'proj_b', 'ada_w', 'ada_b', 'fc1_w', 'fc1_b', 'fc2_w', 'fc2_b')}
    del _L0_cond_all

    def _L1_cond_setup():
        import jax, jax.numpy as jnp
        import numpy as np
        H = 16
        EPS = 1e-05

        def layer_norm(x, g, b):
            mu = jnp.mean(x, axis=-1, keepdims=True)
            var = jnp.var(x, axis=-1, keepdims=True)
            return (x - mu) * jax.lax.rsqrt(var + EPS) * g + b
        key = jax.random.key(seed)
        ks = jax.random.split(key, 8)
        B, T, D, TE = (4, 1024, 256, 256)
        s = 0.02
        return {'x': jax.random.normal(ks[0], (B, T, D), jnp.float32), 'emb': jax.random.normal(ks[1], (B, 1, TE), jnp.float32), 'gate_msa': jax.random.normal(ks[2], (B, 1, D), jnp.float32), 'norm_g': jnp.ones((D,), jnp.float32), 'norm_b': jnp.zeros((D,), jnp.float32), 'Wq': jax.random.normal(ks[3], (D, D), jnp.float32) * s, 'bq': jnp.zeros((D,), jnp.float32), 'Wk': jax.random.normal(ks[4], (D, D), jnp.float32) * s, 'bk': jnp.zeros((D,), jnp.float32), 'Wv': jax.random.normal(ks[5], (D, D), jnp.float32) * s, 'bv': jnp.zeros((D,), jnp.float32), 'emb_W': jax.random.normal(ks[6], (TE, 2 * D), jnp.float32) * s, 'emb_b': jnp.zeros((2 * D,), jnp.float32), 'sn_g': jnp.ones((D,), jnp.float32), 'sn_b': jnp.zeros((D,), jnp.float32), 'out_W': jax.random.normal(ks[7], (D, D), jnp.float32) * s, 'out_b': jnp.zeros((D,), jnp.float32)}
    _L1_cond_all = _L1_cond_setup()
    _L1_cond_in = {k: v for k, v in _L1_cond_all.items() if k in ('norm_g', 'norm_b', 'Wq', 'bq', 'Wk', 'bk', 'Wv', 'bv', 'emb_W', 'emb_b', 'sn_g', 'sn_b', 'out_W', 'out_b')}
    del _L1_cond_all
    return {'x': x, 'cond_1024': cond_1024, 'L0_cond_mat_qkv_w': _L0_cond_in['mat_qkv_w'], 'L0_cond_q_bias': _L0_cond_in['q_bias'], 'L0_cond_v_bias': _L0_cond_in['v_bias'], 'L0_cond_scale_mul': _L0_cond_in['scale_mul'], 'L0_cond_proj_w': _L0_cond_in['proj_w'], 'L0_cond_proj_b': _L0_cond_in['proj_b'], 'L0_cond_ada_w': _L0_cond_in['ada_w'], 'L0_cond_ada_b': _L0_cond_in['ada_b'], 'L0_cond_fc1_w': _L0_cond_in['fc1_w'], 'L0_cond_fc1_b': _L0_cond_in['fc1_b'], 'L0_cond_fc2_w': _L0_cond_in['fc2_w'], 'L0_cond_fc2_b': _L0_cond_in['fc2_b'], 'L1_cond_norm_g': _L1_cond_in['norm_g'], 'L1_cond_norm_b': _L1_cond_in['norm_b'], 'L1_cond_Wq': _L1_cond_in['Wq'], 'L1_cond_bq': _L1_cond_in['bq'], 'L1_cond_Wk': _L1_cond_in['Wk'], 'L1_cond_bk': _L1_cond_in['bk'], 'L1_cond_Wv': _L1_cond_in['Wv'], 'L1_cond_bv': _L1_cond_in['bv'], 'L1_cond_emb_W': _L1_cond_in['emb_W'], 'L1_cond_emb_b': _L1_cond_in['emb_b'], 'L1_cond_sn_g': _L1_cond_in['sn_g'], 'L1_cond_sn_b': _L1_cond_in['sn_b'], 'L1_cond_out_W': _L1_cond_in['out_W'], 'L1_cond_out_b': _L1_cond_in['out_b']}

def reference(x, cond_1024, L0_cond_mat_qkv_w, L0_cond_q_bias, L0_cond_v_bias, L0_cond_scale_mul, L0_cond_proj_w, L0_cond_proj_b, L0_cond_ada_w, L0_cond_ada_b, L0_cond_fc1_w, L0_cond_fc1_b, L0_cond_fc2_w, L0_cond_fc2_b, L1_cond_norm_g, L1_cond_norm_b, L1_cond_Wq, L1_cond_bq, L1_cond_Wk, L1_cond_bk, L1_cond_Wv, L1_cond_bv, L1_cond_emb_W, L1_cond_emb_b, L1_cond_sn_g, L1_cond_sn_b, L1_cond_out_W, L1_cond_out_b):
    import jax
    import jax.numpy as jnp

    def _L0_cond_ref(x, cond, mat_qkv_w, q_bias, v_bias, scale_mul, proj_w, proj_b, ada_w, ada_b, fc1_w, fc1_b, fc2_w, fc2_b):
        import jax, jax.numpy as jnp
        import numpy as np
        EPS_LN = 1e-06
        EPS_NORM = 1e-12
        MAX_SCALE_MUL = float(np.log(100.0))
        H = 16

        def _ln(x):
            mu = jnp.mean(x, axis=-1, keepdims=True)
            var = jnp.mean((x - mu) ** 2, axis=-1, keepdims=True)
            return (x - mu) / jnp.sqrt(var + EPS_LN)

        def _l2norm(x):
            n = jnp.sqrt(jnp.sum(x * x, axis=-1, keepdims=True))
            return x / jnp.maximum(n, EPS_NORM)
        B, L, C = x.shape
        hd = C // H
        ada = jax.nn.silu(cond) @ ada_w.T + ada_b
        ada = ada.reshape(B, 1, 6, C)
        gamma1, gamma2, scale1, scale2, shift1, shift2 = [ada[:, :, i] for i in range(6)]
        x1 = _ln(x) * (scale1 + 1.0) + shift1
        qkv_bias = jnp.concatenate([q_bias, jnp.zeros_like(q_bias), v_bias])
        qkv = (x1 @ mat_qkv_w.T + qkv_bias).reshape(B, L, 3, H, hd)
        q, k, v = [jnp.transpose(qkv[:, :, i], (0, 2, 1, 3)) for i in range(3)]
        sm = jnp.exp(jnp.minimum(scale_mul, MAX_SCALE_MUL))
        q = _l2norm(q) * sm
        k = _l2norm(k)
        scores = jnp.einsum('bhqd,bhkd->bhqk', q, k)
        probs = jax.nn.softmax(scores, axis=-1)
        o = jnp.einsum('bhqk,bhkd->bhqd', probs, v)
        o = jnp.transpose(o, (0, 2, 1, 3)).reshape(B, L, C)
        attn_out = o @ proj_w.T + proj_b
        x = x + attn_out * gamma1
        x2 = _ln(x) * (scale2 + 1.0) + shift2
        h = jax.nn.gelu(x2 @ fc1_w.T + fc1_b, approximate=False)
        ffn_out = h @ fc2_w.T + fc2_b
        x = x + ffn_out * gamma2
        return x

    def _L1_cond_ref(x, emb, gate_msa, norm_g, norm_b, Wq, bq, Wk, bk, Wv, bv, emb_W, emb_b, sn_g, sn_b, out_W, out_b):
        import jax, jax.numpy as jnp
        import numpy as np
        H = 16
        EPS = 1e-05

        def layer_norm(x, g, b):
            mu = jnp.mean(x, axis=-1, keepdims=True)
            var = jnp.var(x, axis=-1, keepdims=True)
            return (x - mu) * jax.lax.rsqrt(var + EPS) * g + b
        B, T, D = x.shape
        dh = D // H
        xn = layer_norm(x, norm_g, norm_b)
        q = (xn @ Wq + bq).reshape(B, T, H, dh)
        k = (xn @ Wk + bk).reshape(B, T, H, dh)
        v = (xn @ Wv + bv).reshape(B, T, H, dh)
        q = jax.nn.softmax(q, axis=-1)
        k = jax.nn.softmax(k, axis=1)
        ctx = jnp.einsum('bnhd,bnhl->bhdl', k, v)
        y = jnp.einsum('bnhd,bhdl->bnhl', q, ctx).reshape(B, T, D)
        emb_out = jax.nn.silu(emb) @ emb_W + emb_b
        scale, shift = jnp.split(emb_out, 2, axis=-1)
        h = layer_norm(y, sn_g, sn_b) * (1.0 + scale) + shift
        h = jax.nn.silu(h) @ out_W + out_b
        return x + gate_msa * h
    x = _L0_cond_ref(x, cond_1024, L0_cond_mat_qkv_w, L0_cond_q_bias, L0_cond_v_bias, L0_cond_scale_mul, L0_cond_proj_w, L0_cond_proj_b, L0_cond_ada_w, L0_cond_ada_b, L0_cond_fc1_w, L0_cond_fc1_b, L0_cond_fc2_w, L0_cond_fc2_b)
    x = _L1_cond_ref(x, cond_1024[:, None, :], cond_1024[:, None, :], L1_cond_norm_g, L1_cond_norm_b, L1_cond_Wq, L1_cond_bq, L1_cond_Wk, L1_cond_bk, L1_cond_Wv, L1_cond_bv, L1_cond_emb_W, L1_cond_emb_b, L1_cond_sn_g, L1_cond_sn_b, L1_cond_out_W, L1_cond_out_b)
    return x

_drawn_inputs = setup_inputs


def setup_inputs(seed=0):
    import zlib

    import numpy as np

    out = dict(_drawn_inputs(seed))
    spreads = {'L0_cond_q_bias': (0.0, 0.783),
     'L0_cond_v_bias': (0.0, 0.1),
     'L0_cond_scale_mul': (1.3862943649291992, 0.2),
     'L0_cond_proj_b': (0.0, 0.1),
     'L0_cond_ada_b': (0.0, 0.1),
     'L0_cond_fc1_b': (0.0, 0.1),
     'L0_cond_fc2_b': (0.0, 0.1),
     'L1_cond_norm_g': (1.0, 0.555),
     'L1_cond_norm_b': (0.0, 0.33),
     'L1_cond_bq': (0.0, 0.8),
     'L1_cond_bk': (0.0, 2.0),
     'L1_cond_bv': (0.0, 0.1),
     'L1_cond_emb_b': (0.0, 0.333),
     'L1_cond_sn_g': (1.0, 0.2),
     'L1_cond_sn_b': (0.0, 0.495),
     'L1_cond_out_b': (0.0, 0.1)}
    factors = {'L1_cond_Wq': 8.0, 'L1_cond_Wk': 8.0}
    for name, (base, spread) in spreads.items():
        noise = np.random.default_rng([zlib.crc32(name.encode()), seed]).standard_normal(out[name].shape)
        drawn = base * np.exp(spread * noise) if base else spread * noise
        out[name] = jnp.asarray(drawn.astype(out[name].dtype))
    for name, factor in factors.items():
        out[name] = (out[name] * factor).astype(out[name].dtype)
    return out
```

```python
import math
from contextlib import ExitStack

import numpy as np

import concourse.bass as bass
from concourse import mybir

ALU = mybir.AluOpType
ACT = mybir.ActivationFunctionType
F32 = mybir.dt.float32
BF16 = mybir.dt.bfloat16
X_AXIS = mybir.AxisListType.X

P = 128
B, L, C = 128, 64, 256
H = 16
HD = C // H
D_FF = 1024
NC_ = C // P
SEQ = P // L
TILES = B // SEQ
UNROLL = 4
GROUPS = TILES // UNROLL
HPC = P // HD
G_ = HPC // 2
HI, LO = 0, 1
LOG_100 = math.log(100.0)
LN2 = math.log(2.0)


class Tile:

    def __init__(self, j, u, unroll=UNROLL):
        self.j, self.u = j + u // unroll, u % unroll
        self.n = self.j * unroll + self.u

    def slot(self, slots):
        return self.u % slots

    def since(self, slots, each=1):
        if isinstance(self.n, int) and self.n < slots:
            return None
        return (self.n + 1 - slots) * each

    def rows(self, x):
        return x[:, bass.ds(self.j, 1), self.u]


def pipeline(eng, stages, tiles=TILES, unroll=UNROLL, reach=4):
    deepest = max(lag for lag, _ in stages)
    ahead = min(lag for lag, _ in stages)
    first = -(-(deepest + reach) // unroll)
    last = tiles // unroll + ahead // unroll

    def step(j, u, known):
        for lag, stage in stages:
            if known and not 0 <= unroll * j + u - lag < tiles:
                continue
            stage(Tile(j, u - lag, unroll))

    for s in range(unroll * (ahead // unroll), unroll * first):
        step(0, s, True)
    with eng.Fori(first, last) as j:
        for u in range(unroll):
            step(j, u, False)
    for s in range(unroll * last, tiles + deepest):
        step(0, s, True)


def condition_kernel(nc, x, cond, qkv_w, q_bias, v_bias, scale_mul, proj_w, proj_b, ada_w, ada_b,
                     fc1_w, fc1_b, fc2_w, fc2_b, norm_g, norm_b, wq, bq, wk, bk, wv, bv,
                     emb_w, emb_b, sn_g, sn_b, out_w, out_b, out):
    with ExitStack() as ctx:
        m = Shared(nc, ctx)
        setup(nc, m, x, cond, qkv_w, q_bias, v_bias, scale_mul, proj_w, proj_b, ada_w, ada_b,
              fc1_w, fc1_b, fc2_w, fc2_b, norm_g, norm_b, wq, bq, wk, bk, wv, bv,
              emb_w, emb_b, sn_g, sn_b, out_w, out_b)
        attention_pass(nc, m, x)
        feed_forward_pass(nc, m)
        linear_pass(nc, m, cond, out)


class Shared:

    def __init__(self, nc, ctx):
        def sb(name, shape, dt):
            return ctx.enter_context(nc.sbuf_tensor(name, shape, dt))

        self.x_all = sb("x_all", [P, GROUPS, UNROLL, C], F32)
        self.ident = sb("ident", [P, P], F32)
        self.minus_half = sb("minus_half", [P, UNROLL], F32)
        self.eps_norm3 = sb("eps_norm3", [P, 1], F32)
        self.eps_ln = sb("eps_ln", [P, 1], F32)
        self.scale1, self.shift1, self.scale2, self.shift2, self.scale3, self.shift3 = (
            sb(n, [P, NC_, B], F32) for n in ("scale1", "shift1", "scale2", "shift2", "scale3", "shift3"))
        self.gammas = nc.dram_tensor("gammas", [B, 2 * C], F32, kind="Internal").ap()
        self.w_qkv = sb("w_qkv", [P, NC_, 3 * C], F32)
        self.w_proj = sb("w_proj", [P, NC_, C], F32)
        self.w_fc1 = sb("w_fc1", [P, 2, NC_, D_FF], BF16)
        self.w_fc2 = sb("w_fc2", [P, 2, D_FF // P, C], BF16)
        self.w_qv3 = sb("w_qv3", [P, NC_, 2 * C], F32)
        self.w_k3 = sb("w_k3", [P, NC_, C], F32)
        self.w_out3 = sb("w_out3", [P, NC_, C], F32)
        self.b_qkv = sb("b_qkv", [P, 3 * C], F32)
        self.b_proj = sb("b_proj", [P, C], F32)
        self.b_fc2 = sb("b_fc2", [P, C], F32)
        self.b_qv3 = sb("b_qv3", [P, 2 * C], F32)
        self.b_out3 = sb("b_out3", [P, C], F32)
        self.b_fc1 = sb("b_fc1", [P, D_FF // P], F32)
        self.b_k3 = sb("b_k3", [P, NC_], F32)
        self.g_norm3 = sb("g_norm3", [P, NC_], F32)
        self.b_norm3 = sb("b_norm3", [P, NC_], F32)
        self.norm_weight = sb("norm_weight", [P, 2 * H], F32)
        self.log_256 = sb("log_256", [P, 1], F32)
        self.minus_shift = sb("minus_shift", [P, 1], F32)
        self.same_head = sb("same_head", [P, P], F32)


def setup(nc, m, x, cond, qkv_w, q_bias, v_bias, scale_mul, proj_w, proj_b, ada_w, ada_b,
          fc1_w, fc1_b, fc2_w, fc2_b, norm_g, norm_b, wq, bq, wk, bk, wv, bv,
          emb_w, emb_b, sn_g, sn_b, out_w, out_b):
    chunked = "(c p) n -> p c n"
    with ExitStack() as ctx:
        def sb(name, shape, dt=F32):
            return ctx.enter_context(nc.sbuf_tensor(name, shape, dt))

        def sem(name):
            return ctx.enter_context(nc.semaphore(name))

        cond_sb = sb("cond_sb", [P, C])
        cond_act = sb("cond_act", [P, C])
        cond_t = sb("cond_t", [P, NC_, B])
        w_ada = sb("w_ada", [P, NC_, 6 * C])
        w_emb = sb("w_emb", [P, NC_, 2 * C])
        b_ada_row = sb("b_ada_row", [P, 2 * C])
        b_ada = sb("b_ada", [P, 6 * NC_])
        b_emb = sb("b_emb", [P, 2 * NC_])
        g_sn = sb("g_sn", [P, NC_])
        b_sn = sb("b_sn", [P, NC_])
        fc1_full = sb("fc1_full", [P, NC_, D_FF])
        fc2_full = sb("fc2_full", [P, D_FF // P, C])
        gamma_rows = sb("gamma_rows", [P, 2 * C])
        head_scale = sb("head_scale", [P, H])
        head_exp = sb("head_exp", [P, H])
        top = sb("top", [P, 1])
        scale_plus = sb("scale_plus", [P, NC_, B])
        out_w_full = sb("out_w_full", [P, NC_, C])
        band = sb("band", [P, P])
        ps = [ctx.enter_context(nc.psum_tensor(f"set_ps{i}", [P, 512], F32)) for i in range(6)]

        cond_here = sem("cond_here")
        heads_here = sem("heads_here")
        ada_here = sem("ada_here")
        ff_here = sem("ff_here")
        out_w_here = sem("out_w_here")
        others_here = sem("others_here")
        silu_done = sem("silu_done")
        exp_done = sem("exp_done")
        hi_done = sem("hi_done")
        consts_made = sem("consts_made")
        heads_made = sem("heads_made")
        transposed = sem("transposed")
        cond_t_made = sem("cond_t_made")
        products = sem("products")
        modulations = sem("modulations")
        gammas_made = sem("gammas_made")
        gammas_stored = sem("gammas_stored")
        N_OTHERS = 18
        block = ctx.enter_context(nc.Block())

        @block.sync
        def _(sp):
            sp.dma_start(cond_sb[:], cond).then_inc(cond_here, 16)
            sp.dma_start(head_scale[:], scale_mul.rearrange("a h b c -> (a b c) h").to_broadcast([P, H])
                         ).then_inc(heads_here, 16)
            sp.dma_start(w_ada[:], ada_w.rearrange(chunked, p=P)).then_inc(ada_here, 16)
            sp.dma_start(w_emb[:], emb_w.rearrange(chunked, p=P)).then_inc(ada_here, 16)
            sp.dma_start(b_ada_row[:], ada_b[None, 0:2 * C].to_broadcast([P, 2 * C])).then_inc(ada_here, 16)
            sp.dma_start(b_ada[:], ada_b.rearrange("(k p) -> p k", p=P), allow_slow_non_contiguous=True).then_inc(ada_here, 16)
            sp.dma_start(b_emb[:], emb_b.rearrange("(k p) -> p k", p=P), allow_slow_non_contiguous=True).then_inc(ada_here, 16)
            sp.dma_start(g_sn[:], sn_g.rearrange("(k p) -> p k", p=P), allow_slow_non_contiguous=True).then_inc(ada_here, 16)
            sp.dma_start(b_sn[:], sn_b.rearrange("(k p) -> p k", p=P), allow_slow_non_contiguous=True).then_inc(ada_here, 16)
            sp.dma_start(fc1_full[:], fc1_w.rearrange(chunked, p=P)).then_inc(ff_here, 16)
            sp.dma_start(fc2_full[:], fc2_w.rearrange(chunked, p=P)).then_inc(ff_here, 16)
            sp.wait_ge(gammas_made, 1)
            sp.dma_start(m.gammas, gamma_rows[:]).then_inc(gammas_stored, 16)
            sp.wait_ge(gammas_stored, 16)
            sp.wait_ge(others_here, 16 * N_OTHERS)

        @block.scalar
        def _(act):
            def row(a):
                return a[None, :].to_broadcast([P, C])

            act.dma_start(out_w_full[:], out_w.rearrange(chunked, p=P)).then_inc(out_w_here, 16)
            others = [
                (m.w_qkv[:], qkv_w.rearrange(chunked, p=P)), (m.w_proj[:], proj_w.rearrange(chunked, p=P)),
                (m.w_qv3[:, :, 0:C], wq.rearrange(chunked, p=P)), (m.w_qv3[:, :, C:2 * C], wv.rearrange(chunked, p=P)),
                (m.w_k3[:], wk.rearrange(chunked, p=P)),
                (m.b_qkv[:, 0:C], row(q_bias)), (m.b_qkv[:, 2 * C:3 * C], row(v_bias)),
                (m.b_proj[:], row(proj_b)), (m.b_fc2[:], row(fc2_b)),
                (m.b_qv3[:, 0:C], row(bq)), (m.b_qv3[:, C:2 * C], row(bv)), (m.b_out3[:], row(out_b)),
                (m.b_fc1[:], fc1_b.rearrange("(k p) -> p k", p=P)), (m.b_k3[:], bk.rearrange("(k p) -> p k", p=P)),
                (m.g_norm3[:], norm_g.rearrange("(k p) -> p k", p=P)),
                (m.b_norm3[:], norm_b.rearrange("(k p) -> p k", p=P)),
                (m.x_all[:, 0:GROUPS // 2], x_tiles(x)[:, 0:GROUPS // 2]),
                (m.x_all[:, GROUPS // 2:], x_tiles(x)[:, GROUPS // 2:]),
            ]
            assert len(others) == N_OTHERS
            for to, source in others:
                act.dma_start(to, source, allow_slow_non_contiguous=True).then_inc(others_here, 16)
            act.wait_ge(cond_here, 16)
            act.activation(cond_act[:], cond_sb[:], ACT.Silu).then_inc(silu_done, 1)
            act.wait_ge(heads_made, 1)
            act.activation(head_exp[:], head_scale[:], ACT.Exp).then_inc(exp_done, 1)
            act.wait_ge(consts_made, 8)
            act.activation(m.norm_weight[:, 0:H], head_scale[:], ACT.Exp, scale=-2.0)
            act.wait_ge(ff_here, 32)
            act.activation(m.w_fc1[:, HI], fc1_full[:], ACT.Copy).then_inc(hi_done, 1)
            act.activation(m.w_fc2[:, HI], fc2_full[:], ACT.Copy).then_inc(hi_done, 1)

        @block.gpsimd
        def _(pool):
            pool.memset(m.ident[:], 0.0).then_inc(consts_made, 1)
            pool.memset(m.minus_half[:], -0.5).then_inc(consts_made, 1)
            pool.memset(m.b_qkv[:, C:2 * C], 0.0).then_inc(consts_made, 1)
            pool.memset(m.log_256[:], 8 * LN2).then_inc(consts_made, 1)
            pool.memset(m.norm_weight[:], 1.0).then_inc(consts_made, 1)
            pool.memset(m.eps_norm3[:], 1e-5).then_inc(consts_made, 1)
            pool.memset(m.eps_ln[:], 1e-6).then_inc(consts_made, 1)
            pool.memset(m.same_head[:], 1.0).then_inc(consts_made, 1)
            pool.wait_ge(consts_made, 8)
            pool.affine_select(out=m.ident[:], in_=m.ident[:], compare_op=ALU.not_equal, fill=1.0, base=0,
                               pattern=[[-1, P]], channel_multiplier=1).then_inc(consts_made, 1)
            pool.affine_select(out=band[:].rearrange("p (h e) -> p h e", e=HD),
                               in_=m.same_head[:].rearrange("p (h e) -> p h e", e=HD), compare_op=ALU.is_ge, fill=0.0,
                               base=0, pattern=[[-HD, HPC], [0, HD]], channel_multiplier=1).then_inc(consts_made, 1)
            pool.wait_ge(consts_made, 10)
            pool.affine_select(out=m.same_head[:].rearrange("p (h e) -> p h e", e=HD),
                               in_=band[:].rearrange("p (h e) -> p h e", e=HD), compare_op=ALU.is_ge, fill=0.0,
                               base=HD - 1, pattern=[[HD, HPC], [0, HD]], channel_multiplier=-1).then_inc(consts_made, 1)
            pool.wait_ge(consts_made, 11)

        @block.tensor
        def _(pe):
            pe.wait_ge(consts_made, 9)
            pe.wait_ge(silu_done, 1)
            for c in range(NC_):
                last = pe.transpose(ps[0][:, c * P:(c + 1) * P], cond_act[:, c * P:(c + 1) * P], m.ident[:])
            last.then_inc(transposed, 1)
            pe.wait_ge(cond_t_made, 1)
            pe.wait_ge(ada_here, 16 * 7)
            for c in range(NC_):
                last = pe.matmul(ps[1][:, :], cond_t[:, c, :], w_ada[:, c, 0:2 * C], start=(c == 0), stop=(c == NC_ - 1))
            last.then_inc(products, 1)
            for k in range(8):
                for c in range(NC_):
                    last = pe.matmul(ps[2 + k // 4][:, (k % 4) * B:(k % 4 + 1) * B],
                                     w_ada[:, c, 2 * C + k * P:2 * C + (k + 1) * P], cond_t[:, c, :],
                                     start=(c == 0), stop=(c == NC_ - 1))
            last.then_inc(products, 1)
            for k in range(4):
                for c in range(NC_):
                    last = pe.matmul(ps[4][:, k * B:(k + 1) * B], w_emb[:, c, k * P:(k + 1) * P], cond_t[:, c, :],
                                     start=(c == 0), stop=(c == NC_ - 1))
            last.then_inc(products, 1)

        @block.vector
        def _(dve):
            dve.wait_ge(heads_here, 16)
            dve.tensor_scalar(head_scale[:], head_scale[:], LOG_100, None, ALU.min).then_inc(heads_made, 1)
            dve.wait_ge(heads_made, 1)
            dve.wait_ge(exp_done, 1)
            dve.tensor_reduce(top[:], head_exp[:], X_AXIS, ALU.max).then_inc(heads_made, 1)
            dve.wait_ge(heads_made, 2)
            dve.tensor_scalar(top[:], top[:], -80.0, 0.0, ALU.add, ALU.max).then_inc(heads_made, 1)
            dve.wait_ge(heads_made, 3)
            dve.tensor_scalar(m.minus_shift[:], top[:], -1.0, None, ALU.mult)
            dve.wait_ge(transposed, 1)
            dve.tensor_copy(cond_t[:], ps[0][:, 0:NC_ * B].rearrange("p (c b) -> p c b", c=NC_)).then_inc(cond_t_made, 1)
            dve.wait_ge(ada_here, 16 * 7)
            dve.wait_ge(products, 1)
            dve.tensor_tensor(gamma_rows[:], ps[1][:], b_ada_row[:], ALU.add).then_inc(gammas_made, 1)
            dve.wait_ge(products, 2)
            for k, (to, one) in enumerate(((m.scale1, 1.0), (m.scale2, 1.0), (m.shift1, 0.0), (m.shift2, 0.0))):
                for c in range(NC_):
                    i = k * NC_ + c
                    dve.tensor_scalar(to[:, c, :], ps[2 + i // 4][:, (i % 4) * B:(i % 4 + 1) * B],
                                      b_ada[:, 2 * NC_ + i:2 * NC_ + i + 1], one, ALU.add, ALU.add)
            dve.wait_ge(products, 3)
            for c in range(NC_):
                dve.tensor_scalar(scale_plus[:, c, :], ps[4][:, c * B:(c + 1) * B], b_emb[:, c:c + 1], 1.0,
                                  ALU.add, ALU.add).then_inc(modulations, 1)
                dve.tensor_scalar(m.shift3[:, c, :], ps[4][:, (NC_ + c) * B:(NC_ + c + 1) * B],
                                  b_emb[:, NC_ + c:NC_ + c + 1], None, ALU.add).then_inc(modulations, 1)
            dve.wait_ge(modulations, 4)
            for c in range(NC_):
                dve.tensor_scalar(m.scale3[:, c, :], scale_plus[:, c, :], g_sn[:, c:c + 1], None, ALU.mult)
                dve.scalar_tensor_tensor(m.shift3[:, c, :], scale_plus[:, c, :], b_sn[:, c:c + 1], m.shift3[:, c, :],
                                         ALU.mult, ALU.add)
            dve.wait_ge(out_w_here, 16)
            dve.tensor_scalar(m.w_out3[:], out_w_full[:], 0.5, None, ALU.mult)
            dve.wait_ge(hi_done, 1)
            dve.tensor_tensor(m.w_fc1[:, LO], fc1_full[:], m.w_fc1[:, HI], ALU.subtract)
            dve.wait_ge(hi_done, 2)
            dve.tensor_tensor(m.w_fc2[:, LO], fc2_full[:], m.w_fc2[:, HI], ALU.subtract)


def x_tiles(x):
    return x.rearrange("(j u s) l c -> (s l) j u c", s=SEQ, u=UNROLL)


def reuse(eng, sem, tile, slots, each=1):
    count = tile.since(slots, each)
    if count is not None:
        eng.wait_ge(sem, count)


def bank_free(eng, sem, tile, offset, each=1):
    n = tile.n + offset
    if isinstance(n, int):
        if n < 0:
            return
        n = min(n, TILES - 1)
    eng.wait_ge(sem, (n + 1) * each)


def attention_pass(nc, m, x):
    PAIRS = H // 2
    VW = HD + 1
    with ExitStack() as ctx:
        def sb(name, shape, dt=F32, slots=2):
            return [ctx.enter_context(nc.sbuf_tensor(f"{name}{i}", shape, dt)) for i in range(slots)]

        def sem(name):
            return ctx.enter_context(nc.semaphore(name))

        stats = sb("stats", [P, 6])
        mean_var = sb("mean_var", [P, 2])
        rstd = sb("rstd", [P, 1])
        x_hat = sb("x_hat", [P, C])
        x1_t = sb("x1_t", [P, NC_, P])
        qk = sb("qk", [P, 2 * C])
        v_full = sb("v_full", [P, C])
        v_split = sb("v_split", [P, 2, PAIRS, 2, HD], BF16)
        v_pairs = sb("v_pairs", [P, SEQ, 2, 2, PAIRS, VW], BF16, 4)
        squares = sb("squares", [P, 2 * C])
        norms = sb("norms", [P, 2 * H])
        log_norms = sb("log_norms", [P, 2 * H])
        factors = sb("factors", [P, 2 * H])
        qk_hat = sb("qk_hat", [P, 2 * C])
        qk_t = sb("qk_t", [P, 2, 2, NC_, P], BF16)
        k_pairs = sb("k_pairs", [P, 2, NC_, SEQ, G_, 2, L], BF16)
        e_full = sb("e_full", [P, SEQ, PAIRS, L])
        e_split = sb("e_split", [P, 2, SEQ, PAIRS, L], BF16)
        inv_sum = sb("inv_sum", [P, SEQ, PAIRS // 2, 2])
        o_full = sb("o_full", [P, C])
        o_t = sb("o_t", [P, NC_, P])
        gain = sb("gain", [P, C], F32, 4)
        branch = sb("branch", [P, C])

        ps_x = ctx.enter_context(nc.psum_tensor("ps_x", [P, 512], F32))
        ps_qk = ctx.enter_context(nc.psum_tensor("ps_qk", [P, 512], F32))
        ps_v = ctx.enter_context(nc.psum_tensor("ps_v", [P, 512], F32))
        ps_qkt = ctx.enter_context(nc.psum_tensor("ps_qkt", [P, 512], F32))
        ps_s = ctx.enter_context(nc.psum_tensor("ps_s", [P, SEQ, PAIRS, L], F32))
        ps_o = ctx.enter_context(nc.psum_tensor("ps_o", [P, SEQ, 512], F32))

        o_blocks = ps_o[:, :, 0:PAIRS // 2 * 4 * VW].rearrange(
            "p s (k g r e) -> p s k g r e", k=PAIRS // 2, g=2, r=2)
        ps_xt, ps_ot = ps_x[:, 0:C], ps_x[:, C:2 * C]
        ps_vv, ps_y = ps_v[:, 0:C], ps_v[:, C:2 * C]

        gain_here = [sem(f"gain_here{i}") for i in range(4)]
        k_pairs_here = [sem(f"k_pairs_here{i}") for i in range(2)]
        cleared = sem("cleared")
        ones_set = sem("ones_set")
        stats_made = sem("stats_made")
        mean_made = sem("mean_made")
        var_eps_made = sem("var_eps_made")
        rstd_made = sem("rstd_made")
        x_hat_made = sem("x_hat_made")
        x_hat_t = sem("x_hat_t")
        x1_made = sem("x1_made")
        qkv_done = sem("qkv_done")
        qk_biased = sem("qk_biased")
        v_biased = sem("v_biased")
        v_hi_made = sem("v_hi_made")
        v_lo_made = sem("v_lo_made")
        v_placed = sem("v_placed")
        squared = sem("squared")
        norms_made = sem("norms_made")
        norms_weighted = sem("norms_weighted")
        logs_made = sem("logs_made")
        factors_made = sem("factors_made")
        qk_hat_made = sem("qk_hat_made")
        qk_turned = sem("qk_turned")
        qk_hi_made = sem("qk_hi_made")
        qk_lo_made = sem("qk_lo_made")
        scores_done = sem("scores_done")
        exp_made = sem("exp_made")
        e_hi_made = sem("e_hi_made")
        e_lo_made = sem("e_lo_made")
        pv_done = sem("pv_done")
        sums_inverted = sem("sums_inverted")
        o_made = sem("o_made")
        o_turned = sem("o_turned")
        o_t_made = sem("o_t_made")
        proj_done = sem("proj_done")
        branch_made = sem("branch_made")
        branch_gained = sem("branch_gained")
        x_updated = sem("x_updated")
        block = ctx.enter_context(nc.Block())
        gamma1 = m.gammas.rearrange("(j u s) n -> s j u n", s=SEQ, u=UNROLL)

        @block.sync
        def _(sp):
            def load_gain(t):
                for s in range(SEQ):
                    source = gamma1[s:s + 1, bass.ds(t.j, 1), t.u, 0:C]
                    sp.dma_start(gain[t.slot(4)][s * L:(s + 1) * L, :],
                                 source.rearrange("s j n -> (s j) n").to_broadcast([L, C])
                                 ).then_inc(gain_here[t.slot(4)], 16)

            def place_k(t):
                if t.since(2) is None:
                    sp.wait_ge(cleared, 6)
                sp.wait_ge(qk_lo_made, t.n + 1)
                a = t.slot(2)
                for g in range(G_):
                    for r in range(2):
                        rows = slice((2 * g + r) * HD, (2 * g + r + 1) * HD)
                        sp.dma_start(
                            k_pairs[a][rows, :, :, :, g, r, :].rearrange("p a c s k -> p (a c s) k"),
                            qk_t[a][rows, 1].rearrange("p a c (s k) -> p (a c s) k", s=SEQ)
                        ).then_inc(k_pairs_here[a], 16)

            pipeline(sp, [(3, place_k), (5, load_gain)])
            sp.wait_ge(x_updated, TILES)

        @block.gpsimd
        def _(pool):
            for a in range(2):
                pool.memset(k_pairs[a][:], 0.0).then_inc(cleared, 1)
            for a in range(4):
                pool.memset(v_pairs[a][:], 0.0).then_inc(cleared, 1)
            pool.wait_ge(cleared, 6)
            for a in range(4):
                for r in range(2):
                    pool.memset(v_pairs[a][r * L:(r + 1) * L, :, HI, r, :, HD:VW], 1.0).then_inc(ones_set, 1)
            pool.wait_ge(ones_set, 8)

            def rstd_of(t):
                a = t.slot(2)
                reuse(pool, x_hat_made, t, 2)
                pool.wait_ge(mean_made, t.n + 1)
                pool.tensor_tensor(rstd[a][:], mean_var[a][:, 1:2], m.eps_ln[:], ALU.add).then_inc(var_eps_made, 1)
                pool.wait_ge(var_eps_made, t.n + 1)
                pool.tensor_tensor(rstd[a][:], rstd[a][:], m.minus_half[:, 0:1], ALU.pow).then_inc(rstd_made, 1)

            def normalise(t):
                a = t.slot(2)
                pool.wait_ge(factors_made, t.n + 1)
                reuse(pool, qk_turned, t, 2)
                pool.tensor_tensor(heads(qk_hat[a][:]), heads(qk[a][:]), over_channels(factors[a][:]), ALU.mult
                                   ).then_inc(qk_hat_made, 1)

            def update(t):
                a = t.slot(2)
                pool.wait_ge(branch_made, t.n + 1)
                pool.wait_ge(gain_here[t.slot(4)], (t.j + 1) * 16 * SEQ)
                pool.tensor_tensor(branch[a][:], branch[a][:], gain[t.slot(4)][:], ALU.mult).then_inc(branch_gained, 1)

            def add(t):
                a = t.slot(2)
                pool.wait_ge(branch_gained, t.n + 1)
                pool.tensor_tensor(t.rows(m.x_all), t.rows(m.x_all), branch[a][:, None, :], ALU.add
                                   ).then_inc(x_updated, 1)

            def e_lo(t):
                a = t.slot(2)
                pool.wait_ge(e_hi_made, t.n + 1)
                reuse(pool, pv_done, t, 2)
                pool.tensor_tensor(flat(e_split[a][:, LO]), flat(e_full[a][:]), flat(e_split[a][:, HI]), ALU.subtract
                                   ).then_inc(e_lo_made, 1)

            pipeline(pool, [(7, update), (3, normalise), (7, add),
                            (0, rstd_of), (4, e_lo)])

        @block.scalar
        def _(act):
            def square(t):
                a = t.slot(2)
                act.wait_ge(qk_biased, t.n + 1)
                reuse(act, norms_made, t, 2)
                act.activation(squares[a][:], qk[a][:], ACT.Square).then_inc(squared, 1)

            def v_hi(t):
                a = t.slot(2)
                act.wait_ge(v_biased, t.n + 1)
                reuse(act, v_placed, t, 2)
                act.activation(v_split[a][:, HI].rearrange("p k r e -> p (k r e)"), v_full[a][:], ACT.Copy
                               ).then_inc(v_hi_made, 1)

            def logs(t):
                a = t.slot(2)
                act.wait_ge(norms_weighted, t.n + 1)
                reuse(act, factors_made, t, 2)
                act.activation(log_norms[a][:], norms[a][:], ACT.Ln, scale=65536.0).then_inc(logs_made, 1)

            def factor(t):
                a = t.slot(2)
                act.wait_ge(logs_made, t.n + 1)
                reuse(act, qk_hat_made, t, 2)
                act.activation(factors[a][:], log_norms[a][:], ACT.Exp, bias=m.log_256[:], scale=-0.5).then_inc(factors_made, 1)

            def qk_hi(t):
                a = t.slot(2)
                act.wait_ge(qk_turned, t.n + 1)
                reuse(act, scores_done, t, 2)
                act.activation(qk_t[a][:, :, HI].rearrange("p w c k -> p w (c k)"),
                               ps_qkt[:, :].rearrange("p (w k) -> p w k", w=2), ACT.Copy).then_inc(qk_hi_made, 1)

            def exponentials(t):
                a = t.slot(2)
                act.wait_ge(scores_done, t.n + 1)
                reuse(act, e_lo_made, t, 2)
                act.activation(flat(e_full[a][:]), flat(ps_s[:]), ACT.Exp, bias=m.minus_shift[:]).then_inc(exp_made, 1)

            def o_copy(t):
                a = t.slot(2)
                act.wait_ge(o_turned, t.n + 1)
                reuse(act, proj_done, t, 2)
                act.activation(o_t[a][:].rearrange("p c k -> p (c k)"), ps_ot, ACT.Copy).then_inc(o_t_made, 1)

            pipeline(act, [(3, square), (6, o_copy), (3, v_hi), (3, logs), (3, factor), (4, exponentials), (3, qk_hi)])

        @block.tensor
        def _(pe):
            def project(t):
                a = t.slot(2)
                pe.wait_ge(o_t_made, t.n + 1)
                reuse(pe, branch_made, t, 1)
                bank_free(pe, v_biased, t, 4)
                for c in range(NC_):
                    last = pe.matmul(ps_y, o_t[a][:, c, :], m.w_proj[:, c, :], start=(c == 0), stop=(c == NC_ - 1))
                last.then_inc(proj_done, 1)

            def turn_o(t):
                a = t.slot(2)
                pe.wait_ge(o_made, t.n + 1)
                reuse(pe, o_t_made, t, 1)
                bank_free(pe, x1_made, t, 4, NC_ * SEQ)
                for c in range(NC_):
                    last = pe.transpose(ps_ot[:, c * P:(c + 1) * P], o_full[a][:, c * P:(c + 1) * P], m.ident[:])
                last.then_inc(o_turned, 1)

            def probs_v(t):
                a = t.slot(2)
                pe.wait_ge(e_lo_made, t.n + 1)
                pe.wait_ge(v_placed, t.n + 1)
                if isinstance(t.n, int) and t.n < 4:
                    pe.wait_ge(ones_set, 8)
                reuse(pe, o_made, t, 1)
                for s in range(SEQ):
                    for k in range(PAIRS // 2):
                        for i, (e, v) in enumerate(((HI, HI), (HI, LO), (LO, HI))):
                            last = pe.matmul(
                                o_blocks[:, s, k].rearrange("p g r e -> p (g r e)"),
                                e_split[a][:, e, s, 2 * k:2 * k + 2].rearrange("p k q -> p (k q)"),
                                v_pairs[t.slot(4)][:, s, v, :, 2 * k:2 * k + 2].rearrange("p r k e -> p k r e"),
                                start=(i == 0), stop=(i == 2))
                last.then_inc(pv_done, 1)

            def scores(t):
                a = t.slot(2)
                pe.wait_ge(k_pairs_here[a], half(t, 16 * HPC))
                reuse(pe, e_hi_made, t, 1)
                for s in range(SEQ):
                    for c in range(NC_):
                        for g in range(G_):
                            for i, (k, q) in enumerate(((HI, HI), (HI, LO), (LO, HI))):
                                last = pe.matmul(ps_s[:, s, G_ * c + g],
                                                 k_pairs[a][:, k, c, s, g].rearrange("p r k -> p (r k)"),
                                                 qk_t[a][:, 0, q, c, s * L:(s + 1) * L], start=(i == 0), stop=(i == 2))
                last.then_inc(scores_done, 1)

            def turn_qk(t):
                a = t.slot(2)
                pe.wait_ge(qk_hat_made, t.n + 1)
                reuse(pe, qk_lo_made, t, 1)
                for k in range(2 * NC_):
                    last = pe.transpose(ps_qkt[:, k * P:(k + 1) * P], qk_hat[a][:, k * P:(k + 1) * P], m.ident[:])
                last.then_inc(qk_turned, 1)

            def qkv(t):
                a = t.slot(2)
                pe.wait_ge(x1_made, (t.n + 1) * NC_ * SEQ)
                reuse(pe, qk_biased, t, 1)
                for c in range(NC_):
                    pe.matmul(ps_qk[:, :], x1_t[a][:, c, :], m.w_qkv[:, c, 0:2 * C], start=(c == 0), stop=(c == NC_ - 1))
                reuse(pe, v_biased, t, 1)
                bank_free(pe, branch_made, t, -5)
                for c in range(NC_):
                    last = pe.matmul(ps_vv, x1_t[a][:, c, :], m.w_qkv[:, c, 2 * C:3 * C], start=(c == 0), stop=(c == NC_ - 1))
                last.then_inc(qkv_done, 1)

            def turn_x(t):
                a = t.slot(2)
                pe.wait_ge(x_hat_made, t.n + 1)
                reuse(pe, x1_made, t, 1, NC_ * SEQ)
                bank_free(pe, o_t_made, t, -5)
                for c in range(NC_):
                    last = pe.transpose(ps_xt[:, c * P:(c + 1) * P], x_hat[a][:, c * P:(c + 1) * P], m.ident[:])
                last.then_inc(x_hat_t, 1)

            pipeline(pe, [(7, project), (6, turn_o), (5, probs_v), (4, scores), (3, turn_qk), (2, qkv), (1, turn_x)])

        @block.vector
        def _(dve):
            def reduce_norms(t):
                a = t.slot(2)
                dve.wait_ge(squared, t.n + 1)
                reuse(dve, logs_made, t, 2)
                dve.tensor_reduce(norms[a][:], heads(squares[a][:]), X_AXIS, ALU.add).then_inc(norms_made, 1)
                dve.wait_ge(norms_made, t.n + 1)
                dve.scalar_tensor_tensor(norms[a][:], norms[a][:], 1e-24, m.norm_weight[:], ALU.max, ALU.mult
                                         ).then_inc(norms_weighted, 1)

            def modulate(t):
                a = t.slot(2)
                dve.wait_ge(x_hat_t, t.n + 1)
                reuse(dve, qkv_done, t, 2)
                for c in range(NC_):
                    for s in range(SEQ):
                        at = slice(c * P + s * L, c * P + (s + 1) * L)
                        dve.tensor_scalar(x1_t[a][:, c, s * L:(s + 1) * L], ps_xt[:, at],
                                          by_seq(m.scale1, c, t, s), by_seq(m.shift1, c, t, s), ALU.mult, ALU.add
                                          ).then_inc(x1_made, 1)

            def residual(t):
                a = t.slot(2)
                dve.wait_ge(proj_done, t.n + 1)
                reuse(dve, x_updated, t, 2)
                dve.tensor_tensor(branch[a][:], ps_y, m.b_proj[:], ALU.add).then_inc(branch_made, 1)

            def v_low(t):
                a = t.slot(2)
                dve.wait_ge(v_hi_made, t.n + 1)
                dve.tensor_tensor(v_split[a][:, LO].rearrange("p k r e -> p (k r e)"), v_full[a][:],
                                  v_split[a][:, HI].rearrange("p k r e -> p (k r e)"), ALU.subtract).then_inc(v_lo_made, 1)

            def place_v(t):
                a = t.slot(2)
                dve.wait_ge(v_lo_made, t.n + 1)
                reuse(dve, pv_done, t, 4)
                if isinstance(t.n, int) and t.n < 4:
                    dve.wait_ge(cleared, 6)
                for s in range(SEQ):
                    for r in range(2):
                        last = dve.tensor_copy(v_pairs[t.slot(4)][r * L:(r + 1) * L, s, :, r, :, 0:HD],
                                               v_split[a][s * L:(s + 1) * L, :, :, r, :])
                last.then_inc(v_placed, 1)

            def outputs(t):
                a = t.slot(2)
                dve.wait_ge(pv_done, t.n + 1)
                dve.reciprocal(inv_sum[a][:], o_blocks[:, :, :, 0, :, HD]).then_inc(sums_inverted, 1)
                dve.wait_ge(sums_inverted, t.n + 1)
                reuse(dve, o_turned, t, 2)
                for g in range(2):
                    for s in range(SEQ):
                        to = o_full[a][s * L:(s + 1) * L, :].rearrange("p (k g r e) -> p k g r e", g=2, r=2, e=HD)[:, :, g]
                        last = dve.tensor_tensor(
                            to, o_blocks[g * L:(g + 1) * L, s, :, g, :, 0:HD],
                            inv_sum[a][g * L:(g + 1) * L, s, :, :, None].to_broadcast([L, PAIRS // 2, 2, HD]), ALU.mult)
                last.then_inc(o_made, 1)

            def statistics(t):
                a = t.slot(2)
                if not isinstance(t.n, int) or t.n:
                    dve.wait_ge(stats_made, t.n)
                reuse(dve, x_hat_made, t, 2)
                dve.bn_stats(stats[a][:], t.rows(m.x_all).rearrange("p j n -> p (j n)")).then_inc(stats_made, 1)

            def aggregate(t):
                a = t.slot(2)
                if t.n is TILES - 1:
                    dve.wait_ge(stats_made, TILES)
                    dve.wait_ge(x_hat_made, TILES - 2)
                dve.bn_aggr(mean_var[a][:], stats[a][:]).then_inc(mean_made, 1)

            def qk_lo(t):
                a = t.slot(2)
                dve.wait_ge(qk_hi_made, t.n + 1)
                dve.tensor_tensor(qk_t[a][:, :, LO].rearrange("p w c k -> p w (c k)"),
                                  ps_qkt[:, :].rearrange("p (w k) -> p w k", w=2),
                                  qk_t[a][:, :, HI].rearrange("p w c k -> p w (c k)"), ALU.subtract).then_inc(qk_lo_made, 1)

            def e_hi(t):
                a = t.slot(2)
                dve.wait_ge(exp_made, t.n + 1)
                reuse(dve, pv_done, t, 2)
                dve.tensor_copy(flat(e_split[a][:, HI]), flat(e_full[a][:])).then_inc(e_hi_made, 1)

            def hat(t):
                a = t.slot(2)
                dve.wait_ge(rstd_made, t.n + 1)
                reuse(dve, x_hat_t, t, 2)
                dve.tensor_scalar(x_hat[a][:, None, :], t.rows(m.x_all), mean_var[a][:, 0:1], rstd[a][:],
                                  ALU.subtract, ALU.mult).then_inc(x_hat_made, 1)

            def biases(t):
                a = t.slot(2)
                dve.wait_ge(qkv_done, t.n + 1)
                reuse(dve, qk_hat_made, t, 2)
                dve.tensor_tensor(qk[a][:], ps_qk[:, :], m.b_qkv[:, 0:2 * C], ALU.add).then_inc(qk_biased, 1)
                dve.tensor_tensor(v_full[a][:], ps_vv, m.b_qkv[:, 2 * C:3 * C], ALU.add).then_inc(v_biased, 1)

            pipeline(dve, [(3, reduce_norms), (2, modulate), (7, residual), (3, v_low), (3, place_v), (-1, statistics), (0, aggregate),
                           (5, outputs), (4, e_hi), (3, qk_lo), (0, hat), (2, biases)])


def half(t, each):
    return ((t.j * UNROLL + t.u) // 2 + 1) * each if isinstance(t.j, int) else (t.j * (UNROLL // 2) + t.u // 2 + 1) * each


def heads(a):
    return a.rearrange("p (h e) -> p h e", e=HD)


def over_channels(a):
    return a[:, :, None].to_broadcast([a.shape[0], a.shape[1], HD])


def flat(a):
    names = " ".join("abcdef"[:len(a.shape) - 1])
    return a.rearrange(f"p {names} -> p ({names})")


def by_seq(a, c, t, s):
    return a[:, c, :].rearrange("p (j k) -> p j k", k=UNROLL * SEQ)[:, bass.ds(t.j, 1), t.u * SEQ + s]


def feed_forward_pass(nc, m):
    T = UNROLL
    BLOCKS = TILES // T
    SPLITS = ((HI, HI), (HI, LO), (LO, HI))
    F_CHUNKS = D_FF // P
    N = T * P
    with ExitStack() as ctx:
        def sb(name, shape, dt=F32, slots=2):
            return [ctx.enter_context(nc.sbuf_tensor(f"f_{name}{i}", shape, dt)) for i in range(slots)]

        def sem(name):
            return ctx.enter_context(nc.semaphore(f"f_{name}"))

        stats = sb("stats", [P, T, 6])
        mean_var = sb("mean_var", [P, T, 2])
        rstd = sb("rstd", [P, T])
        x_hat = sb("x_hat", [P, T, C])
        x2 = sb("x2", [P, NC_, N], F32, 1)[0]
        x2_split = sb("x2_split", [P, 2, NC_, N], BF16)
        h = sb("h", [P, N], F32, 4)
        h_split = sb("h_split", [P, 2, F_CHUNKS, N], BF16)
        gain = sb("gain", [P, T, C])
        branch = sb("branch", [P, T, C])
        ps_t = ctx.enter_context(nc.psum_tensor("f_ps_t", [P, NC_, N], F32))
        ps_h = [ctx.enter_context(nc.psum_tensor(f"f_ps_h{i}", [P, N], F32)) for i in range(4)]
        ps_y = ctx.enter_context(nc.psum_tensor("f_ps_y", [P, T, C], F32))

        gain_here = [sem(f"gain_here{i}") for i in range(2)]
        stats_made = sem("stats_made")
        mean_made = sem("mean_made")
        var_eps_made = sem("var_eps_made")
        rstd_made = sem("rstd_made")
        x_hat_made = sem("x_hat_made")
        x_turned = sem("x_turned")
        x_scaled = sem("x_scaled")
        x2_made = sem("x2_made")
        x2_hi_made = sem("x2_hi_made")
        x2_lo_made = sem("x2_lo_made")
        fc1_done = sem("fc1_done")
        h_made = sem("h_made")
        h_lo_even = sem("h_lo_even")
        h_lo_odd = sem("h_lo_odd")
        fc2_done = sem("fc2_done")
        branch_made = sem("branch_made")
        branch_gained = sem("branch_gained")
        x_updated = sem("x_updated")
        block = ctx.enter_context(nc.Block())
        gamma2 = m.gammas.rearrange("(b u s) n -> s b u n", s=SEQ, u=T)

        def rows(t):
            return m.x_all[:, bass.ds(t.n, 1)].rearrange("p b u n -> p (b u) n")

        def by_block(a, t):
            a = a[:].rearrange("p c (b s) -> p c b s", s=T * SEQ)[:, :, bass.ds(t.n, 1), :]
            return a.rearrange("p c b s -> p c (b s)")[:, :, :, None].to_broadcast([P, NC_, T * SEQ, L])

        def run(eng, stages):
            pipeline(eng, stages, BLOCKS, 2, 2)

        @block.gpsimd
        def _(pool):
            def shift(t):
                pool.wait_ge(x_scaled, t.n + 1)
                pool.tensor_tensor(x2[:].rearrange("p c (s l) -> p c s l", l=L),
                                   x2[:].rearrange("p c (s l) -> p c s l", l=L), by_block(m.shift2, t), ALU.add
                                   ).then_inc(x2_made, 1)

            def rstd_of(t):
                a = t.slot(2)
                reuse(pool, x_hat_made, t, 2, T)
                pool.wait_ge(mean_made, (t.n + 1) * T)
                pool.tensor_tensor(rstd[a][:], mean_var[a][:, :, 1], m.eps_ln[:].to_broadcast([P, T]), ALU.add
                                   ).then_inc(var_eps_made, 1)
                pool.wait_ge(var_eps_made, t.n + 1)
                pool.tensor_tensor(rstd[a][:], rstd[a][:], m.minus_half[:], ALU.pow).then_inc(rstd_made, 1)

            def update(t):
                a = t.slot(2)
                pool.wait_ge(branch_made, t.n + 1)
                pool.wait_ge(gain_here[a], (t.j + 1) * 16 * SEQ)
                pool.tensor_tensor(branch[a][:], branch[a][:], gain[a][:], ALU.mult).then_inc(branch_gained, 1)

            def add(t):
                a = t.slot(2)
                pool.wait_ge(branch_gained, t.n + 1)
                pool.tensor_tensor(rows(t), rows(t), branch[a][:], ALU.add).then_inc(x_updated, 1)

            def h_low_odd(t):
                a = t.slot(2)
                for f in range(1, F_CHUNKS, 2):
                    pool.wait_ge(h_made, t.n * F_CHUNKS + f + 1)
                    pool.tensor_tensor(h_split[a][:, LO, f], h[f % 4][:], h_split[a][:, HI, f], ALU.subtract
                                       ).then_inc(h_lo_odd, 1)

            run(pool, [(2, shift), (0, rstd_of), (5, update), (5, add), (3, h_low_odd)])

        @block.scalar
        def _(act):
            def load_gain(t):
                a = t.slot(2)
                reuse(act, branch_gained, t, 2)
                for s in range(SEQ):
                    source = gamma2[s:s + 1, bass.ds(t.n, 1), :, C:2 * C].rearrange("s b u n -> (s b) u n")
                    act.dma_start(gain[a][s * L:(s + 1) * L], source.to_broadcast([L, T, C])
                                  ).then_inc(gain_here[a], 16)

            def x2_high(t):
                a = t.slot(2)
                act.wait_ge(x2_made, t.n + 1)
                reuse(act, fc1_done, t, 2, F_CHUNKS)
                act.activation(x2_split[a][:, HI], x2[:], ACT.Copy).then_inc(x2_hi_made, 1)

            def gelus(t):
                a = t.slot(2)
                reuse(act, fc2_done, t, 2)
                for f in range(F_CHUNKS):
                    act.wait_ge(fc1_done, t.n * F_CHUNKS + f + 1)
                    if f >= 4 or not isinstance(t.n, int) or t.n > 0:
                        half_way = t.n * (F_CHUNKS // 2) + f // 2 - 1
                        act.wait_ge(h_lo_odd if f % 2 else h_lo_even, half_way)
                    act.activation(h_split[a][:, HI, f], ps_h[f % 4][:], ACT.Gelu, bias=m.b_fc1[:, f:f + 1])
                    act.activation(h[f % 4][:], ps_h[f % 4][:], ACT.Gelu, bias=m.b_fc1[:, f:f + 1]).then_inc(h_made, 1)

            run(act, [(4, load_gain), (2, x2_high), (3, gelus)])

        @block.tensor
        def _(pe):
            def fc2(t):
                a = t.slot(2)
                pe.wait_ge(h_lo_even, (t.n + 1) * (F_CHUNKS // 2))
                pe.wait_ge(h_lo_odd, (t.n + 1) * (F_CHUNKS // 2))
                reuse(pe, branch_made, t, 1)
                for i in range(T):
                    for f in range(F_CHUNKS):
                        for k, (hs, ws) in enumerate(SPLITS):
                            last = pe.matmul(ps_y[:, i], h_split[a][:, hs, f, i * P:(i + 1) * P], m.w_fc2[:, ws, f],
                                             start=(f == 0 and k == 0), stop=(f == F_CHUNKS - 1 and k == 2))
                last.then_inc(fc2_done, 1)

            def turn_x(t):
                a = t.slot(2)
                pe.wait_ge(x_hat_made, (t.n + 1) * T)
                reuse(pe, x_scaled, t, 1)
                for i in range(T):
                    for c in range(NC_):
                        last = pe.transpose(ps_t[:, c, i * P:(i + 1) * P], x_hat[a][:, i, c * P:(c + 1) * P], m.ident[:])
                last.then_inc(x_turned, 1)

            def fc1(t):
                a = t.slot(2)
                pe.wait_ge(x2_lo_made, t.n + 1)
                for f in range(F_CHUNKS):
                    if f >= 4 or not isinstance(t.n, int) or t.n > 0:
                        pe.wait_ge(h_made, t.n * F_CHUNKS + f - 3)
                    for k, (ws, xs) in enumerate(SPLITS):
                        for c in range(NC_):
                            last = pe.matmul(ps_h[f % 4][:], m.w_fc1[:, ws, c, f * P:(f + 1) * P], x2_split[a][:, xs, c],
                                             start=(k == 0 and c == 0), stop=(k == 2 and c == NC_ - 1))
                    last.then_inc(fc1_done, 1)

            run(pe, [(4, fc2), (1, turn_x), (3, fc1)])

        @block.vector
        def _(dve):
            def scale(t):
                dve.wait_ge(x_turned, t.n + 1)
                reuse(dve, x2_hi_made, t, 1)
                reuse(dve, x2_lo_made, t, 1)
                dve.tensor_tensor(x2[:].rearrange("p c (s l) -> p c s l", l=L),
                                  ps_t[:].rearrange("p c (s l) -> p c s l", l=L), by_block(m.scale2, t), ALU.mult
                                  ).then_inc(x_scaled, 1)

            def hat(t):
                a = t.slot(2)
                dve.wait_ge(rstd_made, t.n + 1)
                reuse(dve, x_turned, t, 2)
                for i in range(T):
                    dve.tensor_scalar(x_hat[a][:, i], rows(t)[:, i], mean_var[a][:, i, 0:1], rstd[a][:, i:i + 1],
                                      ALU.subtract, ALU.mult).then_inc(x_hat_made, 1)

            def statistics(t):
                a = t.slot(2)
                if not isinstance(t.n, int) or t.n:
                    dve.wait_ge(stats_made, t.n * T)
                reuse(dve, x_hat_made, t, 2, T)
                for i in range(T):
                    dve.bn_stats(stats[a][:, i], rows(t)[:, i]).then_inc(stats_made, 1)

            def aggregate(t):
                a = t.slot(2)
                if t.n is BLOCKS - 1:
                    dve.wait_ge(stats_made, BLOCKS * T)
                    dve.wait_ge(x_hat_made, (BLOCKS - 2) * T)
                for i in range(T):
                    dve.bn_aggr(mean_var[a][:, i], stats[a][:, i]).then_inc(mean_made, 1)

            def x2_low(t):
                a = t.slot(2)
                dve.wait_ge(x2_hi_made, t.n + 1)
                reuse(dve, fc1_done, t, 2, F_CHUNKS)
                dve.tensor_tensor(x2_split[a][:, LO], x2[:], x2_split[a][:, HI], ALU.subtract).then_inc(x2_lo_made, 1)

            def residual(t):
                a = t.slot(2)
                dve.wait_ge(fc2_done, t.n + 1)
                reuse(dve, x_updated, t, 2)
                dve.tensor_tensor(branch[a][:], ps_y[:], m.b_fc2[:, None, :].to_broadcast([P, T, C]), ALU.add
                                  ).then_inc(branch_made, 1)

            def h_low_even(t):
                a = t.slot(2)
                reuse(dve, fc2_done, t, 2)
                for f in range(0, F_CHUNKS, 2):
                    dve.wait_ge(h_made, t.n * F_CHUNKS + f + 1)
                    dve.tensor_tensor(h_split[a][:, LO, f], h[f % 4][:], h_split[a][:, HI, f], ALU.subtract
                                      ).then_inc(h_lo_even, 1)

            run(dve, [(2, scale), (1, hat), (-1, statistics), (0, aggregate), (2, x2_low), (4, residual),
                      (3, h_low_even)])


def linear_pass(nc, m, cond, out):
    SPLITS = ((HI, HI), (HI, LO), (LO, HI))
    NK = NC_ * SEQ
    with ExitStack() as ctx:
        def sb(name, shape, dt=F32, slots=2):
            return [ctx.enter_context(nc.sbuf_tensor(f"l_{name}{i}", shape, dt)) for i in range(slots)]

        def ps(name, shape):
            return ctx.enter_context(nc.psum_tensor(f"l_{name}", shape, F32))

        def sem(name):
            return ctx.enter_context(nc.semaphore(f"l_{name}"))

        stats = sb("stats", [P, 6])
        mean_var = sb("mean_var", [P, 2])
        rstd = sb("rstd", [P, 1])
        x_hat = sb("x_hat", [P, C])
        x3_t = sb("x3_t", [P, NC_, P])
        kq = sb("kq", [P, 2 * C], F32, 4)
        tops = sb("tops", [P, NK + H])
        sums = sb("sums", [P, NK + H])
        v_full = sb("v_full", [P, C])
        v_split = sb("v_split", [P, 2, C], BF16, 4)
        kq_t = sb("kq_t", [P, 2, 2 * C], BF16, 2)
        kv = sb("kv", [P, NC_, SEQ, P])
        kv_split = sb("kv_split", [P, 2, NC_, SEQ, P], BF16)
        y_stats = sb("y_stats", [P, 6])
        y_mean_var = sb("y_mean_var", [P, 2])
        y_rstd = sb("y_rstd", [P, 1])
        y_hat = sb("y_hat", [P, C])
        z_t = sb("z_t", [P, NC_, P])
        tanh = sb("tanh", [P, NC_, P])
        silu = sb("silu", [P, NC_, P])
        gate = sb("gate", [P, C], F32, 4)
        branch = sb("branch", [P, C])
        ps_xt = ps("ps_xt", [P, NC_, P])
        ps_qv = ps("ps_qv", [P, 2 * C])
        ps_k = ps("ps_k", [P, NC_, P])
        ps_kq = ps("ps_kq", [P, 2 * C])
        ps_kv = ps("ps_kv", [P, NC_, SEQ, P])
        ps_y = ps("ps_y", [P, C])
        ps_yt = ps("ps_yt", [P, NC_, P])
        ps_out = ps("ps_out", [P, C])

        gate_here = [sem(f"gate_here{i}") for i in range(4)]
        stats_made = sem("stats_made")
        mean_made = sem("mean_made")
        var_eps_made = sem("var_eps_made")
        rstd_made = sem("rstd_made")
        x_hat_made = sem("x_hat_made")
        x_turned = sem("x_turned")
        x3_made = sem("x3_made")
        k_done = sem("k_done")
        qv_done = sem("qv_done")
        k_biased = sem("k_biased")
        q_biased = sem("q_biased")
        v_biased = sem("v_biased")
        v_hi_made = sem("v_hi_made")
        v_lo_made = sem("v_lo_made")
        tops_made = sem("tops_made")
        lowered = sem("lowered")
        exp_made = sem("exp_made")
        sums_made = sem("sums_made")
        sums_inverted = sem("sums_inverted")
        softmax_made = sem("softmax_made")
        kq_turned = sem("kq_turned")
        kq_hi_made = sem("kq_hi_made")
        kq_lo_made = sem("kq_lo_made")
        kv_first = sem("kv_first")
        kv_done = sem("kv_done")
        kv_masked = sem("kv_masked")
        kv_hi_made = sem("kv_hi_made")
        kv_lo_made = sem("kv_lo_made")
        y_done = sem("y_done")
        y_stats_made = sem("y_stats_made")
        y_mean_made = sem("y_mean_made")
        y_var_eps_made = sem("y_var_eps_made")
        y_rstd_made = sem("y_rstd_made")
        y_hat_made = sem("y_hat_made")
        y_turned = sem("y_turned")
        z_scaled = sem("z_scaled")
        z_made = sem("z_made")
        tanh_made = sem("tanh_made")
        silu_made = sem("silu_made")
        out_done = sem("out_done")
        branch_made = sem("branch_made")
        branch_gained = sem("branch_gained")
        x_updated = sem("x_updated")
        stored = sem("stored")
        block = ctx.enter_context(nc.Block())
        gates = cond.rearrange("(j u s) n -> s j u n", s=SEQ, u=UNROLL)

        def k_of(a):
            return a[:, 0:C].rearrange("p (k l) -> p k l", l=L)

        def q_of(a):
            return a[:, C:2 * C].rearrange("p (h e) -> p h e", e=HD)

        def by_token(a):
            return a[:, :, None].to_broadcast([P, NK, L])

        def by_seq_over_tokens(a, t):
            a = a[:].rearrange("p c (j u s) -> p c j u s", u=UNROLL, s=SEQ)[:, :, bass.ds(t.j, 1), t.u, :]
            return a.rearrange("p c j s -> p c (j s)")[:, :, :, None].to_broadcast([P, NC_, SEQ, L])

        def tokens_by_seq(a):
            return a.rearrange("p c (s l) -> p c s l", l=L)

        @block.sync
        def _(sp):
            sp.wait_ge(stored, 16 * GROUPS)

        @block.gpsimd
        def _(pool):
            def update(t):
                a = t.slot(2)
                pool.wait_ge(branch_made, t.n + 1)
                pool.wait_ge(gate_here[t.slot(4)], (t.j + 1) * 16 * SEQ)
                pool.tensor_tensor(branch[a][:], branch[a][:], gate[t.slot(4)][:], ALU.mult).then_inc(branch_gained, 1)

            def add(t):
                a = t.slot(2)
                pool.wait_ge(branch_gained, t.n + 1)
                pool.tensor_tensor(t.rows(m.x_all), t.rows(m.x_all), branch[a][:, None, :], ALU.add
                                   ).then_inc(x_updated, 1)

            def shift(t):
                a = t.slot(2)
                pool.wait_ge(z_scaled, t.n + 1)
                pool.tensor_tensor(tokens_by_seq(z_t[a][:]), tokens_by_seq(z_t[a][:]),
                                   by_seq_over_tokens(m.shift3, t), ALU.add).then_inc(z_made, 1)

            def y_rstd_of(t):
                a = t.slot(2)
                pool.wait_ge(y_mean_made, t.n + 1)
                reuse(pool, y_hat_made, t, 2)
                pool.tensor_tensor(y_rstd[a][:], y_mean_var[a][:, 1:2], m.eps_norm3[:], ALU.add
                                   ).then_inc(y_var_eps_made, 1)
                pool.wait_ge(y_var_eps_made, t.n + 1)
                pool.tensor_tensor(y_rstd[a][:], y_rstd[a][:], m.minus_half[:, 0:1], ALU.pow).then_inc(y_rstd_made, 1)

            def kv_low(t):
                a = t.slot(2)
                pool.wait_ge(kv_hi_made, t.n + 1)
                reuse(pool, y_done, t, 2)
                pool.tensor_tensor(kv_split[a][:, LO], kv[a][:], kv_split[a][:, HI], ALU.subtract
                                   ).then_inc(kv_lo_made, 1)

            def softmax(t):
                a = t.slot(2)
                pool.wait_ge(sums_inverted, t.n + 1)
                pool.tensor_tensor(k_of(kq[t.slot(4)]), k_of(kq[t.slot(4)]), by_token(sums[a][:, 0:NK]), ALU.mult
                                   ).then_inc(softmax_made, 1)
                pool.tensor_tensor(q_of(kq[t.slot(4)]), q_of(kq[t.slot(4)]), over_channels(sums[a][:, NK:]), ALU.mult
                                   ).then_inc(softmax_made, 1)

            def lower(t):
                a = t.slot(2)
                pool.wait_ge(tops_made, (t.n + 1) * 2)
                pool.tensor_tensor(k_of(kq[t.slot(4)]), k_of(kq[t.slot(4)]), by_token(tops[a][:, 0:NK]), ALU.subtract
                                   ).then_inc(lowered, 1)
                pool.tensor_tensor(q_of(kq[t.slot(4)]), q_of(kq[t.slot(4)]), over_channels(tops[a][:, NK:]), ALU.subtract
                                   ).then_inc(lowered, 1)

            def v_low(t):
                a = t.slot(2)
                pool.wait_ge(v_hi_made, t.n + 1)
                reuse(pool, kv_done, t, 4)
                pool.tensor_tensor(v_split[t.slot(4)][:, LO], v_full[a][:], v_split[t.slot(4)][:, HI], ALU.subtract
                                   ).then_inc(v_lo_made, 1)

            def rstd_of(t):
                a = t.slot(2)
                reuse(pool, x_hat_made, t, 2)
                pool.wait_ge(mean_made, t.n + 1)
                pool.tensor_tensor(rstd[a][:], mean_var[a][:, 1:2], m.eps_norm3[:], ALU.add).then_inc(var_eps_made, 1)
                pool.wait_ge(var_eps_made, t.n + 1)
                pool.tensor_tensor(rstd[a][:], rstd[a][:], m.minus_half[:, 0:1], ALU.pow).then_inc(rstd_made, 1)

            pipeline(pool, [(5, softmax), (4, lower), (9, shift), (3, v_low), (6, kv_low), (7, y_rstd_of),
                            (10, update), (0, rstd_of), (10, add)])

        @block.scalar
        def _(act):
            def load_gate(t):
                reuse(act, branch_gained, t, 4)
                for s in range(SEQ):
                    source = gates[s:s + 1, bass.ds(t.j, 1), t.u, :].rearrange("s j n -> (s j) n")
                    act.dma_start(gate[t.slot(4)][s * L:(s + 1) * L], source.to_broadcast([L, C])
                                  ).then_inc(gate_here[t.slot(4)], 16)

            def store(t):
                if t.u == UNROLL - 1:
                    act.wait_ge(x_updated, t.n + 1)
                    act.dma_start(x_tiles(out)[:, bass.ds(t.j, 1)], m.x_all[:, bass.ds(t.j, 1)]).then_inc(stored, 16)

            def tanhs(t):
                a = t.slot(2)
                act.wait_ge(z_made, t.n + 1)
                reuse(act, silu_made, t, 2)
                act.activation(tanh[a][:], z_t[a][:], ACT.Tanh, scale=0.5).then_inc(tanh_made, 1)

            def kv_high(t):
                a = t.slot(2)
                act.wait_ge(kv_masked, t.n + 1)
                reuse(act, y_done, t, 2)
                act.activation(kv_split[a][:, HI], kv[a][:], ACT.Copy).then_inc(kv_hi_made, 1)

            def kq_high(t):
                a = t.slot(2)
                act.wait_ge(kq_turned, t.n + 1)
                reuse(act, y_done, t, 2)
                act.activation(kq_t[a][:, HI], ps_kq[:], ACT.Copy).then_inc(kq_hi_made, 1)

            def exponentials(t):
                a = t.slot(2)
                act.wait_ge(lowered, (t.n + 1) * 2)
                act.activation(kq[t.slot(4)][:], kq[t.slot(4)][:], ACT.Exp).then_inc(exp_made, 1)

            def k_bias(t):
                a = t.slot(2)
                act.wait_ge(k_done, t.n + 1)
                reuse(act, kq_turned, t, 4)
                for c in range(NC_):
                    act.activation(kq[t.slot(4)][:, c * P:(c + 1) * P], ps_k[:, c], ACT.Identity, bias=m.b_k3[:, c:c + 1]
                                   ).then_inc(k_biased, 1)

            def v_high(t):
                a = t.slot(2)
                act.wait_ge(v_biased, t.n + 1)
                reuse(act, kv_done, t, 4)
                act.activation(v_split[t.slot(4)][:, HI], v_full[a][:], ACT.Copy).then_inc(v_hi_made, 1)

            def affine(t):
                a = t.slot(2)
                act.wait_ge(x_turned, t.n + 1)
                reuse(act, k_done, t, 2)
                for c in range(NC_):
                    act.activation(x3_t[a][:, c], ps_xt[:, c], ACT.Identity, bias=m.b_norm3[:, c:c + 1],
                                   scale=m.g_norm3[:, c:c + 1]).then_inc(x3_made, 1)

            pipeline(act, [(2, affine), (3, k_bias), (3, v_high), (4, exponentials), (9, tanhs), (5, kq_high),
                           (6, kv_high), (8, load_gate), (11, store)])

        @block.tensor
        def _(pe):
            def project(t):
                a = t.slot(2)
                pe.wait_ge(silu_made, t.n + 1)
                reuse(pe, branch_made, t, 1)
                for c in range(NC_):
                    last = pe.matmul(ps_out[:], silu[a][:, c], m.w_out3[:, c], start=(c == 0), stop=(c == NC_ - 1))
                last.then_inc(out_done, 1)

            def turn_y(t):
                a = t.slot(2)
                pe.wait_ge(y_hat_made, t.n + 1)
                reuse(pe, z_scaled, t, 1)
                for c in range(NC_):
                    last = pe.transpose(ps_yt[:, c], y_hat[a][:, c * P:(c + 1) * P], m.ident[:])
                last.then_inc(y_turned, 1)

            def q_kv(t):
                a = t.slot(2)
                pe.wait_ge(kv_lo_made, t.n + 1)
                reuse(pe, y_hat_made, t, 1)
                for s in range(SEQ):
                    for c in range(NC_):
                        q_cols = C + c * P + s * L
                        for i, (q, w) in enumerate(SPLITS):
                            last = pe.matmul(ps_y[s * L:(s + 1) * L, c * P:(c + 1) * P],
                                             kq_t[a][:, q, q_cols:q_cols + L], kv_split[a][:, w, c, s],
                                             start=(i == 0), stop=(i == 2))
                last.then_inc(y_done, 1)

            def k_v(t):
                a = t.slot(2)
                pe.wait_ge(kq_lo_made, t.n + 1)
                pe.wait_ge(v_lo_made, t.n + 1)
                reuse(pe, kv_masked, t, 1)
                for s in range(SEQ):
                    own = slice(s * L, (s + 1) * L)
                    for c in range(NC_):
                        chans = slice(c * P, (c + 1) * P)
                        for i, (k, v) in enumerate(SPLITS):
                            last = pe.matmul(ps_kv[:, c, s], kq_t[a][own, k, chans], v_split[t.slot(4)][own, v, chans],
                                             start=(i == 0), stop=(i == 2))
                    if s < SEQ - 1:
                        last.then_inc(kv_first, 1)
                        pe.wait_ge(kv_first, t.n + 1)
                last.then_inc(kv_done, 1)

            def turn_kq(t):
                a = t.slot(2)
                pe.wait_ge(softmax_made, (t.n + 1) * 2)
                reuse(pe, kq_lo_made, t, 1)
                for k in range(2 * NC_):
                    last = pe.transpose(ps_kq[:, k * P:(k + 1) * P], kq[t.slot(4)][:, k * P:(k + 1) * P], m.ident[:])
                last.then_inc(kq_turned, 1)

            def qkv(t):
                a = t.slot(2)
                pe.wait_ge(x3_made, (t.n + 1) * NC_)
                reuse(pe, v_biased, t, 1)
                for c in range(NC_):
                    last = pe.matmul(ps_qv[:], x3_t[a][:, c], m.w_qv3[:, c], start=(c == 0), stop=(c == NC_ - 1))
                last.then_inc(qv_done, 1)
                reuse(pe, k_biased, t, 1, NC_)
                for to in range(NC_):
                    for c in range(NC_):
                        last = pe.matmul(ps_k[:, to], m.w_k3[:, c, to * P:(to + 1) * P], x3_t[a][:, c],
                                         start=(c == 0), stop=(c == NC_ - 1))
                last.then_inc(k_done, 1)

            def turn_x(t):
                a = t.slot(2)
                pe.wait_ge(x_hat_made, t.n + 1)
                reuse(pe, x3_made, t, 1, NC_)
                for c in range(NC_):
                    last = pe.transpose(ps_xt[:, c], x_hat[a][:, c * P:(c + 1) * P], m.ident[:])
                last.then_inc(x_turned, 1)

            pipeline(pe, [(10, project), (8, turn_y), (7, q_kv), (6, k_v), (5, turn_kq), (2, qkv), (1, turn_x)])

        @block.vector
        def _(dve):
            def residual(t):
                a = t.slot(2)
                dve.wait_ge(out_done, t.n + 1)
                reuse(dve, x_updated, t, 2)
                dve.tensor_tensor(branch[a][:], ps_out[:], m.b_out3[:], ALU.add).then_inc(branch_made, 1)

            def scale(t):
                a = t.slot(2)
                dve.wait_ge(y_turned, t.n + 1)
                reuse(dve, silu_made, t, 2)
                dve.tensor_tensor(tokens_by_seq(z_t[a][:]), tokens_by_seq(ps_yt[:]), by_seq_over_tokens(m.scale3, t),
                                  ALU.mult).then_inc(z_scaled, 1)

            def silus(t):
                a = t.slot(2)
                dve.wait_ge(tanh_made, t.n + 1)
                reuse(dve, out_done, t, 2)
                dve.scalar_tensor_tensor(silu[a][:], tanh[a][:], 1.0, z_t[a][:], ALU.add, ALU.mult
                                         ).then_inc(silu_made, 1)

            def y_statistics(t):
                a = t.slot(2)
                dve.wait_ge(y_done, t.n + 1)
                reuse(dve, y_hat_made, t, 2)
                dve.bn_stats(y_stats[a][:], ps_y[:]).then_inc(y_stats_made, 1)

            def y_aggregate(t):
                a = t.slot(2)
                if isinstance(t.n, int):
                    dve.wait_ge(y_stats_made, t.n + 1)
                dve.bn_aggr(y_mean_var[a][:], y_stats[a][:]).then_inc(y_mean_made, 1)

            def y_hats(t):
                a = t.slot(2)
                dve.wait_ge(y_rstd_made, t.n + 1)
                reuse(dve, y_turned, t, 2)
                dve.tensor_scalar(y_hat[a][:], ps_y[:], y_mean_var[a][:, 0:1], y_rstd[a][:], ALU.subtract, ALU.mult
                                  ).then_inc(y_hat_made, 1)

            def mask(t):
                a = t.slot(2)
                dve.wait_ge(kv_done, t.n + 1)
                reuse(dve, kv_lo_made, t, 2)
                dve.tensor_tensor(kv[a][:].rearrange("p c s l -> p (c s) l"), ps_kv[:].rearrange("p c s l -> p (c s) l"),
                                  m.same_head[:, None, :].to_broadcast([P, NC_ * SEQ, P]), ALU.mult
                                  ).then_inc(kv_masked, 1)

            def kq_low(t):
                a = t.slot(2)
                dve.wait_ge(kq_hi_made, t.n + 1)
                if not isinstance(t.n, int):
                    dve.wait_ge(y_stats_made, t.n - 1)
                dve.tensor_tensor(kq_t[a][:, LO], ps_kq[:], kq_t[a][:, HI], ALU.subtract).then_inc(kq_lo_made, 1)

            def total(t):
                a = t.slot(2)
                dve.wait_ge(exp_made, t.n + 1)
                reuse(dve, softmax_made, t, 2, 2)
                dve.tensor_reduce(sums[a][:, 0:NK], k_of(kq[t.slot(4)]), X_AXIS, ALU.add).then_inc(sums_made, 1)
                dve.tensor_reduce(sums[a][:, NK:], q_of(kq[t.slot(4)]), X_AXIS, ALU.add).then_inc(sums_made, 1)
                dve.wait_ge(sums_made, (t.n + 1) * 2)
                dve.reciprocal(sums[a][:], sums[a][:]).then_inc(sums_inverted, 1)

            def biases(t):
                a = t.slot(2)
                dve.wait_ge(qv_done, t.n + 1)
                reuse(dve, kq_turned, t, 4)
                dve.tensor_tensor(kq[t.slot(4)][:, C:2 * C], ps_qv[:, 0:C], m.b_qv3[:, 0:C], ALU.add).then_inc(q_biased, 1)
                reuse(dve, v_lo_made, t, 2)
                dve.tensor_tensor(v_full[a][:], ps_qv[:, C:2 * C], m.b_qv3[:, C:2 * C], ALU.add).then_inc(v_biased, 1)

            def maxima(t):
                a = t.slot(2)
                reuse(dve, lowered, t, 2, 2)
                dve.wait_ge(k_biased, (t.n + 1) * NC_)
                dve.tensor_reduce(tops[a][:, 0:NK], k_of(kq[t.slot(4)]), X_AXIS, ALU.max).then_inc(tops_made, 1)
                dve.wait_ge(q_biased, t.n + 1)
                dve.tensor_reduce(tops[a][:, NK:], q_of(kq[t.slot(4)]), X_AXIS, ALU.max).then_inc(tops_made, 1)

            def statistics(t):
                a = t.slot(2)
                if not isinstance(t.n, int) or t.n:
                    dve.wait_ge(stats_made, t.n)
                reuse(dve, x_hat_made, t, 2)
                dve.bn_stats(stats[a][:], t.rows(m.x_all).rearrange("p j n -> p (j n)")).then_inc(stats_made, 1)

            def aggregate(t):
                a = t.slot(2)
                if t.n is TILES - 1:
                    dve.wait_ge(stats_made, TILES)
                    dve.wait_ge(x_hat_made, TILES - 2)
                dve.bn_aggr(mean_var[a][:], stats[a][:]).then_inc(mean_made, 1)

            def hat(t):
                a = t.slot(2)
                dve.wait_ge(rstd_made, t.n + 1)
                reuse(dve, x_turned, t, 2)
                dve.tensor_scalar(x_hat[a][:, None, :], t.rows(m.x_all), mean_var[a][:, 0:1], rstd[a][:],
                                  ALU.subtract, ALU.mult).then_inc(x_hat_made, 1)

            pipeline(dve, [(1, hat), (9, scale), (3, biases), (3, maxima), (8, y_hats), (6, mask), (-1, statistics),
                           (0, aggregate), (4, total), (7, y_statistics), (5, kq_low), (7, y_aggregate),
                           (10, residual), (9, silus)])


_INS = ["x", "cond_1024", "L0_cond_mat_qkv_w", "L0_cond_q_bias", "L0_cond_v_bias", "L0_cond_scale_mul",
        "L0_cond_proj_w", "L0_cond_proj_b", "L0_cond_ada_w", "L0_cond_ada_b", "L0_cond_fc1_w", "L0_cond_fc1_b",
        "L0_cond_fc2_w", "L0_cond_fc2_b", "L1_cond_norm_g", "L1_cond_norm_b", "L1_cond_Wq", "L1_cond_bq",
        "L1_cond_Wk", "L1_cond_bk", "L1_cond_Wv", "L1_cond_bv", "L1_cond_emb_W", "L1_cond_emb_b",
        "L1_cond_sn_g", "L1_cond_sn_b", "L1_cond_out_W", "L1_cond_out_b"]
_TURNED = {"L0_cond_mat_qkv_w", "L0_cond_proj_w", "L0_cond_ada_w", "L0_cond_fc1_w", "L0_cond_fc2_w"}


def kernel(**inputs):
    import concourse.bacc as bacc
    from concourse.bass_utils import run_bass_kernel_spmd

    nc = bacc.Bacc("TRN2", target_bir_lowering=False, num_devices=1)
    arrays, args = {}, []
    for name in _INS:
        a = np.asarray(inputs[name])
        a = np.ascontiguousarray(a.T if name in _TURNED else a)
        arrays[f"in_{name}"] = a
        args.append(nc.dram_tensor(f"in_{name}", a.shape, mybir.dt.from_np(a.dtype), kind="ExternalInput").ap())
    args.append(nc.dram_tensor("out_0", (B, L, C), F32, kind="ExternalOutput").ap())
    condition_kernel(nc, *args)
    r = run_bass_kernel_spmd(nc, [arrays], core_ids=[0])
    return r.results[0]["out_0"]
```

```python
import math
from contextlib import ExitStack

import numpy as np

import concourse.bass as bass
from concourse import mybir

ALU = mybir.AluOpType
ACT = mybir.ActivationFunctionType
F32 = mybir.dt.float32
BF16 = mybir.dt.bfloat16
X_AXIS = mybir.AxisListType.X

P = 128
B, L, C = 128, 64, 256
H = 16
HD = C // H
D_FF = 1024
NC_ = C // P
SEQ = P // L
TILES = B // SEQ
UNROLL = 4
GROUPS = TILES // UNROLL
HPC = P // HD
G_ = HPC // 2
HI, LO = 0, 1
CHUNKED = "(c p) n -> p c n"
X_PARTS = (0, 1, 4, GROUPS)
LOG_100 = math.log(100.0)
LN2 = math.log(2.0)


class Tile:

    def __init__(self, j, u, unroll=UNROLL):
        self.j, self.u = j + u // unroll, u % unroll
        self.n = self.j * unroll + self.u

    def slot(self, slots):
        return self.u % slots

    def since(self, slots, each=1):
        if isinstance(self.n, int) and self.n < slots:
            return None
        return (self.n + 1 - slots) * each

    def rows(self, x):
        return x[:, bass.ds(self.j, 1), self.u]


def pipeline(eng, stages, tiles=TILES, unroll=UNROLL, reach=4):
    deepest = max(lag for lag, _ in stages)
    ahead = min(lag for lag, _ in stages)
    first = -(-(deepest + reach) // unroll)
    last = tiles // unroll + ahead // unroll

    def step(j, u, known):
        for lag, stage in stages:
            if known and not 0 <= unroll * j + u - lag < tiles:
                continue
            stage(Tile(j, u - lag, unroll))

    for s in range(unroll * (ahead // unroll), unroll * first):
        step(0, s, True)
    with eng.Fori(first, last) as j:
        for u in range(unroll):
            step(j, u, False)
    for s in range(unroll * last, tiles + deepest):
        step(0, s, True)


def condition_kernel(nc, x, cond, qkv_w, q_bias, v_bias, scale_mul, proj_w, proj_b, ada_w, ada_b,
                     fc1_w, fc1_b, fc2_w, fc2_b, norm_g, norm_b, wq, bq, wk, bk, wv, bv,
                     emb_w, emb_b, sn_g, sn_b, out_w, out_b, out):
    with ExitStack() as ctx:
        m = Shared(nc, ctx)
        setup(nc, m, x, cond, qkv_w, q_bias, v_bias, scale_mul, proj_w, proj_b, ada_w, ada_b,
              fc1_w, fc1_b, fc2_w, fc2_b, norm_g, norm_b, wq, bq, wk, bk, wv, bv,
              emb_w, emb_b, sn_g, sn_b, out_w, out_b)
        attention_pass(nc, m, x, fc1_w)
        feed_forward_pass(nc, m, fc2_w, wq, wk, wv, out_w)
        linear_pass(nc, m, cond, out)


class Shared:

    def __init__(self, nc, ctx):
        def sb(name, shape, dt):
            return ctx.enter_context(nc.sbuf_tensor(name, shape, dt))

        self.x_all = sb("x_all", [P, GROUPS, UNROLL, C], F32)
        self.ident = sb("ident", [P, P], F32)
        self.minus_half = sb("minus_half", [P, UNROLL], F32)
        self.eps_norm3 = sb("eps_norm3", [P, 1], F32)
        self.eps_ln = sb("eps_ln", [P, 1], F32)
        self.scale1, self.shift1, self.scale2, self.shift2, self.scale3, self.shift3 = (
            sb(n, [P, NC_, B], F32) for n in ("scale1", "shift1", "scale2", "shift2", "scale3", "shift3"))
        self.gammas = nc.dram_tensor("gammas", [B, 2 * C], F32, kind="Internal").ap()
        self.w_qkv = sb("w_qkv", [P, NC_, 3 * C], F32)
        self.w_proj = sb("w_proj", [P, NC_, C], F32)
        self.w_fc1 = sb("w_fc1", [P, 2, NC_, D_FF], BF16)
        self.w_fc2 = sb("w_fc2", [P, 2, D_FF // P, C], BF16)
        self.w_qv3 = sb("w_qv3", [P, NC_, 2 * C], F32)
        self.w_k3 = sb("w_k3", [P, NC_, C], F32)
        self.w_out3 = sb("w_out3", [P, NC_, C], F32)
        self.fc1_full = sb("fc1_full", [P, NC_, D_FF], F32)
        self.x_here = [ctx.enter_context(nc.semaphore(f"x_here{i}")) for i in range(3)]
        self.ff_here = ctx.enter_context(nc.semaphore("ff_here"))
        self.linear_here = ctx.enter_context(nc.semaphore("linear_here"))
        self.b_qkv = sb("b_qkv", [P, 3 * C], F32)
        self.b_proj = sb("b_proj", [P, C], F32)
        self.b_fc2 = sb("b_fc2", [P, C], F32)
        self.b_qv3 = sb("b_qv3", [P, 2 * C], F32)
        self.b_out3 = sb("b_out3", [P, C], F32)
        self.b_fc1 = sb("b_fc1", [P, D_FF // P], F32)
        self.b_k3 = sb("b_k3", [P, NC_], F32)
        self.g_norm3 = sb("g_norm3", [P, NC_], F32)
        self.b_norm3 = sb("b_norm3", [P, NC_], F32)
        self.norm_weight = sb("norm_weight", [P, 2 * H], F32)
        self.log_256 = sb("log_256", [P, 1], F32)
        self.minus_shift = sb("minus_shift", [P, 1], F32)
        self.same_head = sb("same_head", [P, P], F32)


def setup(nc, m, x, cond, qkv_w, q_bias, v_bias, scale_mul, proj_w, proj_b, ada_w, ada_b,
          fc1_w, fc1_b, fc2_w, fc2_b, norm_g, norm_b, wq, bq, wk, bk, wv, bv,
          emb_w, emb_b, sn_g, sn_b, out_w, out_b):
    with ExitStack() as ctx:
        def sb(name, shape, dt=F32):
            return ctx.enter_context(nc.sbuf_tensor(name, shape, dt))

        def sem(name):
            return ctx.enter_context(nc.semaphore(name))

        cond_sb = sb("cond_sb", [P, C])
        cond_act = sb("cond_act", [P, C])
        cond_t = sb("cond_t", [P, NC_, B])
        w_ada = sb("w_ada", [P, NC_, 6 * C])
        w_emb = sb("w_emb", [P, NC_, 2 * C])
        b_ada_row = sb("b_ada_row", [P, 2 * C])
        b_ada = sb("b_ada", [P, 6 * NC_])
        b_emb = sb("b_emb", [P, 2 * NC_])
        g_sn = sb("g_sn", [P, NC_])
        b_sn = sb("b_sn", [P, NC_])
        gamma_rows = sb("gamma_rows", [P, 2 * C])
        head_scale = sb("head_scale", [P, H])
        head_exp = sb("head_exp", [P, H])
        top = sb("top", [P, 1])
        scale_plus = sb("scale_plus", [P, NC_, B])
        b_sn_half = sb("b_sn_half", [P, NC_])
        band = sb("band", [P, P])
        ps = [ctx.enter_context(nc.psum_tensor(f"set_ps{i}", [P, 512], F32)) for i in range(6)]

        cond_here = sem("cond_here")
        heads_here = sem("heads_here")
        ada_here = sem("ada_here")
        emb_here = sem("emb_here")
        attention_here = sem("attention_here")
        silu_done = sem("silu_done")
        exp_done = sem("exp_done")
        b_halved = sem("b_halved")
        consts_made = sem("consts_made")
        heads_made = sem("heads_made")
        transposed = sem("transposed")
        cond_t_made = sem("cond_t_made")
        products = sem("products")
        modulations = sem("modulations")
        gammas_made = sem("gammas_made")
        gammas_stored = sem("gammas_stored")
        block = ctx.enter_context(nc.Block())

        def row(a):
            return a[None, :].to_broadcast([P, a.shape[0]])

        def column(a):
            return a.rearrange("(k p) -> p k", p=P)

        def load(eng, loads, signal):
            for to, source in loads:
                eng.dma_start(to, source, allow_slow_non_contiguous=True).then_inc(signal, 16)

        @block.sync
        def _(sp):
            load(sp, [(cond_sb[:], cond)], cond_here)
            load(sp, [(w_ada[:], ada_w.rearrange(CHUNKED, p=P))], ada_here)
            load(sp, [(m.x_all[:, X_PARTS[0]:X_PARTS[1]], x_tiles(x)[:, X_PARTS[0]:X_PARTS[1]])], m.x_here[0])
            load(sp, [(m.w_qkv[:], qkv_w.rearrange(CHUNKED, p=P))], attention_here)
            load(sp, [(w_emb[:], emb_w.rearrange(CHUNKED, p=P))], emb_here)
            load(sp, [(m.w_proj[:], proj_w.rearrange(CHUNKED, p=P))], attention_here)
            sp.wait_ge(gammas_made, 1)
            sp.dma_start(m.gammas, gamma_rows[:]).then_inc(gammas_stored, 16)
            sp.wait_ge(gammas_stored, 16)
            part = slice(X_PARTS[1], X_PARTS[2])
            load(sp, [(m.x_all[:, part], x_tiles(x)[:, part])], m.x_here[1])
            sp.wait_ge(attention_here, 16 * 5)

        @block.scalar
        def _(act):
            load(act, [(head_scale[:], scale_mul.rearrange("a h b c -> (a b c) h").to_broadcast([P, H]))], heads_here)
            load(act, [(b_ada_row[:], row(ada_b[0:2 * C])), (b_ada[:], column(ada_b))], ada_here)
            load(act, [(b_emb[:], column(emb_b)), (g_sn[:], column(sn_g)), (b_sn[:], column(sn_b))], emb_here)
            load(act, [(m.b_qkv[:, 0:C], row(q_bias)), (m.b_qkv[:, 2 * C:3 * C], row(v_bias)), (m.b_proj[:], row(proj_b))],
                 attention_here)
            act.wait_ge(cond_here, 16)
            act.activation(cond_act[:], cond_sb[:], ACT.Silu).then_inc(silu_done, 1)
            load(act, [(m.b_fc1[:], column(fc1_b)), (m.b_fc2[:], row(fc2_b))], m.ff_here)
            load(act, [(m.b_qv3[:, 0:C], row(bq)), (m.b_qv3[:, C:2 * C], row(bv)), (m.b_out3[:], row(out_b)),
                       (m.b_k3[:], column(bk)), (m.g_norm3[:], column(norm_g)), (m.b_norm3[:], column(norm_b))],
                 m.linear_here)
            act.wait_ge(heads_made, 1)
            act.activation(head_exp[:], head_scale[:], ACT.Exp).then_inc(exp_done, 1)
            act.wait_ge(consts_made, 8)
            act.activation(m.norm_weight[:, 0:H], head_scale[:], ACT.Exp, scale=-2.0)

        @block.gpsimd
        def _(pool):
            pool.memset(m.ident[:], 0.0).then_inc(consts_made, 1)
            pool.memset(m.minus_half[:], -0.5).then_inc(consts_made, 1)
            pool.memset(m.b_qkv[:, C:2 * C], 0.0).then_inc(consts_made, 1)
            pool.memset(m.log_256[:], 8 * LN2).then_inc(consts_made, 1)
            pool.memset(m.norm_weight[:], 1.0).then_inc(consts_made, 1)
            pool.memset(m.eps_norm3[:], 1e-5).then_inc(consts_made, 1)
            pool.memset(m.eps_ln[:], 1e-6).then_inc(consts_made, 1)
            pool.memset(m.same_head[:], 1.0).then_inc(consts_made, 1)
            pool.wait_ge(consts_made, 8)
            pool.affine_select(out=m.ident[:], in_=m.ident[:], compare_op=ALU.not_equal, fill=1.0, base=0,
                               pattern=[[-1, P]], channel_multiplier=1).then_inc(consts_made, 1)
            pool.affine_select(out=band[:].rearrange("p (h e) -> p h e", e=HD),
                               in_=m.same_head[:].rearrange("p (h e) -> p h e", e=HD), compare_op=ALU.is_ge, fill=0.0,
                               base=0, pattern=[[-HD, HPC], [0, HD]], channel_multiplier=1).then_inc(consts_made, 1)
            pool.wait_ge(consts_made, 10)
            pool.affine_select(out=m.same_head[:].rearrange("p (h e) -> p h e", e=HD),
                               in_=band[:].rearrange("p (h e) -> p h e", e=HD), compare_op=ALU.is_ge, fill=0.0,
                               base=HD - 1, pattern=[[HD, HPC], [0, HD]], channel_multiplier=-1).then_inc(consts_made, 1)
            pool.wait_ge(consts_made, 11)

        @block.tensor
        def _(pe):
            pe.wait_ge(consts_made, 9)
            pe.wait_ge(silu_done, 1)
            for c in range(NC_):
                last = pe.transpose(ps[0][:, c * P:(c + 1) * P], cond_act[:, c * P:(c + 1) * P], m.ident[:])
            last.then_inc(transposed, 1)
            pe.wait_ge(cond_t_made, 1)
            pe.wait_ge(ada_here, 16 * 3)
            for c in range(NC_):
                last = pe.matmul(ps[1][:, :], cond_t[:, c, :], w_ada[:, c, 0:2 * C], start=(c == 0), stop=(c == NC_ - 1))
            last.then_inc(products, 1)
            for k in range(8):
                for c in range(NC_):
                    last = pe.matmul(ps[2 + k // 4][:, (k % 4) * B:(k % 4 + 1) * B],
                                     w_ada[:, c, 2 * C + k * P:2 * C + (k + 1) * P], cond_t[:, c, :],
                                     start=(c == 0), stop=(c == NC_ - 1))
            last.then_inc(products, 1)
            pe.wait_ge(emb_here, 16 * 4)
            for k in range(4):
                for c in range(NC_):
                    last = pe.matmul(ps[4][:, k * B:(k + 1) * B], w_emb[:, c, k * P:(k + 1) * P], cond_t[:, c, :],
                                     start=(c == 0), stop=(c == NC_ - 1))
            last.then_inc(products, 1)

        @block.vector
        def _(dve):
            dve.wait_ge(heads_here, 16)
            dve.tensor_scalar(head_scale[:], head_scale[:], LOG_100, None, ALU.min).then_inc(heads_made, 1)
            dve.wait_ge(heads_made, 1)
            dve.wait_ge(exp_done, 1)
            dve.tensor_reduce(top[:], head_exp[:], X_AXIS, ALU.max).then_inc(heads_made, 1)
            dve.wait_ge(heads_made, 2)
            dve.tensor_scalar(top[:], top[:], -80.0, 0.0, ALU.add, ALU.max).then_inc(heads_made, 1)
            dve.wait_ge(heads_made, 3)
            dve.tensor_scalar(m.minus_shift[:], top[:], -1.0, None, ALU.mult)
            dve.wait_ge(transposed, 1)
            dve.tensor_copy(cond_t[:], ps[0][:, 0:NC_ * B].rearrange("p (c b) -> p c b", c=NC_)).then_inc(cond_t_made, 1)
            dve.wait_ge(ada_here, 16 * 3)
            dve.wait_ge(products, 1)
            dve.tensor_tensor(gamma_rows[:], ps[1][:], b_ada_row[:], ALU.add).then_inc(gammas_made, 1)
            dve.wait_ge(products, 2)
            for k, (to, one) in enumerate(((m.scale1, 1.0), (m.scale2, 1.0), (m.shift1, 0.0), (m.shift2, 0.0))):
                for c in range(NC_):
                    i = k * NC_ + c
                    dve.tensor_scalar(to[:, c, :], ps[2 + i // 4][:, (i % 4) * B:(i % 4 + 1) * B],
                                      b_ada[:, 2 * NC_ + i:2 * NC_ + i + 1], one, ALU.add, ALU.add)
            dve.wait_ge(emb_here, 16 * 4)
            dve.tensor_scalar(b_sn_half[:], b_sn[:], 0.5, None, ALU.mult).then_inc(b_halved, 1)
            dve.wait_ge(products, 3)
            for c in range(NC_):
                dve.tensor_scalar(scale_plus[:, c, :], ps[4][:, c * B:(c + 1) * B], b_emb[:, c:c + 1], 1.0,
                                  ALU.add, ALU.add).then_inc(modulations, 1)
                dve.tensor_scalar(m.shift3[:, c, :], ps[4][:, (NC_ + c) * B:(NC_ + c + 1) * B],
                                  b_emb[:, NC_ + c:NC_ + c + 1], 0.5, ALU.add, ALU.mult).then_inc(modulations, 1)
            dve.wait_ge(modulations, 4)
            dve.wait_ge(b_halved, 1)
            for c in range(NC_):
                dve.tensor_scalar(m.scale3[:, c, :], scale_plus[:, c, :], g_sn[:, c:c + 1], 0.5, ALU.mult, ALU.mult)
                dve.scalar_tensor_tensor(m.shift3[:, c, :], scale_plus[:, c, :], b_sn_half[:, c:c + 1], m.shift3[:, c, :],
                                         ALU.mult, ALU.add)


def x_tiles(x):
    return x.rearrange("(j u s) l c -> (s l) j u c", s=SEQ, u=UNROLL)


def reuse(eng, sem, tile, slots, each=1):
    count = tile.since(slots, each)
    if count is not None:
        eng.wait_ge(sem, count)


def bank_free(eng, sem, tile, offset, each=1):
    n = tile.n + offset
    if isinstance(n, int):
        if n < 0:
            return
        n = min(n, TILES - 1)
    eng.wait_ge(sem, (n + 1) * each)


def attention_pass(nc, m, x, fc1_w):
    PAIRS = H // 2
    VW = HD + 1
    FIRST_OF_PART = [UNROLL * g for g in X_PARTS[:3]]
    with ExitStack() as ctx:
        def sb(name, shape, dt=F32, slots=2):
            return [ctx.enter_context(nc.sbuf_tensor(f"{name}{i}", shape, dt)) for i in range(slots)]

        def sem(name):
            return ctx.enter_context(nc.semaphore(name))

        stats = sb("stats", [P, 6])
        mean_var = sb("mean_var", [P, 2], F32, 4)
        rstd = sb("rstd", [P, 1], F32, 4)
        x_hat = sb("x_hat", [P, C])
        x1_t = sb("x1_t", [P, NC_, P])
        qk = sb("qk", [P, 2 * C], F32, 4)
        v_full = sb("v_full", [P, C], F32, 4)
        v_split = sb("v_split", [P, 2, PAIRS, 2, HD], BF16)
        v_pairs = sb("v_pairs", [P, SEQ, 2, 2, PAIRS, VW], BF16, 4)
        squares = sb("squares", [P, 2 * C])
        norms = sb("norms", [P, 2 * H])
        log_norms = sb("log_norms", [P, 2 * H])
        factors = sb("factors", [P, 2 * H])
        qk_hat = sb("qk_hat", [P, 2 * C])
        qk_t = sb("qk_t", [P, 2, 2, NC_, P], BF16)
        k_pairs = sb("k_pairs", [P, 2, NC_, SEQ, G_, 2, L], BF16)
        e_full = sb("e_full", [P, SEQ, PAIRS, L])
        e_split = sb("e_split", [P, 2, SEQ, PAIRS, L], BF16)
        inv_sum = sb("inv_sum", [P, SEQ, PAIRS // 2, 2])
        o_full = sb("o_full", [P, C])
        o_t = sb("o_t", [P, NC_, P])
        gain = sb("gain", [P, C], F32, 4)
        branch = sb("branch", [P, C])

        ps_x = ctx.enter_context(nc.psum_tensor("ps_x", [P, 512], F32))
        ps_qk = ctx.enter_context(nc.psum_tensor("ps_qk", [P, 512], F32))
        ps_v = ctx.enter_context(nc.psum_tensor("ps_v", [P, 512], F32))
        ps_qkt = ctx.enter_context(nc.psum_tensor("ps_qkt", [P, 512], F32))
        ps_s = ctx.enter_context(nc.psum_tensor("ps_s", [P, SEQ, PAIRS, L], F32))
        ps_o = ctx.enter_context(nc.psum_tensor("ps_o", [P, SEQ, 512], F32))

        o_blocks = ps_o[:, :, 0:PAIRS // 2 * 4 * VW].rearrange(
            "p s (k g r e) -> p s k g r e", k=PAIRS // 2, g=2, r=2)
        ps_xt, ps_ot = ps_x[:, 0:C], ps_x[:, C:2 * C]
        ps_vv, ps_y = ps_v[:, 0:C], ps_v[:, C:2 * C]

        gain_here = [sem(f"gain_here{i}") for i in range(4)]
        k_pairs_here = [sem(f"k_pairs_here{i}") for i in range(2)]
        fc1_hi_made = sem("fc1_hi_made")
        cleared = sem("cleared")
        k_cleared = sem("k_cleared")
        ones_set = sem("ones_set")
        stats_made = sem("stats_made")
        mean_made = sem("mean_made")
        var_eps_made = sem("var_eps_made")
        rstd_made = sem("rstd_made")
        x_hat_made = sem("x_hat_made")
        x_hat_t = sem("x_hat_t")
        x1_made = sem("x1_made")
        x1_second = sem("x1_second")
        qk_done = sem("qk_done")
        qkv_done = sem("qkv_done")
        qk_biased = sem("qk_biased")
        v_biased = sem("v_biased")
        v_hi_made = sem("v_hi_made")
        v_lo_made = sem("v_lo_made")
        v_placed = sem("v_placed")
        squared = sem("squared")
        norms_made = sem("norms_made")
        norms_weighted = sem("norms_weighted")
        logs_made = sem("logs_made")
        factors_made = sem("factors_made")
        qk_hat_made = sem("qk_hat_made")
        qk_turned = sem("qk_turned")
        qk_hi_made = sem("qk_hi_made")
        qk_lo_made = sem("qk_lo_made")
        scores_done = sem("scores_done")
        exp_made = sem("exp_made")
        e_lo_made = sem("e_lo_made")
        pv_done = sem("pv_done")
        sums_inverted = sem("sums_inverted")
        o_made = sem("o_made")
        o_turned = sem("o_turned")
        o_t_made = sem("o_t_made")
        proj_done = sem("proj_done")
        branch_made = sem("branch_made")
        branch_gained = sem("branch_gained")
        x_updated = sem("x_updated")
        block = ctx.enter_context(nc.Block())
        gamma1 = m.gammas.rearrange("(j u s) n -> s j u n", s=SEQ, u=UNROLL)

        @block.sync
        def _(sp):
            def load_gain(t):
                if isinstance(t.n, int):
                    reuse(sp, branch_gained, t, 4)
                for s in range(SEQ):
                    source = gamma1[s:s + 1, bass.ds(t.j, 1), t.u, 0:C]
                    sp.dma_start(gain[t.slot(4)][s * L:(s + 1) * L, :],
                                 source.rearrange("s j n -> (s j) n").to_broadcast([L, C])
                                 ).then_inc(gain_here[t.slot(4)], 16)

            def load_later(t):
                if isinstance(t.n, int) and t.n < GROUPS - X_PARTS[2]:
                    group = slice(X_PARTS[2] + t.n, X_PARTS[2] + t.n + 1)
                    sp.dma_start(m.x_all[:, group], x_tiles(x)[:, group]).then_inc(m.x_here[2], 16)
                if isinstance(t.n, int) and t.n == GROUPS - X_PARTS[2] - 1:
                    sp.dma_start(m.fc1_full[:], fc1_w.rearrange(CHUNKED, p=P)).then_inc(m.ff_here, 16)

            def place_k(t):
                if t.since(2) is None:
                    sp.wait_ge(k_cleared, 2)
                sp.wait_ge(qk_lo_made, t.n + 1)
                a = t.slot(2)
                for g in range(G_):
                    for r in range(2):
                        rows = slice((2 * g + r) * HD, (2 * g + r + 1) * HD)
                        sp.dma_start(
                            k_pairs[a][rows, :, :, :, g, r, :].rearrange("p a c s k -> p (a c s) k"),
                            qk_t[a][rows, 1].rearrange("p a c (s k) -> p (a c s) k", s=SEQ)
                        ).then_inc(k_pairs_here[a], 16)

            pipeline(sp, [(4, place_k), (0, load_later), (8, load_gain)])
            sp.wait_ge(x_updated, TILES)
            sp.wait_ge(m.ff_here, 16 * 3)

        @block.gpsimd
        def _(pool):
            for a in range(4):
                pool.memset(v_pairs[a][:], 0.0).then_inc(cleared, 1)
            pool.wait_ge(cleared, 4)
            for a in range(4):
                for r in range(2):
                    pool.memset(v_pairs[a][r * L:(r + 1) * L, :, HI, r, :, HD:VW], 1.0).then_inc(ones_set, 1)
            pool.wait_ge(ones_set, 8)

            def rstd_of(t):
                a = t.slot(2)
                reuse(pool, x_hat_made, t, 4)
                pool.wait_ge(mean_made, t.n + 1)
                pool.tensor_tensor(rstd[t.slot(4)][:], mean_var[t.slot(4)][:, 1:2], m.eps_ln[:], ALU.add).then_inc(var_eps_made, 1)
                pool.wait_ge(var_eps_made, t.n + 1)
                pool.tensor_tensor(rstd[t.slot(4)][:], rstd[t.slot(4)][:], m.minus_half[:, 0:1], ALU.pow).then_inc(rstd_made, 1)

            def normalise(t):
                a = t.slot(2)
                pool.wait_ge(factors_made, t.n + 1)
                reuse(pool, qk_turned, t, 2)
                pool.tensor_tensor(heads(qk_hat[a][:]), heads(qk[t.slot(4)][:]), over_channels(factors[a][:]), ALU.mult
                                   ).then_inc(qk_hat_made, 1)

            def update(t):
                a = t.slot(2)
                pool.wait_ge(branch_made, t.n + 1)
                pool.wait_ge(gain_here[t.slot(4)], (t.j + 1) * 16 * SEQ)
                pool.tensor_tensor(branch[a][:], branch[a][:], gain[t.slot(4)][:], ALU.mult).then_inc(branch_gained, 1)

            def add(t):
                a = t.slot(2)
                pool.wait_ge(branch_gained, t.n + 1)
                pool.tensor_tensor(t.rows(m.x_all), t.rows(m.x_all), branch[a][:, None, :], ALU.add
                                   ).then_inc(x_updated, 1)

            def split_fc1(t):
                if isinstance(t.n, int) and t.n == TILES - 1:
                    pool.wait_ge(fc1_hi_made, 1)
                    pool.tensor_tensor(m.w_fc1[:, LO], m.fc1_full[:], m.w_fc1[:, HI], ALU.subtract)

            def e_lo(t):
                a = t.slot(2)
                pool.wait_ge(exp_made, t.n + 1)
                reuse(pool, pv_done, t, 2)
                pool.tensor_tensor(flat(e_split[a][:, LO]), flat(e_full[a][:]), flat(e_split[a][:, HI]), ALU.subtract
                                   ).then_inc(e_lo_made, 1)

            pipeline(pool, [(4, normalise), (1, rstd_of), (10, update), (10, add), (6, e_lo), (7, split_fc1)])

        @block.scalar
        def _(act):
            def modulate_second(t):
                a = t.slot(2)
                act.wait_ge(x1_made, t.n + 1)
                reuse(act, qkv_done, t, 2)
                for s in range(SEQ):
                    act.activation(x1_t[a][:, 1, s * L:(s + 1) * L], ps_xt[:, P + s * L:P + (s + 1) * L], ACT.Identity,
                                   bias=by_seq(m.shift1, 1, t, s), scale=by_seq(m.scale1, 1, t, s)
                                   ).then_inc(x1_second, 1)

            def square(t):
                a = t.slot(2)
                act.wait_ge(qk_biased, t.n + 1)
                reuse(act, norms_made, t, 2)
                act.activation(squares[a][:], qk[t.slot(4)][:], ACT.Square).then_inc(squared, 1)

            def v_hi(t):
                a = t.slot(2)
                act.wait_ge(v_biased, t.n + 1)
                reuse(act, v_placed, t, 2)
                act.activation(v_split[a][:, HI].rearrange("p k r e -> p (k r e)"), v_full[t.slot(4)][:], ACT.Copy
                               ).then_inc(v_hi_made, 1)

            def logs(t):
                a = t.slot(2)
                act.wait_ge(norms_weighted, t.n + 1)
                reuse(act, factors_made, t, 2)
                act.activation(log_norms[a][:], norms[a][:], ACT.Ln, scale=65536.0).then_inc(logs_made, 1)

            def factor(t):
                a = t.slot(2)
                act.wait_ge(logs_made, t.n + 1)
                reuse(act, qk_hat_made, t, 2)
                act.activation(factors[a][:], log_norms[a][:], ACT.Exp, bias=m.log_256[:], scale=-0.5).then_inc(factors_made, 1)

            def qk_hi(t):
                a = t.slot(2)
                act.wait_ge(qk_turned, t.n + 1)
                reuse(act, scores_done, t, 2)
                act.activation(qk_t[a][:, :, HI].rearrange("p w c k -> p w (c k)"),
                               ps_qkt[:, :].rearrange("p (w k) -> p w k", w=2), ACT.Copy).then_inc(qk_hi_made, 1)

            def split_fc1(t):
                if isinstance(t.n, int) and t.n == TILES - 1:
                    act.wait_ge(m.ff_here, 16 * 3)
                    act.activation(m.w_fc1[:, HI], m.fc1_full[:], ACT.Copy).then_inc(fc1_hi_made, 1)

            def high_exponentials(t):
                a = t.slot(2)
                act.wait_ge(scores_done, t.n + 1)
                reuse(act, pv_done, t, 2)
                act.activation(flat(e_split[a][:, HI]), flat(ps_s[:]), ACT.Exp, bias=m.minus_shift[:])

            def full_exponentials(t):
                a = t.slot(2)
                reuse(act, e_lo_made, t, 2)
                act.activation(flat(e_full[a][:]), flat(ps_s[:]), ACT.Exp, bias=m.minus_shift[:]).then_inc(exp_made, 1)

            def o_copy(t):
                a = t.slot(2)
                act.wait_ge(o_turned, t.n + 1)
                reuse(act, proj_done, t, 2)
                act.activation(o_t[a][:].rearrange("p c k -> p (c k)"), ps_ot, ACT.Copy).then_inc(o_t_made, 1)

            act.preload_act_table_set("natural_log_exp_and_others")
            pipeline(act, [(3, square), (6, high_exponentials), (2, modulate_second), (4, split_fc1), (4, qk_hi),
                           (6, full_exponentials), (3, logs), (3, factor), (4, v_hi), (8, o_copy)])

        @block.tensor
        def _(pe):
            def project(t):
                a = t.slot(2)
                pe.wait_ge(o_t_made, t.n + 1)
                reuse(pe, branch_made, t, 1)
                bank_free(pe, v_biased, t, 6)
                for c in range(NC_):
                    last = pe.matmul(ps_y, o_t[a][:, c, :], m.w_proj[:, c, :], start=(c == 0), stop=(c == NC_ - 1))
                last.then_inc(proj_done, 1)

            def turn_o(t):
                a = t.slot(2)
                pe.wait_ge(o_made, t.n + 1)
                reuse(pe, o_t_made, t, 1)
                bank_free(pe, x1_second, t, 6, SEQ)
                for c in range(NC_):
                    last = pe.transpose(ps_ot[:, c * P:(c + 1) * P], o_full[a][:, c * P:(c + 1) * P], m.ident[:])
                last.then_inc(o_turned, 1)

            def probs_v(t):
                a = t.slot(2)
                pe.wait_ge(e_lo_made, t.n + 1)
                pe.wait_ge(v_placed, t.n + 1)
                if isinstance(t.n, int) and t.n < 4:
                    pe.wait_ge(ones_set, 8)
                reuse(pe, o_made, t, 1)
                for s in range(SEQ):
                    for k in range(PAIRS // 2):
                        for i, (e, v) in enumerate(((HI, HI), (HI, LO), (LO, HI))):
                            last = pe.matmul(
                                o_blocks[:, s, k].rearrange("p g r e -> p (g r e)"),
                                e_split[a][:, e, s, 2 * k:2 * k + 2].rearrange("p k q -> p (k q)"),
                                v_pairs[t.slot(4)][:, s, v, :, 2 * k:2 * k + 2].rearrange("p r k e -> p k r e"),
                                start=(i == 0), stop=(i == 2))
                last.then_inc(pv_done, 1)

            def scores(t):
                a = t.slot(2)
                pe.wait_ge(k_pairs_here[a], half(t, 16 * HPC))
                reuse(pe, exp_made, t, 1)
                for s in range(SEQ):
                    for c in range(NC_):
                        for g in range(G_):
                            for i, (k, q) in enumerate(((HI, HI), (HI, LO), (LO, HI))):
                                last = pe.matmul(ps_s[:, s, G_ * c + g],
                                                 k_pairs[a][:, k, c, s, g].rearrange("p r k -> p (r k)"),
                                                 qk_t[a][:, 0, q, c, s * L:(s + 1) * L], start=(i == 0), stop=(i == 2))
                last.then_inc(scores_done, 1)

            def turn_qk(t):
                a = t.slot(2)
                pe.wait_ge(qk_hat_made, t.n + 1)
                reuse(pe, qk_lo_made, t, 1)
                for k in range(2 * NC_):
                    last = pe.transpose(ps_qkt[:, k * P:(k + 1) * P], qk_hat[a][:, k * P:(k + 1) * P], m.ident[:])
                last.then_inc(qk_turned, 1)

            def qkv(t):
                a = t.slot(2)
                pe.wait_ge(x1_second, (t.n + 1) * SEQ)
                reuse(pe, qk_biased, t, 1)
                for c in range(NC_):
                    last = pe.matmul(ps_qk[:, :], x1_t[a][:, c, :], m.w_qkv[:, c, 0:2 * C],
                                     start=(c == 0), stop=(c == NC_ - 1))
                last.then_inc(qk_done, 1)
                reuse(pe, v_biased, t, 1)
                bank_free(pe, branch_made, t, -7)
                for c in range(NC_):
                    last = pe.matmul(ps_vv, x1_t[a][:, c, :], m.w_qkv[:, c, 2 * C:3 * C], start=(c == 0), stop=(c == NC_ - 1))
                last.then_inc(qkv_done, 1)

            def turn_x(t):
                a = t.slot(2)
                pe.wait_ge(x_hat_made, t.n + 1)
                reuse(pe, x1_second, t, 1, SEQ)
                bank_free(pe, o_t_made, t, -7)
                for c in range(NC_):
                    last = pe.transpose(ps_xt[:, c * P:(c + 1) * P], x_hat[a][:, c * P:(c + 1) * P], m.ident[:])
                last.then_inc(x_hat_t, 1)

            pipeline(pe, [(6, scores), (4, turn_qk), (9, project), (7, probs_v), (8, turn_o), (2, qkv), (1, turn_x)])

        @block.vector
        def _(dve):
            def reduce_norms(t):
                a = t.slot(2)
                dve.wait_ge(squared, t.n + 1)
                reuse(dve, logs_made, t, 2)
                dve.tensor_reduce(norms[a][:], heads(squares[a][:]), X_AXIS, ALU.add).then_inc(norms_made, 1)
                dve.wait_ge(norms_made, t.n + 1)
                dve.scalar_tensor_tensor(norms[a][:], norms[a][:], 1e-24, m.norm_weight[:], ALU.max, ALU.mult
                                         ).then_inc(norms_weighted, 1)

            def modulate(t):
                a = t.slot(2)
                dve.wait_ge(x_hat_t, t.n + 1)
                reuse(dve, qkv_done, t, 2)
                for s in range(SEQ):
                    at = slice(s * L, (s + 1) * L)
                    last = dve.tensor_scalar(x1_t[a][:, 0, at], ps_xt[:, at], by_seq(m.scale1, 0, t, s),
                                             by_seq(m.shift1, 0, t, s), ALU.mult, ALU.add)
                last.then_inc(x1_made, 1)

            def residual(t):
                a = t.slot(2)
                dve.wait_ge(proj_done, t.n + 1)
                reuse(dve, x_updated, t, 2)
                dve.tensor_tensor(branch[a][:], ps_y, m.b_proj[:], ALU.add).then_inc(branch_made, 1)

            def v_low(t):
                a = t.slot(2)
                dve.wait_ge(v_hi_made, t.n + 1)
                reuse(dve, v_placed, t, 2)
                dve.tensor_tensor(v_split[a][:, LO].rearrange("p k r e -> p (k r e)"), v_full[t.slot(4)][:],
                                   v_split[a][:, HI].rearrange("p k r e -> p (k r e)"), ALU.subtract
                                   ).then_inc(v_lo_made, 1)

            def place_v(t):
                a = t.slot(2)
                dve.wait_ge(v_lo_made, t.n + 1)
                reuse(dve, pv_done, t, 4)
                if isinstance(t.n, int) and t.n < 4:
                    dve.wait_ge(cleared, 4)
                for s in range(SEQ):
                    for r in range(2):
                        last = dve.tensor_copy(v_pairs[t.slot(4)][r * L:(r + 1) * L, s, :, r, :, 0:HD],
                                               v_split[a][s * L:(s + 1) * L, :, :, r, :])
                last.then_inc(v_placed, 1)

            def outputs(t):
                a = t.slot(2)
                dve.wait_ge(pv_done, t.n + 1)
                dve.reciprocal(inv_sum[a][:], o_blocks[:, :, :, 0, :, HD]).then_inc(sums_inverted, 1)
                dve.wait_ge(sums_inverted, t.n + 1)
                reuse(dve, o_turned, t, 2)
                for g in range(2):
                    for s in range(SEQ):
                        to = o_full[a][s * L:(s + 1) * L, :].rearrange("p (k g r e) -> p k g r e", g=2, r=2, e=HD)[:, :, g]
                        last = dve.tensor_tensor(
                            to, o_blocks[g * L:(g + 1) * L, s, :, g, :, 0:HD],
                            inv_sum[a][g * L:(g + 1) * L, s, :, :, None].to_broadcast([L, PAIRS // 2, 2, HD]), ALU.mult)
                last.then_inc(o_made, 1)

            def statistics(t):
                a = t.slot(2)
                if isinstance(t.n, int) and t.n in FIRST_OF_PART:
                    part = FIRST_OF_PART.index(t.n)
                    dve.wait_ge(m.x_here[part], 16 * (GROUPS - X_PARTS[2] if part == 2 else 1))
                if not isinstance(t.n, int) or t.n:
                    dve.wait_ge(stats_made, t.n)
                reuse(dve, mean_made, t, 2)
                reuse(dve, x_hat_made, t, 4)
                dve.bn_stats(stats[a][:], t.rows(m.x_all).rearrange("p j n -> p (j n)")).then_inc(stats_made, 1)

            def aggregate(t):
                a = t.slot(2)
                if t.n is TILES - 1:
                    dve.wait_ge(stats_made, TILES)
                    dve.wait_ge(x_hat_made, TILES - 4)
                dve.bn_aggr(mean_var[t.slot(4)][:], stats[a][:]).then_inc(mean_made, 1)

            def qk_lo(t):
                a = t.slot(2)
                dve.wait_ge(qk_hi_made, t.n + 1)
                dve.tensor_tensor(qk_t[a][:, :, LO].rearrange("p w c k -> p w (c k)"),
                                  ps_qkt[:, :].rearrange("p (w k) -> p w k", w=2),
                                  qk_t[a][:, :, HI].rearrange("p w c k -> p w (c k)"), ALU.subtract).then_inc(qk_lo_made, 1)

            def hat(t):
                a = t.slot(2)
                dve.wait_ge(rstd_made, t.n + 1)
                reuse(dve, x_hat_t, t, 2)
                dve.tensor_scalar(x_hat[a][:, None, :], t.rows(m.x_all), mean_var[t.slot(4)][:, 0:1], rstd[t.slot(4)][:],
                                  ALU.subtract, ALU.mult).then_inc(x_hat_made, 1)

            def biases(t):
                a = t.slot(2)
                dve.wait_ge(qk_done, t.n + 1)
                reuse(dve, qk_hat_made, t, 4)
                dve.tensor_tensor(qk[t.slot(4)][:], ps_qk[:, :], m.b_qkv[:, 0:2 * C], ALU.add).then_inc(qk_biased, 1)
                dve.wait_ge(qkv_done, t.n + 1)
                reuse(dve, v_lo_made, t, 4)
                dve.tensor_tensor(v_full[t.slot(4)][:], ps_vv, m.b_qkv[:, 2 * C:3 * C], ALU.add).then_inc(v_biased, 1)

            for a in range(2):
                dve.memset(k_pairs[a][:], 0.0).then_inc(k_cleared, 1)
            pipeline(dve, [(3, biases), (2, modulate), (8, outputs), (5, place_v), (3, reduce_norms), (4, qk_lo),
                           (1, hat), (9, residual), (-1, statistics), (0, aggregate), (4, v_low)])



def half(t, each):
    return ((t.j * UNROLL + t.u) // 2 + 1) * each if isinstance(t.j, int) else (t.j * (UNROLL // 2) + t.u // 2 + 1) * each


def heads(a):
    return a.rearrange("p (h e) -> p h e", e=HD)


def over_channels(a):
    return a[:, :, None].to_broadcast([a.shape[0], a.shape[1], HD])


def flat(a):
    names = " ".join("abcdef"[:len(a.shape) - 1])
    return a.rearrange(f"p {names} -> p ({names})")


def by_seq(a, c, t, s):
    return a[:, c, :].rearrange("p (j k) -> p j k", k=UNROLL * SEQ)[:, bass.ds(t.j, 1), t.u * SEQ + s]


def feed_forward_pass(nc, m, fc2_w, wq, wk, wv, out_w):
    T = UNROLL
    BLOCKS = TILES // T
    SPLITS = ((HI, HI), (HI, LO), (LO, HI))
    F_CHUNKS = D_FF // P
    N = T * P
    with ExitStack() as ctx:
        def sb(name, shape, dt=F32, slots=2):
            return [ctx.enter_context(nc.sbuf_tensor(f"f_{name}{i}", shape, dt)) for i in range(slots)]

        def sem(name):
            return ctx.enter_context(nc.semaphore(f"f_{name}"))

        fc2_full = sb("fc2_full", [P, F_CHUNKS, C], F32, 1)[0]
        stats = sb("stats", [P, T, 6])
        mean_var = sb("mean_var", [P, T, 2])
        rstd = sb("rstd", [P, T])
        x_hat = sb("x_hat", [P, T, C])
        x2 = sb("x2", [P, NC_, N], F32, 1)[0]
        x2_split = sb("x2_split", [P, 2, NC_, N], BF16)
        h = sb("h", [P, N], F32, 4)
        h_split = sb("h_split", [P, 2, F_CHUNKS, N], BF16)
        gain = sb("gain", [P, T, C])
        branch = sb("branch", [P, T, C])
        ps_t = ctx.enter_context(nc.psum_tensor("f_ps_t", [P, NC_, N], F32))
        ps_h = [ctx.enter_context(nc.psum_tensor(f"f_ps_h{i}", [P, N], F32)) for i in range(4)]
        ps_y = ctx.enter_context(nc.psum_tensor("f_ps_y", [P, T, C], F32))

        gain_here = [sem(f"gain_here{i}") for i in range(2)]
        fc2_here = sem("fc2_here")
        w_hi_made = sem("w_hi_made")
        w_lo_made = sem("w_lo_made")
        stats_made = sem("stats_made")
        mean_made = sem("mean_made")
        var_eps_made = sem("var_eps_made")
        rstd_made = sem("rstd_made")
        x_hat_made = sem("x_hat_made")
        x_turned = sem("x_turned")
        x_scaled = sem("x_scaled")
        x2_made = sem("x2_made")
        x2_hi_made = sem("x2_hi_made")
        x2_lo_made = sem("x2_lo_made")
        fc1_done = sem("fc1_done")
        h_made = sem("h_made")
        h_lo_even = sem("h_lo_even")
        h_lo_odd = sem("h_lo_odd")
        fc2_done = sem("fc2_done")
        branch_made = sem("branch_made")
        branch_gained = sem("branch_gained")
        x_updated = sem("x_updated")
        block = ctx.enter_context(nc.Block())
        gamma2 = m.gammas.rearrange("(b u s) n -> s b u n", s=SEQ, u=T)

        def rows(t):
            return m.x_all[:, bass.ds(t.n, 1)].rearrange("p b u n -> p (b u) n")

        def by_block(a, t):
            a = a[:].rearrange("p c (b s) -> p c b s", s=T * SEQ)[:, :, bass.ds(t.n, 1), :]
            return a.rearrange("p c b s -> p c (b s)")[:, :, :, None].to_broadcast([P, NC_, T * SEQ, L])

        def run(eng, stages):
            pipeline(eng, stages, BLOCKS, 2, 2)

        @block.sync
        def _(sp):
            sp.dma_start(fc2_full[:], fc2_w.rearrange(CHUNKED, p=P)).then_inc(fc2_here, 16)
            for to, source in ((m.w_qv3[:, :, 0:C], wq), (m.w_qv3[:, :, C:2 * C], wv), (m.w_k3[:], wk), (m.w_out3[:], out_w)):
                sp.dma_start(to, source.rearrange(CHUNKED, p=P)).then_inc(m.linear_here, 16)
            sp.wait_ge(m.linear_here, 16 * 10)

        @block.gpsimd
        def _(pool):
            def shift(t):
                pool.wait_ge(x_scaled, t.n + 1)
                pool.tensor_tensor(x2[:].rearrange("p c (s l) -> p c s l", l=L),
                                   x2[:].rearrange("p c (s l) -> p c s l", l=L), by_block(m.shift2, t), ALU.add
                                   ).then_inc(x2_made, 1)

            def rstd_of(t):
                a = t.slot(2)
                reuse(pool, x_hat_made, t, 2, T)
                pool.wait_ge(mean_made, (t.n + 1) * T)
                pool.tensor_tensor(rstd[a][:], mean_var[a][:, :, 1], m.eps_ln[:].to_broadcast([P, T]), ALU.add
                                   ).then_inc(var_eps_made, 1)
                pool.wait_ge(var_eps_made, t.n + 1)
                pool.tensor_tensor(rstd[a][:], rstd[a][:], m.minus_half[:], ALU.pow).then_inc(rstd_made, 1)

            def update(t):
                a = t.slot(2)
                pool.wait_ge(branch_made, t.n + 1)
                pool.wait_ge(gain_here[a], (t.j + 1) * 16 * SEQ)
                pool.tensor_tensor(branch[a][:], branch[a][:], gain[a][:], ALU.mult).then_inc(branch_gained, 1)

            def add(t):
                a = t.slot(2)
                pool.wait_ge(branch_gained, t.n + 1)
                pool.tensor_tensor(rows(t), rows(t), branch[a][:], ALU.add).then_inc(x_updated, 1)

            def split_fc2(t):
                if isinstance(t.n, int) and t.n == 0:
                    pool.wait_ge(w_hi_made, 1)
                    pool.tensor_tensor(m.w_fc2[:, LO], fc2_full[:], m.w_fc2[:, HI], ALU.subtract).then_inc(w_lo_made, 1)

            def h_low_odd(t):
                a = t.slot(2)
                for f in range(1, F_CHUNKS, 2):
                    pool.wait_ge(h_made, t.n * F_CHUNKS + f + 1)
                    pool.tensor_tensor(h_split[a][:, LO, f], h[f % 4][:], h_split[a][:, HI, f], ALU.subtract
                                       ).then_inc(h_lo_odd, 1)

            run(pool, [(2, shift), (2, split_fc2), (0, rstd_of), (5, update), (5, add), (3, h_low_odd)])

        @block.scalar
        def _(act):
            def load_gain(t):
                a = t.slot(2)
                reuse(act, branch_gained, t, 2)
                for s in range(SEQ):
                    source = gamma2[s:s + 1, bass.ds(t.n, 1), :, C:2 * C].rearrange("s b u n -> (s b) u n")
                    act.dma_start(gain[a][s * L:(s + 1) * L], source.to_broadcast([L, T, C])
                                  ).then_inc(gain_here[a], 16)

            def split_fc2(t):
                if isinstance(t.n, int) and t.n == 0:
                    act.wait_ge(fc2_here, 16)
                    act.activation(m.w_fc2[:, HI], fc2_full[:], ACT.Copy).then_inc(w_hi_made, 1)

            def x2_high(t):
                a = t.slot(2)
                act.wait_ge(x2_made, t.n + 1)
                reuse(act, fc1_done, t, 2, F_CHUNKS)
                act.activation(x2_split[a][:, HI], x2[:], ACT.Copy).then_inc(x2_hi_made, 1)

            def gelus(t):
                a = t.slot(2)
                reuse(act, fc2_done, t, 2, 2)
                for f in range(F_CHUNKS):
                    act.wait_ge(fc1_done, t.n * F_CHUNKS + f + 1)
                    if f >= 4 or not isinstance(t.n, int) or t.n > 0:
                        half_way = t.n * (F_CHUNKS // 2) + f // 2 - 1
                        act.wait_ge(h_lo_odd if f % 2 else h_lo_even, half_way)
                    act.activation(h_split[a][:, HI, f], ps_h[f % 4][:], ACT.Gelu, bias=m.b_fc1[:, f:f + 1])
                    act.activation(h[f % 4][:], ps_h[f % 4][:], ACT.Gelu, bias=m.b_fc1[:, f:f + 1]).then_inc(h_made, 1)

            run(act, [(0, split_fc2), (4, load_gain), (2, x2_high), (3, gelus)])

        @block.tensor
        def _(pe):
            def fc2(t, tiles):
                a = t.slot(2)
                pe.wait_ge(h_lo_even, (t.n + 1) * (F_CHUNKS // 2))
                pe.wait_ge(h_lo_odd, (t.n + 1) * (F_CHUNKS // 2))
                if isinstance(t.n, int) and t.n == 0:
                    pe.wait_ge(w_lo_made, 1)
                reuse(pe, branch_made, t, 1)
                for i in tiles:
                    for f in range(F_CHUNKS):
                        for k, (hs, ws) in enumerate(SPLITS):
                            last = pe.matmul(ps_y[:, i], h_split[a][:, hs, f, i * P:(i + 1) * P], m.w_fc2[:, ws, f],
                                             start=(f == 0 and k == 0), stop=(f == F_CHUNKS - 1 and k == 2))
                last.then_inc(fc2_done, 1)

            def fc2_first(t):
                fc2(t, range(T // 2))

            def fc2_second(t):
                fc2(t, range(T // 2, T))

            def turn_x(t):
                a = t.slot(2)
                pe.wait_ge(x_hat_made, (t.n + 1) * T)
                reuse(pe, x_scaled, t, 1)
                for i in range(T):
                    for c in range(NC_):
                        last = pe.transpose(ps_t[:, c, i * P:(i + 1) * P], x_hat[a][:, i, c * P:(c + 1) * P], m.ident[:])
                last.then_inc(x_turned, 1)

            def fc1(t, chunks):
                a = t.slot(2)
                pe.wait_ge(x2_lo_made, t.n + 1)
                for f in chunks:
                    if f >= 4 or not isinstance(t.n, int) or t.n > 0:
                        pe.wait_ge(h_made, t.n * F_CHUNKS + f - 3)
                    for k, (ws, xs) in enumerate(SPLITS):
                        for c in range(NC_):
                            last = pe.matmul(ps_h[f % 4][:], m.w_fc1[:, ws, c, f * P:(f + 1) * P], x2_split[a][:, xs, c],
                                             start=(k == 0 and c == 0), stop=(k == 2 and c == NC_ - 1))
                    last.then_inc(fc1_done, 1)

            def fc1_first(t):
                fc1(t, range(F_CHUNKS // 2))

            def fc1_second(t):
                fc1(t, range(F_CHUNKS // 2, F_CHUNKS))

            run(pe, [(3, fc1_first), (4, fc2_first), (3, fc1_second), (1, turn_x), (4, fc2_second)])

        @block.vector
        def _(dve):
            def scale(t):
                dve.wait_ge(x_turned, t.n + 1)
                reuse(dve, x2_hi_made, t, 1)
                reuse(dve, x2_lo_made, t, 1)
                dve.tensor_tensor(x2[:].rearrange("p c (s l) -> p c s l", l=L),
                                  ps_t[:].rearrange("p c (s l) -> p c s l", l=L), by_block(m.scale2, t), ALU.mult
                                  ).then_inc(x_scaled, 1)

            def hat(t):
                a = t.slot(2)
                dve.wait_ge(rstd_made, t.n + 1)
                reuse(dve, x_turned, t, 2)
                for i in range(T):
                    dve.tensor_scalar(x_hat[a][:, i], rows(t)[:, i], mean_var[a][:, i, 0:1], rstd[a][:, i:i + 1],
                                      ALU.subtract, ALU.mult).then_inc(x_hat_made, 1)

            def statistics(t):
                a = t.slot(2)
                if not isinstance(t.n, int) or t.n:
                    dve.wait_ge(stats_made, t.n * T)
                reuse(dve, x_hat_made, t, 2, T)
                for i in range(T):
                    dve.bn_stats(stats[a][:, i], rows(t)[:, i]).then_inc(stats_made, 1)

            def aggregate(t):
                a = t.slot(2)
                if t.n is BLOCKS - 1:
                    dve.wait_ge(stats_made, BLOCKS * T)
                    dve.wait_ge(x_hat_made, (BLOCKS - 2) * T)
                for i in range(T):
                    dve.bn_aggr(mean_var[a][:, i], stats[a][:, i]).then_inc(mean_made, 1)

            def x2_low(t):
                a = t.slot(2)
                dve.wait_ge(x2_hi_made, t.n + 1)
                reuse(dve, fc1_done, t, 2, F_CHUNKS)
                dve.tensor_tensor(x2_split[a][:, LO], x2[:], x2_split[a][:, HI], ALU.subtract).then_inc(x2_lo_made, 1)

            def residual(t):
                a = t.slot(2)
                dve.wait_ge(fc2_done, (t.n + 1) * 2)
                reuse(dve, x_updated, t, 2)
                dve.tensor_tensor(branch[a][:], ps_y[:], m.b_fc2[:, None, :].to_broadcast([P, T, C]), ALU.add
                                  ).then_inc(branch_made, 1)

            def h_low_even(t):
                a = t.slot(2)
                reuse(dve, fc2_done, t, 2, 2)
                for f in range(0, F_CHUNKS, 2):
                    dve.wait_ge(h_made, t.n * F_CHUNKS + f + 1)
                    dve.tensor_tensor(h_split[a][:, LO, f], h[f % 4][:], h_split[a][:, HI, f], ALU.subtract
                                      ).then_inc(h_lo_even, 1)

            run(dve, [(2, scale), (1, hat), (-1, statistics), (0, aggregate), (2, x2_low), (3, h_low_even),
                      (4, residual)])


def linear_pass(nc, m, cond, out):
    SPLITS = ((HI, HI), (HI, LO), (LO, HI))
    Y_LAG = 8
    NK = NC_ * SEQ
    with ExitStack() as ctx:
        def sb(name, shape, dt=F32, slots=2):
            return [ctx.enter_context(nc.sbuf_tensor(f"l_{name}{i}", shape, dt)) for i in range(slots)]

        def ps(name, shape):
            return ctx.enter_context(nc.psum_tensor(f"l_{name}", shape, F32))

        def sem(name):
            return ctx.enter_context(nc.semaphore(f"l_{name}"))

        stats = sb("stats", [P, 6])
        mean_var = sb("mean_var", [P, 2, 2])
        rstd = sb("rstd", [P, 2])
        x_hat = sb("x_hat", [P, C])
        x3_t = sb("x3_t", [P, NC_, P])
        kq = sb("kq", [P, 2 * C], F32, 4)
        k_tops = sb("k_tops", [P, NC_, SEQ])
        k_shift = sb("k_shift", [P, NC_, SEQ])
        q_tops = sb("q_tops", [P, H])
        sums = sb("sums", [P, NK + H], F32, 4)
        v_full = sb("v_full", [P, C], F32, 4)
        v_split = sb("v_split", [P, 2, C], BF16, 4)
        kq_t = sb("kq_t", [P, 2, 2 * C], BF16, 4)
        kv = sb("kv", [P, NC_, SEQ, P])
        kv_split = sb("kv_split", [P, 2, NC_, SEQ, P], BF16)
        y_stats = sb("y_stats", [P, 6])
        y_hat = sb("y_hat", [P, C])
        z_t = sb("z_t", [P, NC_, P])
        tanh = sb("tanh", [P, NC_, P])
        silu = sb("silu", [P, NC_, P])
        gate = sb("gate", [P, C], F32, 4)
        branch = sb("branch", [P, C])
        ps_xt = ps("ps_xt", [P, NC_, P])
        ps_qv = ps("ps_qv", [P, 2 * C])
        ps_k = ps("ps_k", [P, NC_, P])
        ps_kq = ps("ps_kq", [P, 2 * C])
        ps_kv = ps("ps_kv", [P, NC_, SEQ, P])
        ps_y = ps("ps_y", [P, C])
        ps_yt = ps("ps_yt", [P, NC_, P])
        ps_out = ps("ps_out", [P, C])

        gate_here = [sem(f"gate_here{i}") for i in range(4)]
        stats_made = sem("stats_made")
        mean_made = sem("mean_made")
        var_eps_made = sem("var_eps_made")
        rstd_made = sem("rstd_made")
        x_hat_made = sem("x_hat_made")
        x_turned = sem("x_turned")
        x3_made = sem("x3_made")
        k_done = sem("k_done")
        qv_done = sem("qv_done")
        k_top_found = sem("k_top_found")
        k_top_biased = sem("k_top_biased")
        k_shift_made = sem("k_shift_made")
        k_exp_made = sem("k_exp_made")
        q_biased = sem("q_biased")
        v_biased = sem("v_biased")
        v_hi_made = sem("v_hi_made")
        v_lo_made = sem("v_lo_made")
        tops_made = sem("tops_made")
        q_lowered = sem("q_lowered")
        q_exp_made = sem("q_exp_made")
        sums_made = sem("sums_made")
        sums_inverted = sem("sums_inverted")
        softmax_made = sem("softmax_made")
        kq_turned = sem("kq_turned")
        kq_hi_made = sem("kq_hi_made")
        kq_lo_made = sem("kq_lo_made")
        kv_first = sem("kv_first")
        kv_done = sem("kv_done")
        kv_masked = sem("kv_masked")
        kv_hi_made = sem("kv_hi_made")
        kv_lo_made = sem("kv_lo_made")
        y_done = sem("y_done")
        y_stats_made = sem("y_stats_made")
        y_mean_made = sem("y_mean_made")
        y_hat_made = sem("y_hat_made")
        y_turned = sem("y_turned")
        z_made = sem("z_made")
        tanh_made = sem("tanh_made")
        silu_made = sem("silu_made")
        out_done = sem("out_done")
        branch_made = sem("branch_made")
        branch_gained = sem("branch_gained")
        x_updated = sem("x_updated")
        stored = sem("stored")
        block = ctx.enter_context(nc.Block())
        gates = cond.rearrange("(j u s) n -> s j u n", s=SEQ, u=UNROLL)

        def k_of(a):
            return a[:, 0:C].rearrange("p (k l) -> p k l", l=L)

        def q_of(a):
            return a[:, C:2 * C].rearrange("p (h e) -> p h e", e=HD)

        def by_token(a):
            return a[:, :, None].to_broadcast([P, NK, L])

        def by_seq_over_tokens(a, t):
            a = a[:].rearrange("p c (j u s) -> p c j u s", u=UNROLL, s=SEQ)[:, :, bass.ds(t.j, 1), t.u, :]
            return a.rearrange("p c j s -> p c (j s)")[:, :, :, None].to_broadcast([P, NC_, SEQ, L])

        def tokens_by_seq(a):
            return a.rearrange("p c (s l) -> p c s l", l=L)

        @block.sync
        def _(sp):
            sp.wait_ge(stored, 16 * GROUPS)

        @block.gpsimd
        def _(pool):
            def update(t):
                a = t.slot(2)
                pool.wait_ge(branch_made, t.n + 1)
                pool.wait_ge(gate_here[t.slot(4)], (t.j + 1) * 16 * SEQ)
                pool.tensor_tensor(branch[a][:], branch[a][:], gate[t.slot(4)][:], ALU.mult).then_inc(branch_gained, 1)

            def add(t):
                a = t.slot(2)
                pool.wait_ge(branch_gained, t.n + 1)
                pool.tensor_tensor(t.rows(m.x_all), t.rows(m.x_all), branch[a][:, None, :], ALU.add
                                   ).then_inc(x_updated, 1)

            def kv_low(t):
                a = t.slot(2)
                pool.wait_ge(kv_hi_made, t.n + 1)
                reuse(pool, y_done, t, 2)
                pool.tensor_tensor(kv_split[a][:, LO], kv[a][:], kv_split[a][:, HI], ALU.subtract
                                   ).then_inc(kv_lo_made, 1)

            def softmax(t):
                a = t.slot(2)
                pool.wait_ge(sums_inverted, t.n + 1)
                pool.tensor_tensor(k_of(kq[t.slot(4)]), k_of(kq[t.slot(4)]), by_token(sums[t.slot(4)][:, 0:NK]), ALU.mult
                                   ).then_inc(softmax_made, 1)
                pool.tensor_tensor(q_of(kq[t.slot(4)]), q_of(kq[t.slot(4)]), over_channels(sums[t.slot(4)][:, NK:]), ALU.mult
                                   ).then_inc(softmax_made, 1)

            def lower(t):
                a = t.slot(2)
                pool.wait_ge(tops_made, t.n + 1)
                pool.tensor_tensor(q_of(kq[t.slot(4)]), q_of(kq[t.slot(4)]), over_channels(q_tops[a][:]), ALU.subtract
                                   ).then_inc(q_lowered, 1)

            def v_low(t):
                pool.wait_ge(v_hi_made, t.n + 1)
                reuse(pool, kv_done, t, 4)
                pool.tensor_tensor(v_split[t.slot(4)][:, LO], v_full[t.slot(4)][:], v_split[t.slot(4)][:, HI],
                                   ALU.subtract).then_inc(v_lo_made, 1)

            def inverse_deviations(t):
                a = t.slot(2)
                first = isinstance(t.n, int) and t.n < Y_LAG
                pool.wait_ge(mean_made, t.n + 1)
                reuse(pool, x_hat_made, t, 2)
                if not first:
                    pool.wait_ge(y_mean_made, t.n + 1 - Y_LAG)
                power(a, slice(0, 1 if first else 2), t.n + 1)

            def last_inverse_deviations(t):
                if isinstance(t.n, int) and t.n + Y_LAG >= TILES:
                    pool.wait_ge(y_mean_made, t.n + 1)
                    power((t.n + Y_LAG) % 2, slice(1, 2), t.n + Y_LAG + 1)

            def power(a, which, nth):
                width = which.stop - which.start
                pool.tensor_tensor(rstd[a][:, which], mean_var[a][:, which, 1], m.eps_norm3[:].to_broadcast([P, width]),
                                   ALU.add).then_inc(var_eps_made, 1)
                pool.wait_ge(var_eps_made, nth)
                pool.tensor_tensor(rstd[a][:, which], rstd[a][:, which], m.minus_half[:, 0:width], ALU.pow
                                   ).then_inc(rstd_made, 1)

            pipeline(pool, [(5, softmax), (0, inverse_deviations), (Y_LAG, last_inverse_deviations), (4, lower),
                            (7, kv_low), (12, update), (5, v_low), (12, add)])

        @block.scalar
        def _(act):
            def load_gate(t):
                reuse(act, branch_gained, t, 4)
                for s in range(SEQ):
                    source = gates[s:s + 1, bass.ds(t.j, 1), t.u, :].rearrange("s j n -> (s j) n")
                    act.dma_start(gate[t.slot(4)][s * L:(s + 1) * L], source.to_broadcast([L, C])
                                  ).then_inc(gate_here[t.slot(4)], 16)

            def store(t):
                if t.u == UNROLL - 1:
                    act.wait_ge(x_updated, t.n + 1)
                    act.dma_start(x_tiles(out)[:, bass.ds(t.j, 1)], m.x_all[:, bass.ds(t.j, 1)]).then_inc(stored, 16)

            def modulate(t):
                a = t.slot(2)
                act.wait_ge(y_turned, t.n + 1)
                reuse(act, silu_made, t, 2)
                for c in range(NC_):
                    for s in range(SEQ):
                        act.activation(z_t[a][:, c, s * L:(s + 1) * L], ps_yt[:, c, s * L:(s + 1) * L], ACT.Identity,
                                       bias=by_seq(m.shift3, c, t, s), scale=by_seq(m.scale3, c, t, s)
                                       ).then_inc(z_made, 1)

            def tanhs(t):
                a = t.slot(2)
                act.wait_ge(z_made, (t.n + 1) * NK)
                act.activation(tanh[a][:], z_t[a][:], ACT.Tanh).then_inc(tanh_made, 1)

            def kv_high(t):
                a = t.slot(2)
                act.wait_ge(kv_masked, t.n + 1)
                reuse(act, y_done, t, 2)
                act.activation(kv_split[a][:, HI], kv[a][:], ACT.Copy).then_inc(kv_hi_made, 1)

            def kq_high(t):
                a = t.slot(2)
                act.wait_ge(kq_turned, t.n + 1)
                reuse(act, y_done, t, 4)
                act.activation(kq_t[t.slot(4)][:, HI], ps_kq[:], ACT.Copy).then_inc(kq_hi_made, 1)

            def q_exponentials(t):
                act.wait_ge(q_lowered, t.n + 1)
                act.activation(kq[t.slot(4)][:, C:2 * C], kq[t.slot(4)][:, C:2 * C], ACT.Exp).then_inc(q_exp_made, 1)

            def k_exponentials(t):
                a = t.slot(2)
                act.wait_ge(k_shift_made, t.n + 1)
                reuse(act, kq_turned, t, 4)
                for c in range(NC_):
                    for s in range(SEQ):
                        i = c * SEQ + s
                        act.activation(kq[t.slot(4)][:, i * L:(i + 1) * L], ps_k[:, c, s * L:(s + 1) * L], ACT.Exp,
                                       bias=k_shift[a][:, c, s:s + 1], accum_out=sums[t.slot(4)][:, i:i + 1]
                                       ).then_inc(k_exp_made, 1)

            def v_high(t):
                a = t.slot(2)
                act.wait_ge(v_biased, t.n + 1)
                reuse(act, kv_done, t, 4)
                act.activation(v_split[t.slot(4)][:, HI], v_full[t.slot(4)][:], ACT.Copy).then_inc(v_hi_made, 1)

            def affine(t):
                a = t.slot(2)
                act.wait_ge(x_turned, t.n + 1)
                reuse(act, k_done, t, 2)
                for c in range(NC_):
                    act.activation(x3_t[a][:, c], ps_xt[:, c], ACT.Identity, bias=m.b_norm3[:, c:c + 1],
                                   scale=m.g_norm3[:, c:c + 1]).then_inc(x3_made, 1)

            pipeline(act, [(2, affine), (9, modulate), (5, kq_high), (3, k_exponentials), (4, q_exponentials), (9, tanhs), (6, kv_high),
                           (4, v_high), (9, load_gate), (13, store)])

        @block.tensor
        def _(pe):
            def project(t):
                a = t.slot(2)
                pe.wait_ge(silu_made, t.n + 1)
                reuse(pe, branch_made, t, 1)
                for c in range(NC_):
                    last = pe.matmul(ps_out[:], silu[a][:, c], m.w_out3[:, c], start=(c == 0), stop=(c == NC_ - 1))
                last.then_inc(out_done, 1)

            def turn_y(t):
                a = t.slot(2)
                pe.wait_ge(y_hat_made, t.n + 1)
                reuse(pe, z_made, t, 1, NK)
                for c in range(NC_):
                    last = pe.transpose(ps_yt[:, c], y_hat[a][:, c * P:(c + 1) * P], m.ident[:])
                last.then_inc(y_turned, 1)

            def q_kv(t):
                a = t.slot(2)
                pe.wait_ge(kv_lo_made, t.n + 1)
                reuse(pe, y_hat_made, t, 1)
                for s in range(SEQ):
                    for c in range(NC_):
                        q_cols = C + c * P + s * L
                        for i, (q, w) in enumerate(SPLITS):
                            last = pe.matmul(ps_y[s * L:(s + 1) * L, c * P:(c + 1) * P],
                                             kq_t[t.slot(4)][:, q, q_cols:q_cols + L], kv_split[a][:, w, c, s],
                                             start=(i == 0), stop=(i == 2))
                last.then_inc(y_done, 1)

            def k_v(t):
                a = t.slot(2)
                pe.wait_ge(kq_lo_made, t.n + 1)
                pe.wait_ge(v_lo_made, t.n + 1)
                reuse(pe, kv_masked, t, 1)
                for s in range(SEQ):
                    own = slice(s * L, (s + 1) * L)
                    for c in range(NC_):
                        chans = slice(c * P, (c + 1) * P)
                        for i, (k, v) in enumerate(SPLITS):
                            last = pe.matmul(ps_kv[:, c, s], kq_t[t.slot(4)][own, k, chans], v_split[t.slot(4)][own, v, chans],
                                             start=(i == 0), stop=(i == 2))
                    if s < SEQ - 1:
                        last.then_inc(kv_first, 1)
                        pe.wait_ge(kv_first, t.n + 1)
                last.then_inc(kv_done, 1)

            def turn_kq(t):
                a = t.slot(2)
                pe.wait_ge(softmax_made, (t.n + 1) * 2)
                reuse(pe, kq_lo_made, t, 1)
                for k in range(2 * NC_):
                    last = pe.transpose(ps_kq[:, k * P:(k + 1) * P], kq[t.slot(4)][:, k * P:(k + 1) * P], m.ident[:])
                last.then_inc(kq_turned, 1)

            def qkv(t):
                a = t.slot(2)
                pe.wait_ge(x3_made, (t.n + 1) * NC_)
                reuse(pe, v_biased, t, 1)
                for c in range(NC_):
                    last = pe.matmul(ps_qv[:], x3_t[a][:, c], m.w_qv3[:, c], start=(c == 0), stop=(c == NC_ - 1))
                last.then_inc(qv_done, 1)
                reuse(pe, k_exp_made, t, 1, NK)
                for to in range(NC_):
                    for c in range(NC_):
                        last = pe.matmul(ps_k[:, to], m.w_k3[:, c, to * P:(to + 1) * P], x3_t[a][:, c],
                                         start=(c == 0), stop=(c == NC_ - 1))
                last.then_inc(k_done, 1)

            def turn_x(t):
                a = t.slot(2)
                pe.wait_ge(x_hat_made, t.n + 1)
                reuse(pe, x3_made, t, 1, NC_)
                for c in range(NC_):
                    last = pe.transpose(ps_xt[:, c], x_hat[a][:, c * P:(c + 1) * P], m.ident[:])
                last.then_inc(x_turned, 1)

            pipeline(pe, [(6, k_v), (11, project), (5, turn_kq), (2, qkv), (Y_LAG, turn_y), (7, q_kv), (1, turn_x)])

        @block.vector
        def _(dve):
            def residual(t):
                a = t.slot(2)
                dve.wait_ge(out_done, t.n + 1)
                reuse(dve, x_updated, t, 2)
                dve.tensor_tensor(branch[a][:], ps_out[:], m.b_out3[:], ALU.add).then_inc(branch_made, 1)

            def silus(t):
                a = t.slot(2)
                dve.wait_ge(tanh_made, t.n + 1)
                reuse(dve, out_done, t, 2)
                dve.scalar_tensor_tensor(silu[a][:], tanh[a][:], 1.0, z_t[a][:], ALU.add, ALU.mult
                                         ).then_inc(silu_made, 1)

            def y_statistics(t):
                a = t.slot(2)
                dve.wait_ge(y_done, t.n + 1)
                reuse(dve, y_hat_made, t, 2)
                dve.bn_stats(y_stats[a][:], ps_y[:]).then_inc(y_stats_made, 1)

            def y_aggregate(t):
                a = t.slot(2)
                if isinstance(t.n, int):
                    dve.wait_ge(y_stats_made, t.n + 1)
                dve.bn_aggr(mean_var[a][:, 1], y_stats[a][:]).then_inc(y_mean_made, 1)

            def y_hats(t):
                a = t.slot(2)
                dve.wait_ge(rstd_made, t.n + Y_LAG + 1)
                reuse(dve, y_turned, t, 2)
                dve.tensor_scalar(y_hat[a][:], ps_y[:], mean_var[a][:, 1, 0:1], rstd[a][:, 1:2], ALU.subtract, ALU.mult
                                  ).then_inc(y_hat_made, 1)

            def mask(t):
                a = t.slot(2)
                dve.wait_ge(kv_done, t.n + 1)
                reuse(dve, kv_lo_made, t, 2)
                dve.tensor_tensor(kv[a][:].rearrange("p c s l -> p (c s) l"), ps_kv[:].rearrange("p c s l -> p (c s) l"),
                                  m.same_head[:, None, :].to_broadcast([P, NC_ * SEQ, P]), ALU.mult
                                  ).then_inc(kv_masked, 1)

            def kq_low(t):
                a = t.slot(2)
                dve.wait_ge(kq_hi_made, t.n + 1)
                dve.tensor_tensor(kq_t[t.slot(4)][:, LO], ps_kq[:], kq_t[t.slot(4)][:, HI], ALU.subtract).then_inc(kq_lo_made, 1)

            def total(t):
                dve.wait_ge(q_exp_made, t.n + 1)
                dve.wait_ge(k_exp_made, (t.n + 1) * NK)
                dve.tensor_reduce(sums[t.slot(4)][:, NK:], q_of(kq[t.slot(4)]), X_AXIS, ALU.add).then_inc(sums_made, 1)
                dve.wait_ge(sums_made, t.n + 1)
                dve.reciprocal(sums[t.slot(4)][:], sums[t.slot(4)][:]).then_inc(sums_inverted, 1)

            def biases(t):
                dve.wait_ge(qv_done, t.n + 1)
                reuse(dve, kq_turned, t, 4)
                dve.tensor_tensor(kq[t.slot(4)][:, C:2 * C], ps_qv[:, 0:C], m.b_qv3[:, 0:C], ALU.add
                                  ).then_inc(q_biased, 1)
                reuse(dve, v_lo_made, t, 4)
                dve.tensor_tensor(v_full[t.slot(4)][:], ps_qv[:, C:2 * C], m.b_qv3[:, C:2 * C], ALU.add
                                  ).then_inc(v_biased, 1)

            def k_maxima(t):
                a = t.slot(2)
                dve.wait_ge(k_done, t.n + 1)
                if not isinstance(t.n, int):
                    dve.wait_ge(y_stats_made, t.n + 4 - Y_LAG)
                dve.tensor_reduce(k_tops[a][:].rearrange("p c s -> p (c s)"),
                                  ps_k[:].rearrange("p c (s l) -> p (c s) l", l=L), X_AXIS, ALU.max
                                  ).then_inc(k_top_found, 1)

            def k_top_bias(t):
                a = t.slot(2)
                dve.wait_ge(k_top_found, t.n + 1)
                dve.tensor_tensor(k_tops[a][:], k_tops[a][:], k_bias, ALU.add).then_inc(k_top_biased, 1)

            def k_shifts(t):
                a = t.slot(2)
                dve.wait_ge(k_top_biased, t.n + 1)
                reuse(dve, k_exp_made, t, 2, NK)
                dve.tensor_tensor(k_shift[a][:], k_bias, k_tops[a][:], ALU.subtract).then_inc(k_shift_made, 1)

            def q_maxima(t):
                a = t.slot(2)
                reuse(dve, q_lowered, t, 2)
                dve.wait_ge(q_biased, t.n + 1)
                dve.tensor_reduce(q_tops[a][:], q_of(kq[t.slot(4)]), X_AXIS, ALU.max).then_inc(tops_made, 1)

            def statistics(t):
                a = t.slot(2)
                if not isinstance(t.n, int) or t.n:
                    dve.wait_ge(stats_made, t.n)
                reuse(dve, x_hat_made, t, 2)
                dve.bn_stats(stats[a][:], t.rows(m.x_all).rearrange("p j n -> p (j n)")).then_inc(stats_made, 1)

            def aggregate(t):
                a = t.slot(2)
                if t.n is TILES - 1:
                    dve.wait_ge(stats_made, TILES)
                    dve.wait_ge(x_hat_made, TILES - 2)
                dve.bn_aggr(mean_var[a][:, 0], stats[a][:]).then_inc(mean_made, 1)

            def hat(t):
                a = t.slot(2)
                dve.wait_ge(rstd_made, t.n + 1)
                reuse(dve, x_turned, t, 2)
                dve.tensor_scalar(x_hat[a][:, None, :], t.rows(m.x_all), mean_var[a][:, 0, 0:1], rstd[a][:, 0:1],
                                  ALU.subtract, ALU.mult).then_inc(x_hat_made, 1)

            k_bias = m.b_k3[:, :, None].to_broadcast([P, NC_, SEQ])
            pipeline(dve, [(3, biases), (Y_LAG, y_statistics), (-1, statistics), (3, k_maxima), (Y_LAG, y_aggregate), (0, aggregate),
                           (3, k_top_bias), (6, mask), (3, k_shifts), (Y_LAG, y_hats), (5, kq_low),
                           (0, hat), (3, q_maxima), (10, silus), (4, total), (11, residual)])



_INS = ["x", "cond_1024", "L0_cond_mat_qkv_w", "L0_cond_q_bias", "L0_cond_v_bias", "L0_cond_scale_mul",
        "L0_cond_proj_w", "L0_cond_proj_b", "L0_cond_ada_w", "L0_cond_ada_b", "L0_cond_fc1_w", "L0_cond_fc1_b",
        "L0_cond_fc2_w", "L0_cond_fc2_b", "L1_cond_norm_g", "L1_cond_norm_b", "L1_cond_Wq", "L1_cond_bq",
        "L1_cond_Wk", "L1_cond_bk", "L1_cond_Wv", "L1_cond_bv", "L1_cond_emb_W", "L1_cond_emb_b",
        "L1_cond_sn_g", "L1_cond_sn_b", "L1_cond_out_W", "L1_cond_out_b"]
_TURNED = {"L0_cond_mat_qkv_w", "L0_cond_proj_w", "L0_cond_ada_w", "L0_cond_fc1_w", "L0_cond_fc2_w"}


def kernel(**inputs):
    import concourse.bacc as bacc
    from concourse.bass_utils import run_bass_kernel_spmd

    nc = bacc.Bacc("TRN2", target_bir_lowering=False, num_devices=1)
    arrays, args = {}, []
    for name in _INS:
        a = np.asarray(inputs[name])
        a = np.ascontiguousarray(a.T if name in _TURNED else a)
        arrays[f"in_{name}"] = a
        args.append(nc.dram_tensor(f"in_{name}", a.shape, mybir.dt.from_np(a.dtype), kind="ExternalInput").ap())
    args.append(nc.dram_tensor("out_0", (B, L, C), F32, kind="ExternalOutput").ap())
    condition_kernel(nc, *args)
    r = run_bass_kernel_spmd(nc, [arrays], core_ids=[0])
    return r.results[0]["out_0"]
```

```python
import math
from contextlib import ExitStack

import numpy as np

import concourse.bass as bass
from concourse import mybir

ALU = mybir.AluOpType
ACT = mybir.ActivationFunctionType
F32 = mybir.dt.float32
BF16 = mybir.dt.bfloat16
X_AXIS = mybir.AxisListType.X

P = 128
B, L, C = 128, 64, 256
H = 16
HD = C // H
D_FF = 1024
NC_ = C // P
SEQ = P // L
TILES = B // SEQ
UNROLL = 4
GROUPS = TILES // UNROLL
HPC = P // HD
G_ = HPC // 2
HI, LO = 0, 1
SPLITS = ((HI, HI), (HI, LO), (LO, HI))
CHUNKED = "(c p) n -> p c n"
X_PARTS = (0, 1, 4, GROUPS)
LOG_100 = math.log(100.0)
LN2 = math.log(2.0)


class Tile:

    def __init__(self, j, u, unroll=UNROLL):
        self.j, self.u = j + u // unroll, u % unroll
        self.n = self.j * unroll + self.u

    def slot(self, slots):
        return self.u % slots

    def since(self, slots, each=1):
        if isinstance(self.n, int) and self.n < slots:
            return None
        return (self.n + 1 - slots) * each

    def rows(self, x):
        return x[:, bass.ds(self.j, 1), self.u]


def pipeline(eng, stages, tiles=TILES, unroll=UNROLL, reach=4):
    deepest = max(lag for lag, _ in stages)
    ahead = min(lag for lag, _ in stages)
    first = -(-(deepest + reach) // unroll)
    last = tiles // unroll + ahead // unroll

    def step(j, u, known):
        for lag, stage in stages:
            if known and not 0 <= unroll * j + u - lag < tiles:
                continue
            stage(Tile(j, u - lag, unroll))

    for s in range(unroll * (ahead // unroll), unroll * first):
        step(0, s, True)
    with eng.Fori(first, last) as j:
        for u in range(unroll):
            step(j, u, False)
    for s in range(unroll * last, tiles + deepest):
        step(0, s, True)


def condition_kernel(nc, x, cond, qkv_w, q_bias, v_bias, scale_mul, proj_w, proj_b, ada_w, ada_b,
                     fc1_w, fc1_b, fc2_w, fc2_b, norm_g, norm_b, wq, bq, wk, bk, wv, bv,
                     emb_w, emb_b, sn_g, sn_b, out_w, out_b, out):
    with ExitStack() as ctx:
        m = Shared(nc, ctx)
        setup(nc, m, x, cond, qkv_w, q_bias, v_bias, scale_mul, proj_w, proj_b, ada_w, ada_b,
              fc1_w, fc1_b, fc2_w, fc2_b, norm_g, norm_b, wq, bq, wk, bk, wv, bv,
              emb_w, emb_b, sn_g, sn_b, out_w, out_b)
        attention_pass(nc, m, x, fc1_w)
        feed_forward_pass(nc, m, fc2_w, wq, wk, wv, out_w)
        linear_pass(nc, m, cond, out)


class Shared:

    def __init__(self, nc, ctx):
        def sb(name, shape, dt):
            return ctx.enter_context(nc.sbuf_tensor(name, shape, dt))

        self.x_all = sb("x_all", [P, GROUPS, UNROLL, C], F32)
        self.ident = sb("ident", [P, P], F32)
        self.minus_half = sb("minus_half", [P, UNROLL], F32)
        self.eps_norm3 = sb("eps_norm3", [P, 1], F32)
        self.eps_ln = sb("eps_ln", [P, 1], F32)
        self.scale1, self.shift1, self.scale2, self.shift2, self.scale3, self.shift3 = (
            sb(n, [P, NC_, B], F32) for n in ("scale1", "shift1", "scale2", "shift2", "scale3", "shift3"))
        self.gammas = nc.dram_tensor("gammas", [B, 2 * C], F32, kind="Internal").ap()
        self.w_qkv = sb("w_qkv", [P, 2, NC_, 3 * C], BF16)
        self.w_proj = sb("w_proj", [P, NC_, C], F32)
        self.w_fc1 = sb("w_fc1", [P, 2, NC_, D_FF], BF16)
        self.w_fc2 = sb("w_fc2", [P, 2, D_FF // P, C], BF16)
        self.w_qvk3 = sb("w_qvk3", [P, 2, NC_, 3 * C], BF16)
        self.w_out3 = sb("w_out3", [P, NC_, C], F32)
        self.fc1_full = sb("fc1_full", [P, NC_, D_FF], F32)
        self.x_here = [ctx.enter_context(nc.semaphore(f"x_here{i}")) for i in range(3)]
        self.ff_here = ctx.enter_context(nc.semaphore("ff_here"))
        self.linear_here = ctx.enter_context(nc.semaphore("linear_here"))
        self.b_qk = sb("b_qk", [P, 2 * C], F32)
        self.b_fc2 = sb("b_fc2", [P, C], F32)
        self.ones = sb("ones", [P, P], BF16)
        self.bias_rows = sb("bias_rows", [P, 5 * C], BF16)
        self.rows_v, self.rows_proj, self.rows_qv3, self.rows_out3 = (
            self.bias_rows[:, a * C:b * C] for a, b in ((0, 1), (1, 2), (2, 4), (4, 5)))
        self.b_fc1 = sb("b_fc1", [P, D_FF // P], F32)
        self.b_k3 = sb("b_k3", [P, NC_], F32)
        self.g_norm3 = sb("g_norm3", [P, NC_], F32)
        self.b_norm3 = sb("b_norm3", [P, NC_], F32)
        self.norm_weight = sb("norm_weight", [P, 2 * H], F32)
        self.log_256 = sb("log_256", [P, 1], F32)
        self.minus_shift = sb("minus_shift", [P, 1], F32)
        self.same_head = sb("same_head", [P, P], F32)


def setup(nc, m, x, cond, qkv_w, q_bias, v_bias, scale_mul, proj_w, proj_b, ada_w, ada_b,
          fc1_w, fc1_b, fc2_w, fc2_b, norm_g, norm_b, wq, bq, wk, bk, wv, bv,
          emb_w, emb_b, sn_g, sn_b, out_w, out_b):
    with ExitStack() as ctx:
        def sb(name, shape, dt=F32):
            return ctx.enter_context(nc.sbuf_tensor(name, shape, dt))

        def sem(name):
            return ctx.enter_context(nc.semaphore(name))

        cond_sb = sb("cond_sb", [P, C])
        cond_act = sb("cond_act", [P, C])
        cond_t = sb("cond_t", [P, NC_, B])
        w_ada = sb("w_ada", [P, NC_, 6 * C])
        w_emb = sb("w_emb", [P, NC_, 2 * C])
        b_ada_row = sb("b_ada_row", [P, 2 * C])
        b_ada = sb("b_ada", [P, 6 * NC_])
        b_emb = sb("b_emb", [P, 2 * NC_])
        g_sn = sb("g_sn", [P, NC_])
        b_sn = sb("b_sn", [P, NC_])
        gamma_rows = sb("gamma_rows", [P, 2 * C])
        head_scale = sb("head_scale", [P, H])
        head_exp = sb("head_exp", [P, H])
        top = sb("top", [P, 1])
        scale_plus = sb("scale_plus", [P, NC_, B])
        b_sn_half = sb("b_sn_half", [P, NC_])
        qkv_full = sb("qkv_full", [P, NC_, 3 * C])
        bias_full = sb("bias_full", [P, 5 * C])
        bias_rest = sb("bias_rest", [P, 5 * C])
        bias_high = sb("bias_high", [P, 5 * C], BF16)
        bias_mid = sb("bias_mid", [P, 5 * C], BF16)
        band = sb("band", [P, P])
        ps = [ctx.enter_context(nc.psum_tensor(f"set_ps{i}", [P, 512], F32)) for i in range(6)]

        cond_here = sem("cond_here")
        heads_here = sem("heads_here")
        ada_here = sem("ada_here")
        emb_here = sem("emb_here")
        attention_here = sem("attention_here")
        biases_here = sem("biases_here")
        rows_cleared = sem("rows_cleared")
        rows_made = sem("rows_made")
        qkv_here = sem("qkv_here")
        qkv_hi_made = sem("qkv_hi_made")
        biases_split = sem("biases_split")
        silu_done = sem("silu_done")
        exp_done = sem("exp_done")
        b_halved = sem("b_halved")
        consts_made = sem("consts_made")
        heads_made = sem("heads_made")
        transposed = sem("transposed")
        cond_t_made = sem("cond_t_made")
        products = sem("products")
        modulations = sem("modulations")
        gammas_made = sem("gammas_made")
        gammas_stored = sem("gammas_stored")
        block = ctx.enter_context(nc.Block())

        def row(a):
            return a[None, :].to_broadcast([P, a.shape[0]])

        def column(a):
            return a.rearrange("(k p) -> p k", p=P)

        def load(eng, loads, signal):
            for to, source in loads:
                eng.dma_start(to, source, allow_slow_non_contiguous=True).then_inc(signal, 16)

        @block.sync
        def _(sp):
            load(sp, [(cond_sb[:], cond)], cond_here)
            load(sp, [(w_ada[:], ada_w.rearrange(CHUNKED, p=P))], ada_here)
            load(sp, [(m.x_all[:, X_PARTS[0]:X_PARTS[1]], x_tiles(x)[:, X_PARTS[0]:X_PARTS[1]])], m.x_here[0])
            load(sp, [(qkv_full[:], qkv_w.rearrange(CHUNKED, p=P))], qkv_here)
            load(sp, [(w_emb[:], emb_w.rearrange(CHUNKED, p=P))], emb_here)
            load(sp, [(m.w_proj[:], proj_w.rearrange(CHUNKED, p=P))], attention_here)
            sp.wait_ge(gammas_made, 1)
            sp.dma_start(m.gammas, gamma_rows[:]).then_inc(gammas_stored, 16)
            sp.wait_ge(gammas_stored, 16)
            part = slice(X_PARTS[1], X_PARTS[2])
            load(sp, [(m.x_all[:, part], x_tiles(x)[:, part])], m.x_here[1])
            sp.wait_ge(attention_here, 16 * 2)

        @block.scalar
        def _(act):
            load(act, [(head_scale[:], scale_mul.rearrange("a h b c -> (a b c) h").to_broadcast([P, H]))], heads_here)
            load(act, [(bias_full[:, i * C:(i + 1) * C], row(b)) for i, b in enumerate((v_bias, proj_b, bq, bv, out_b))],
                 biases_here)
            load(act, [(b_ada_row[:], row(ada_b[0:2 * C])), (b_ada[:], column(ada_b))], ada_here)
            load(act, [(b_emb[:], column(emb_b)), (g_sn[:], column(sn_g)), (b_sn[:], column(sn_b))], emb_here)
            load(act, [(m.b_qk[:, 0:C], row(q_bias))], attention_here)
            act.wait_ge(cond_here, 16)
            act.activation(cond_act[:], cond_sb[:], ACT.Silu).then_inc(silu_done, 1)
            load(act, [(m.b_fc1[:], column(fc1_b)), (m.b_fc2[:], row(fc2_b))], m.ff_here)
            load(act, [(m.b_k3[:], column(bk)), (m.g_norm3[:], column(norm_g)), (m.b_norm3[:], column(norm_b))],
                 m.linear_here)
            act.wait_ge(heads_made, 1)
            act.activation(head_exp[:], head_scale[:], ACT.Exp).then_inc(exp_done, 1)
            act.wait_ge(consts_made, 8)
            act.activation(m.norm_weight[:, 0:H], head_scale[:], ACT.Exp, scale=-2.0)
            act.wait_ge(qkv_here, 16)
            act.activation(m.w_qkv[:, HI], qkv_full[:], ACT.Copy).then_inc(qkv_hi_made, 1)

        @block.gpsimd
        def _(pool):
            pool.memset(m.ident[:], 0.0).then_inc(consts_made, 1)
            pool.memset(m.minus_half[:], -0.5).then_inc(consts_made, 1)
            pool.memset(m.b_qk[:, C:2 * C], 0.0).then_inc(consts_made, 1)
            pool.memset(m.log_256[:], 8 * LN2).then_inc(consts_made, 1)
            pool.memset(m.norm_weight[:], 1.0).then_inc(consts_made, 1)
            pool.memset(m.eps_norm3[:], 1e-5).then_inc(consts_made, 1)
            pool.memset(m.eps_ln[:], 1e-6).then_inc(consts_made, 1)
            pool.memset(m.same_head[:], 1.0).then_inc(consts_made, 1)
            pool.wait_ge(consts_made, 8)
            pool.affine_select(out=m.ident[:], in_=m.ident[:], compare_op=ALU.not_equal, fill=1.0, base=0,
                               pattern=[[-1, P]], channel_multiplier=1).then_inc(consts_made, 1)
            pool.affine_select(out=band[:].rearrange("p (h e) -> p h e", e=HD),
                               in_=m.same_head[:].rearrange("p (h e) -> p h e", e=HD), compare_op=ALU.is_ge, fill=0.0,
                               base=0, pattern=[[-HD, HPC], [0, HD]], channel_multiplier=1).then_inc(consts_made, 1)
            pool.wait_ge(consts_made, 10)
            pool.affine_select(out=m.same_head[:].rearrange("p (h e) -> p h e", e=HD),
                               in_=band[:].rearrange("p (h e) -> p h e", e=HD), compare_op=ALU.is_ge, fill=0.0,
                               base=HD - 1, pattern=[[HD, HPC], [0, HD]], channel_multiplier=-1).then_inc(consts_made, 1)
            pool.wait_ge(consts_made, 11)
            pool.memset(m.ones[:], 1.0).then_inc(rows_cleared, 1)
            pool.memset(m.bias_rows[:], 0.0).then_inc(rows_cleared, 1)
            pool.wait_ge(rows_cleared, 2)
            pool.wait_ge(qkv_hi_made, 1)
            pool.tensor_tensor(m.w_qkv[:, LO], qkv_full[:], m.w_qkv[:, HI], ALU.subtract)
            pool.wait_ge(biases_split, 1)
            pool.tensor_copy(m.bias_rows[0:1], bias_high[0:1]).then_inc(rows_made, 1)
            pool.wait_ge(biases_split, 3)
            pool.wait_ge(rows_made, 1)
            pool.tensor_copy(m.bias_rows[32:33], bias_mid[32:33]).then_inc(rows_made, 1)
            pool.wait_ge(rows_made, 2)

        @block.tensor
        def _(pe):
            pe.wait_ge(consts_made, 9)
            pe.wait_ge(silu_done, 1)
            for c in range(NC_):
                last = pe.transpose(ps[0][:, c * P:(c + 1) * P], cond_act[:, c * P:(c + 1) * P], m.ident[:])
            last.then_inc(transposed, 1)
            pe.wait_ge(cond_t_made, 1)
            pe.wait_ge(ada_here, 16 * 3)
            for c in range(NC_):
                last = pe.matmul(ps[1][:, :], cond_t[:, c, :], w_ada[:, c, 0:2 * C], start=(c == 0), stop=(c == NC_ - 1))
            last.then_inc(products, 1)
            for k in range(8):
                for c in range(NC_):
                    last = pe.matmul(ps[2 + k // 4][:, (k % 4) * B:(k % 4 + 1) * B],
                                     w_ada[:, c, 2 * C + k * P:2 * C + (k + 1) * P], cond_t[:, c, :],
                                     start=(c == 0), stop=(c == NC_ - 1))
            last.then_inc(products, 1)
            pe.wait_ge(emb_here, 16 * 4)
            for k in range(4):
                for c in range(NC_):
                    last = pe.matmul(ps[4][:, k * B:(k + 1) * B], w_emb[:, c, k * P:(k + 1) * P], cond_t[:, c, :],
                                     start=(c == 0), stop=(c == NC_ - 1))
            last.then_inc(products, 1)

        @block.vector
        def _(dve):
            dve.wait_ge(heads_here, 16)
            dve.tensor_scalar(head_scale[:], head_scale[:], LOG_100, None, ALU.min).then_inc(heads_made, 1)
            dve.wait_ge(heads_made, 1)
            dve.wait_ge(exp_done, 1)
            dve.tensor_reduce(top[:], head_exp[:], X_AXIS, ALU.max).then_inc(heads_made, 1)
            dve.wait_ge(heads_made, 2)
            dve.tensor_scalar(top[:], top[:], -80.0, 0.0, ALU.add, ALU.max).then_inc(heads_made, 1)
            dve.wait_ge(heads_made, 3)
            dve.tensor_scalar(m.minus_shift[:], top[:], -1.0, None, ALU.mult)
            dve.wait_ge(transposed, 1)
            dve.tensor_copy(cond_t[:], ps[0][:, 0:NC_ * B].rearrange("p (c b) -> p c b", c=NC_)).then_inc(cond_t_made, 1)
            dve.wait_ge(biases_here, 16 * 5)
            dve.tensor_copy(bias_high[:], bias_full[:]).then_inc(biases_split, 1)
            dve.wait_ge(biases_split, 1)
            dve.tensor_tensor(bias_rest[:], bias_full[:], bias_high[:], ALU.subtract).then_inc(biases_split, 1)
            dve.wait_ge(biases_split, 2)
            dve.tensor_copy(bias_mid[:], bias_rest[:]).then_inc(biases_split, 1)
            dve.wait_ge(biases_split, 3)
            dve.wait_ge(rows_cleared, 2)
            dve.tensor_tensor(m.bias_rows[64:65], bias_rest[64:65], bias_mid[64:65], ALU.subtract)
            dve.wait_ge(ada_here, 16 * 3)
            dve.wait_ge(products, 1)
            dve.tensor_tensor(gamma_rows[:], ps[1][:], b_ada_row[:], ALU.add).then_inc(gammas_made, 1)
            dve.wait_ge(products, 2)
            for k, (to, one) in enumerate(((m.scale1, 1.0), (m.scale2, 1.0), (m.shift1, 0.0), (m.shift2, 0.0))):
                for c in range(NC_):
                    i = k * NC_ + c
                    dve.tensor_scalar(to[:, c, :], ps[2 + i // 4][:, (i % 4) * B:(i % 4 + 1) * B],
                                      b_ada[:, 2 * NC_ + i:2 * NC_ + i + 1], one, ALU.add, ALU.add)
            dve.wait_ge(emb_here, 16 * 4)
            dve.tensor_scalar(b_sn_half[:], b_sn[:], 0.5, None, ALU.mult).then_inc(b_halved, 1)
            dve.wait_ge(products, 3)
            for c in range(NC_):
                dve.tensor_scalar(scale_plus[:, c, :], ps[4][:, c * B:(c + 1) * B], b_emb[:, c:c + 1], 1.0,
                                  ALU.add, ALU.add).then_inc(modulations, 1)
                dve.tensor_scalar(m.shift3[:, c, :], ps[4][:, (NC_ + c) * B:(NC_ + c + 1) * B],
                                  b_emb[:, NC_ + c:NC_ + c + 1], 0.5, ALU.add, ALU.mult).then_inc(modulations, 1)
            dve.wait_ge(modulations, 4)
            dve.wait_ge(b_halved, 1)
            for c in range(NC_):
                dve.tensor_scalar(m.scale3[:, c, :], scale_plus[:, c, :], g_sn[:, c:c + 1], 0.5, ALU.mult, ALU.mult)
                dve.scalar_tensor_tensor(m.shift3[:, c, :], scale_plus[:, c, :], b_sn_half[:, c:c + 1], m.shift3[:, c, :],
                                         ALU.mult, ALU.add)


def x_tiles(x):
    return x.rearrange("(j u s) l c -> (s l) j u c", s=SEQ, u=UNROLL)


def reuse(eng, sem, tile, slots, each=1):
    count = tile.since(slots, each)
    if count is not None:
        eng.wait_ge(sem, count)


def bank_free(eng, sem, tile, offset, each=1):
    n = tile.n + offset
    if isinstance(n, int):
        if n < 0:
            return
        n = min(n, TILES - 1)
    eng.wait_ge(sem, (n + 1) * each)


def attention_pass(nc, m, x, fc1_w):
    PAIRS = H // 2
    VW = HD + 1
    FIRST_OF_PART = [UNROLL * g for g in X_PARTS[:3]]
    with ExitStack() as ctx:
        def sb(name, shape, dt=F32, slots=2):
            return [ctx.enter_context(nc.sbuf_tensor(f"{name}{i}", shape, dt)) for i in range(slots)]

        def sem(name):
            return ctx.enter_context(nc.semaphore(name))

        stats = sb("stats", [P, 6])
        mean_var = sb("mean_var", [P, 2], F32, 4)
        rstd = sb("rstd", [P, 1], F32, 4)
        x_hat = sb("x_hat", [P, C])
        x1_t = sb("x1_t", [P, NC_, P], F32, 1)[0]
        x1_split = sb("x1_split", [P, 2, NC_, P], BF16)
        qk = sb("qk", [P, 2 * C])
        v_split = sb("v_split", [P, 2, PAIRS, 2, HD], BF16, 4)
        v_pairs = sb("v_pairs", [P, SEQ, 2, 2, PAIRS, VW], BF16, 4)
        squares = sb("squares", [P, 2 * C], F32, 1)[0]
        norms = sb("norms", [P, 2 * H])
        log_norms = sb("log_norms", [P, 2 * H])
        factors = sb("factors", [P, 2 * H])
        qk_hat = sb("qk_hat", [P, 2 * C])
        qk_t = sb("qk_t", [P, 2, 4, 2, NC_, P], BF16, 1)[0]
        k_pairs = sb("k_pairs", [P, 4, 2, NC_, SEQ, G_, 2, L], BF16, 1)[0]
        e_full = sb("e_full", [P, SEQ, PAIRS, L], F32, 1)[0]
        e_split = sb("e_split", [P, 2, SEQ, PAIRS, L], BF16)
        inv_sum = sb("inv_sum", [P, SEQ, PAIRS // 2, 2])
        o_full = sb("o_full", [P, C], F32, 1)[0]
        o_t = sb("o_t", [P, NC_, P])
        gain = sb("gain", [P, 4, C], F32, 1)[0]
        branch = sb("branch", [P, C])

        ps_x = ctx.enter_context(nc.psum_tensor("ps_x", [P, 512], F32))
        ps_qk = ctx.enter_context(nc.psum_tensor("ps_qk", [P, 512], F32))
        ps_v = ctx.enter_context(nc.psum_tensor("ps_v", [P, 512], F32))
        ps_qkt = ctx.enter_context(nc.psum_tensor("ps_qkt", [P, 512], F32))
        ps_s = ctx.enter_context(nc.psum_tensor("ps_s", [P, SEQ, PAIRS, L], F32))
        ps_o = ctx.enter_context(nc.psum_tensor("ps_o", [P, SEQ, 512], F32))

        o_blocks = ps_o[:, :, 0:PAIRS // 2 * 4 * VW].rearrange(
            "p s (k g r e) -> p s k g r e", k=PAIRS // 2, g=2, r=2)
        ps_xt, ps_ot = ps_x[:, 0:C], ps_x[:, C:2 * C]
        ps_vv, ps_y = ps_v[:, 0:C], ps_v[:, C:2 * C]

        gain_here = [sem(f"gain_here{i}") for i in range(2)]
        k_pairs_here = [sem(f"k_pairs_here{i}") for i in range(2)]
        fc1_hi_made = sem("fc1_hi_made")
        cleared = sem("cleared")
        k_cleared = sem("k_cleared")
        ones_set = sem("ones_set")
        stats_made = sem("stats_made")
        mean_made = sem("mean_made")
        var_eps_made = sem("var_eps_made")
        rstd_made = sem("rstd_made")
        x_hat_made = sem("x_hat_made")
        x_hat_t = sem("x_hat_t")
        x1_made = sem("x1_made")
        x1_second = sem("x1_second")
        x1_hi_made = sem("x1_hi_made")
        x1_lo_made = sem("x1_lo_made")
        qk_done = sem("qk_done")
        qkv_done = sem("qkv_done")
        qk_biased = sem("qk_biased")
        v_hi_made = sem("v_hi_made")
        v_lo_made = sem("v_lo_made")
        v_placed = sem("v_placed")
        squared = sem("squared")
        norms_made = sem("norms_made")
        norms_weighted = sem("norms_weighted")
        logs_made = sem("logs_made")
        factors_made = sem("factors_made")
        qk_hat_made = sem("qk_hat_made")
        qk_turned = sem("qk_turned")
        qk_hi_made = sem("qk_hi_made")
        qk_lo_made = sem("qk_lo_made")
        scores_done = sem("scores_done")
        exp_made = sem("exp_made")
        e_lo_made = sem("e_lo_made")
        pv_done = sem("pv_done")
        sums_inverted = sem("sums_inverted")
        o_made = sem("o_made")
        o_turned = sem("o_turned")
        o_t_made = sem("o_t_made")
        proj_done = sem("proj_done")
        branch_made = sem("branch_made")
        x_updated = sem("x_updated")
        block = ctx.enter_context(nc.Block())
        gamma1 = m.gammas.rearrange("(j u s) n -> s j u n", s=SEQ, u=UNROLL)

        @block.sync
        def _(sp):
            def load_gain(t):
                if t.u % 2 == 0:
                    return
                if isinstance(t.n, int):
                    reuse(sp, branch_made, t, 4)
                for s in range(SEQ):
                    source = gamma1[s:s + 1, bass.ds(t.j, 1), t.u - 1:t.u + 1, 0:C]
                    sp.dma_start(gain[s * L:(s + 1) * L, t.u - 1:t.u + 1, :],
                                 source.rearrange("s j u n -> (s j) u n").to_broadcast([L, 2, C])
                                 ).then_inc(gain_here[t.u // 2], 16)

            def load_later(t):
                if isinstance(t.n, int) and t.n < GROUPS - X_PARTS[2]:
                    group = slice(X_PARTS[2] + t.n, X_PARTS[2] + t.n + 1)
                    sp.dma_start(m.x_all[:, group], x_tiles(x)[:, group]).then_inc(m.x_here[2], 16)
                if isinstance(t.n, int) and t.n == GROUPS - X_PARTS[2] - 1:
                    sp.dma_start(m.fc1_full[:], fc1_w.rearrange(CHUNKED, p=P)).then_inc(m.ff_here, 16)

            def place_k(t):
                if t.u % 2 == 0:
                    return
                if isinstance(t.n, int) and t.n == 1:
                    sp.wait_ge(k_cleared, 4)
                sp.wait_ge(qk_lo_made, t.n + 1)
                two = slice(t.u - 1, t.u + 1)
                for g in range(G_):
                    for r in range(2):
                        rows = slice((2 * g + r) * HD, (2 * g + r + 1) * HD)
                        sp.dma_start(
                            k_pairs[rows, two, :, :, :, g, r, :].rearrange("p t a c s k -> p (t a c s) k"),
                            qk_t[rows, 1, two].rearrange("p t a c (s k) -> p (t a c s) k", s=SEQ)
                        ).then_inc(k_pairs_here[t.u // 2], 16)

            pipeline(sp, [(9, load_gain), (5, place_k), (0, load_later)])
            sp.wait_ge(x_updated, TILES)
            sp.wait_ge(m.ff_here, 16 * 3)

        @block.gpsimd
        def _(pool):
            def clear_v(t):
                if isinstance(t.n, int) and t.n < 4:
                    pool.memset(v_pairs[t.n][:], 0.0).then_inc(cleared, 1)
                    pool.wait_ge(cleared, t.n + 1)
                    for r in range(2):
                        pool.memset(v_pairs[t.n][r * L:(r + 1) * L, :, HI, r, :, HD:VW], 1.0).then_inc(ones_set, 1)
                    pool.wait_ge(ones_set, (t.n + 1) * 2)

            def rstd_of(t):
                a = t.slot(2)
                reuse(pool, x_hat_made, t, 4)
                pool.wait_ge(mean_made, t.n + 1)
                pool.tensor_tensor(rstd[t.slot(4)][:], mean_var[t.slot(4)][:, 1:2], m.eps_ln[:], ALU.add).then_inc(var_eps_made, 1)
                pool.wait_ge(var_eps_made, t.n + 1)
                pool.tensor_tensor(rstd[t.slot(4)][:], rstd[t.slot(4)][:], m.minus_half[:, 0:1], ALU.pow).then_inc(rstd_made, 1)

            def normalise(t):
                a = t.slot(2)
                pool.wait_ge(factors_made, t.n + 1)
                reuse(pool, qk_turned, t, 2)
                pool.tensor_tensor(heads(qk_hat[a][:]), heads(qk[a][:]), over_channels(factors[a][:]), ALU.mult
                                   ).then_inc(qk_hat_made, 1)

            def x1_low(t):
                a = t.slot(2)
                pool.wait_ge(x1_hi_made, t.n + 1)
                reuse(pool, qkv_done, t, 2)
                pool.tensor_tensor(x1_split[a][:, LO], x1_t[:], x1_split[a][:, HI], ALU.subtract).then_inc(x1_lo_made, 1)

            def add(t):
                a = t.slot(2)
                pool.wait_ge(branch_made, t.n + 1)
                pool.tensor_tensor(t.rows(m.x_all), t.rows(m.x_all), branch[a][:, None, :], ALU.add
                                   ).then_inc(x_updated, 1)

            def split_fc1(t):
                if isinstance(t.n, int) and t.n == TILES - 1:
                    pool.wait_ge(fc1_hi_made, 1)
                    pool.tensor_tensor(m.w_fc1[:, LO], m.fc1_full[:], m.w_fc1[:, HI], ALU.subtract)

            def e_lo(t):
                a = t.slot(2)
                pool.wait_ge(exp_made, t.n + 1)
                reuse(pool, pv_done, t, 2)
                pool.tensor_tensor(flat(e_split[a][:, LO]), flat(e_full[:]), flat(e_split[a][:, HI]), ALU.subtract
                                   ).then_inc(e_lo_made, 1)

            pipeline(pool, [(5, normalise), (1, rstd_of), (12, add), (2, x1_low), (8, e_lo), (8, split_fc1),
                            (1, clear_v)])

        @block.scalar
        def _(act):
            def modulate_second(t):
                a = t.slot(2)
                act.wait_ge(x1_made, t.n + 1)
                reuse(act, x1_lo_made, t, 1)
                for s in range(SEQ):
                    act.activation(x1_t[:, 1, s * L:(s + 1) * L], ps_xt[:, P + s * L:P + (s + 1) * L], ACT.Identity,
                                   bias=by_seq(m.shift1, 1, t, s), scale=by_seq(m.scale1, 1, t, s)
                                   ).then_inc(x1_second, 1)

            def x1_high(t):
                a = t.slot(2)
                act.wait_ge(x1_second, (t.n + 1) * SEQ)
                reuse(act, qkv_done, t, 2)
                act.activation(x1_split[a][:, HI], x1_t[:], ACT.Copy).then_inc(x1_hi_made, 1)

            def square(t):
                a = t.slot(2)
                act.wait_ge(qk_biased, t.n + 1)
                reuse(act, norms_made, t, 1)
                act.activation(squares[:], qk[a][:], ACT.Square).then_inc(squared, 1)

            def v_hi(t):
                a = t.slot(2)
                act.wait_ge(qkv_done, t.n + 1)
                reuse(act, v_placed, t, 4)
                act.activation(v_split[t.slot(4)][:, HI].rearrange("p k r e -> p (k r e)"), ps_vv, ACT.Copy
                               ).then_inc(v_hi_made, 1)

            def logs(t):
                a = t.slot(2)
                act.wait_ge(norms_weighted, t.n + 1)
                reuse(act, factors_made, t, 2)
                act.activation(log_norms[a][:], norms[a][:], ACT.Ln, scale=65536.0).then_inc(logs_made, 1)

            def factor(t):
                a = t.slot(2)
                act.wait_ge(logs_made, t.n + 1)
                reuse(act, qk_hat_made, t, 2)
                act.activation(factors[a][:], log_norms[a][:], ACT.Exp, bias=m.log_256[:], scale=-0.5).then_inc(factors_made, 1)

            def qk_hi(t):
                a = t.slot(2)
                act.wait_ge(qk_turned, t.n + 1)
                reuse(act, scores_done, t, 4)
                act.activation(qk_t[:, :, t.slot(4), HI].rearrange("p w c k -> p w (c k)"),
                               ps_qkt[:, :].rearrange("p (w k) -> p w k", w=2), ACT.Copy).then_inc(qk_hi_made, 1)

            def split_fc1(t):
                if isinstance(t.n, int) and t.n == TILES - 1:
                    act.wait_ge(m.ff_here, 16 * 3)
                    act.activation(m.w_fc1[:, HI], m.fc1_full[:], ACT.Copy).then_inc(fc1_hi_made, 1)

            def high_exponentials(t):
                a = t.slot(2)
                act.wait_ge(scores_done, t.n + 1)
                reuse(act, pv_done, t, 2)
                act.activation(flat(e_split[a][:, HI]), flat(ps_s[:]), ACT.Exp, bias=m.minus_shift[:])

            def full_exponentials(t):
                a = t.slot(2)
                reuse(act, e_lo_made, t, 1)
                act.activation(flat(e_full[:]), flat(ps_s[:]), ACT.Exp, bias=m.minus_shift[:]).then_inc(exp_made, 1)

            def o_copy(t):
                a = t.slot(2)
                act.wait_ge(o_turned, t.n + 1)
                reuse(act, proj_done, t, 2)
                act.activation(o_t[a][:].rearrange("p c k -> p (c k)"), ps_ot, ACT.Copy).then_inc(o_t_made, 1)

            act.preload_act_table_set("natural_log_exp_and_others")
            pipeline(act, [(4, v_hi), (4, square), (2, modulate_second), (8, high_exponentials), (5, qk_hi),
                           (2, x1_high), (8, full_exponentials), (4, logs), (10, o_copy), (5, split_fc1),
                           (4, factor)])

        @block.tensor
        def _(pe):
            def project(t):
                a = t.slot(2)
                pe.wait_ge(o_t_made, t.n + 1)
                reuse(pe, branch_made, t, 1)
                bank_free(pe, v_lo_made, t, 7)
                pe.matmul(ps_y, m.ones[:], m.rows_proj, start=True, stop=False)
                for c in range(NC_):
                    last = pe.matmul(ps_y, o_t[a][:, c, :], m.w_proj[:, c, :], start=False, stop=(c == NC_ - 1))
                last.then_inc(proj_done, 1)

            def turn_o(t):
                a = t.slot(2)
                pe.wait_ge(o_made, t.n + 1)
                reuse(pe, o_t_made, t, 1)
                bank_free(pe, x1_second, t, 8, SEQ)
                for c in range(NC_):
                    last = pe.transpose(ps_ot[:, c * P:(c + 1) * P], o_full[:, c * P:(c + 1) * P], m.ident[:])
                last.then_inc(o_turned, 1)

            def probs_v(t):
                a = t.slot(2)
                pe.wait_ge(e_lo_made, t.n + 1)
                pe.wait_ge(v_placed, t.n + 1)
                if isinstance(t.n, int) and t.n < 4:
                    pe.wait_ge(ones_set, 8)
                reuse(pe, o_made, t, 1)
                for s in range(SEQ):
                    for k in range(PAIRS // 2):
                        for i, (e, v) in enumerate(SPLITS):
                            last = pe.matmul(
                                o_blocks[:, s, k].rearrange("p g r e -> p (g r e)"),
                                e_split[a][:, e, s, 2 * k:2 * k + 2].rearrange("p k q -> p (k q)"),
                                v_pairs[t.slot(4)][:, s, v, :, 2 * k:2 * k + 2].rearrange("p r k e -> p k r e"),
                                start=(i == 0), stop=(i == 2))
                last.then_inc(pv_done, 1)

            def scores(t):
                a = t.slot(2)
                pe.wait_ge(k_pairs_here[t.u // 2], (t.j + 1) * 16 * HPC)
                reuse(pe, exp_made, t, 1)
                for s in range(SEQ):
                    for c in range(NC_):
                        for g in range(G_):
                            for i, (k, q) in enumerate(SPLITS):
                                last = pe.matmul(ps_s[:, s, G_ * c + g],
                                                 k_pairs[:, t.slot(4), k, c, s, g].rearrange("p r k -> p (r k)"),
                                                 qk_t[:, 0, t.slot(4), q, c, s * L:(s + 1) * L], start=(i == 0), stop=(i == 2))
                last.then_inc(scores_done, 1)

            def turn_qk(t):
                a = t.slot(2)
                pe.wait_ge(qk_hat_made, t.n + 1)
                reuse(pe, qk_lo_made, t, 1)
                for k in range(2 * NC_):
                    last = pe.transpose(ps_qkt[:, k * P:(k + 1) * P], qk_hat[a][:, k * P:(k + 1) * P], m.ident[:])
                last.then_inc(qk_turned, 1)

            def qkv(t):
                a = t.slot(2)
                pe.wait_ge(x1_lo_made, t.n + 1)
                reuse(pe, qk_biased, t, 1)
                for i, (xs, ws) in enumerate(SPLITS):
                    for c in range(NC_):
                        last = pe.matmul(ps_qk[:, :], x1_split[a][:, xs, c, :], m.w_qkv[:, ws, c, 0:2 * C],
                                         start=(i == 0 and c == 0), stop=(i == 2 and c == NC_ - 1))
                last.then_inc(qk_done, 1)
                reuse(pe, v_lo_made, t, 1)
                bank_free(pe, branch_made, t, -8)
                pe.matmul(ps_vv, m.ones[:], m.rows_v, start=True, stop=False)
                for i, (xs, ws) in enumerate(SPLITS):
                    for c in range(NC_):
                        last = pe.matmul(ps_vv, x1_split[a][:, xs, c, :], m.w_qkv[:, ws, c, 2 * C:3 * C],
                                         start=False, stop=(i == 2 and c == NC_ - 1))
                last.then_inc(qkv_done, 1)

            def turn_x(t):
                a = t.slot(2)
                pe.wait_ge(x_hat_made, t.n + 1)
                reuse(pe, x1_second, t, 1, SEQ)
                bank_free(pe, o_t_made, t, -9)
                for c in range(NC_):
                    last = pe.transpose(ps_xt[:, c * P:(c + 1) * P], x_hat[a][:, c * P:(c + 1) * P], m.ident[:])
                last.then_inc(x_hat_t, 1)

            pipeline(pe, [(8, scores), (11, project), (5, turn_qk), (9, probs_v), (10, turn_o), (3, qkv), (1, turn_x)])

        @block.vector
        def _(dve):
            def reduce_norms(t):
                a = t.slot(2)
                dve.wait_ge(squared, t.n + 1)
                reuse(dve, logs_made, t, 2)
                dve.tensor_reduce(norms[a][:], heads(squares[:]), X_AXIS, ALU.add).then_inc(norms_made, 1)
                dve.wait_ge(norms_made, t.n + 1)
                dve.scalar_tensor_tensor(norms[a][:], norms[a][:], 1e-24, m.norm_weight[:], ALU.max, ALU.mult
                                         ).then_inc(norms_weighted, 1)

            def modulate(t):
                a = t.slot(2)
                dve.wait_ge(x_hat_t, t.n + 1)
                reuse(dve, x1_lo_made, t, 1)
                for s in range(SEQ):
                    at = slice(s * L, (s + 1) * L)
                    last = dve.tensor_scalar(x1_t[:, 0, at], ps_xt[:, at], by_seq(m.scale1, 0, t, s),
                                             by_seq(m.shift1, 0, t, s), ALU.mult, ALU.add)
                last.then_inc(x1_made, 1)

            def residual(t):
                a = t.slot(2)
                dve.wait_ge(proj_done, t.n + 1)
                reuse(dve, x_updated, t, 2)
                dve.wait_ge(gain_here[t.u // 2], (t.j + 1) * 16 * SEQ)
                dve.tensor_tensor(branch[a][:], ps_y, gain[:, t.slot(4)], ALU.mult).then_inc(branch_made, 1)

            def v_low(t):
                a = t.slot(2)
                dve.wait_ge(v_hi_made, t.n + 1)
                reuse(dve, v_placed, t, 4)
                dve.tensor_tensor(v_split[t.slot(4)][:, LO].rearrange("p k r e -> p (k r e)"), ps_vv,
                                  v_split[t.slot(4)][:, HI].rearrange("p k r e -> p (k r e)"), ALU.subtract).then_inc(v_lo_made, 1)

            def place_v(t):
                a = t.slot(2)
                dve.wait_ge(v_lo_made, t.n + 1)
                reuse(dve, pv_done, t, 4)
                if isinstance(t.n, int) and t.n < 4:
                    dve.wait_ge(cleared, 4)
                for s in range(SEQ):
                    for r in range(2):
                        last = dve.tensor_copy(v_pairs[t.slot(4)][r * L:(r + 1) * L, s, :, r, :, 0:HD],
                                               v_split[t.slot(4)][s * L:(s + 1) * L, :, :, r, :])
                last.then_inc(v_placed, 1)

            def outputs(t):
                a = t.slot(2)
                dve.wait_ge(pv_done, t.n + 1)
                dve.reciprocal(inv_sum[a][:], o_blocks[:, :, :, 0, :, HD]).then_inc(sums_inverted, 1)
                dve.wait_ge(sums_inverted, t.n + 1)
                reuse(dve, o_turned, t, 1)
                for g in range(2):
                    for s in range(SEQ):
                        to = o_full[s * L:(s + 1) * L, :].rearrange("p (k g r e) -> p k g r e", g=2, r=2, e=HD)[:, :, g]
                        last = dve.tensor_tensor(
                            to, o_blocks[g * L:(g + 1) * L, s, :, g, :, 0:HD],
                            inv_sum[a][g * L:(g + 1) * L, s, :, :, None].to_broadcast([L, PAIRS // 2, 2, HD]), ALU.mult)
                last.then_inc(o_made, 1)

            def statistics(t):
                a = t.slot(2)
                if isinstance(t.n, int) and t.n in FIRST_OF_PART:
                    part = FIRST_OF_PART.index(t.n)
                    dve.wait_ge(m.x_here[part], 16 * (GROUPS - X_PARTS[2] if part == 2 else 1))
                if not isinstance(t.n, int) or t.n:
                    dve.wait_ge(stats_made, t.n)
                reuse(dve, mean_made, t, 2)
                reuse(dve, x_hat_made, t, 4)
                dve.bn_stats(stats[a][:], t.rows(m.x_all).rearrange("p j n -> p (j n)")).then_inc(stats_made, 1)

            def aggregate(t):
                a = t.slot(2)
                if isinstance(t.n, int) and t.n == TILES - 1:
                    dve.wait_ge(stats_made, TILES)
                    dve.wait_ge(x_hat_made, TILES - 4)
                dve.bn_aggr(mean_var[t.slot(4)][:], stats[a][:]).then_inc(mean_made, 1)

            def qk_lo(t):
                a = t.slot(2)
                dve.wait_ge(qk_hi_made, t.n + 1)
                dve.tensor_tensor(qk_t[:, :, t.slot(4), LO].rearrange("p w c k -> p w (c k)"),
                                  ps_qkt[:, :].rearrange("p (w k) -> p w k", w=2),
                                  qk_t[:, :, t.slot(4), HI].rearrange("p w c k -> p w (c k)"), ALU.subtract).then_inc(qk_lo_made, 1)

            def hat(t):
                a = t.slot(2)
                dve.wait_ge(rstd_made, t.n + 1)
                reuse(dve, x_hat_t, t, 2)
                dve.tensor_scalar(x_hat[a][:, None, :], t.rows(m.x_all), mean_var[t.slot(4)][:, 0:1], rstd[t.slot(4)][:],
                                  ALU.subtract, ALU.mult).then_inc(x_hat_made, 1)

            def biases(t):
                a = t.slot(2)
                dve.wait_ge(qk_done, t.n + 1)
                reuse(dve, qk_hat_made, t, 2)
                dve.tensor_tensor(qk[a][:], ps_qk[:, :], m.b_qk[:], ALU.add).then_inc(qk_biased, 1)

            def clear_k(t):
                if isinstance(t.n, int) and t.n < 4:
                    dve.memset(k_pairs[:, t.n], 0.0).then_inc(k_cleared, 1)

            pipeline(dve, [(4, biases), (2, modulate), (4, v_low), (10, outputs), (4, reduce_norms),
                           (11, residual), (1, hat), (5, qk_lo), (-1, statistics), (6, place_v), (0, aggregate), (1, clear_k)])


def heads(a):
    return a.rearrange("p (h e) -> p h e", e=HD)


def over_channels(a):
    return a[:, :, None].to_broadcast([a.shape[0], a.shape[1], HD])


def flat(a):
    names = " ".join("abcdef"[:len(a.shape) - 1])
    return a.rearrange(f"p {names} -> p ({names})")


def by_seq(a, c, t, s):
    return a[:, c, :].rearrange("p (j k) -> p j k", k=UNROLL * SEQ)[:, bass.ds(t.j, 1), t.u * SEQ + s]


def feed_forward_pass(nc, m, fc2_w, wq, wk, wv, out_w):
    T = UNROLL
    BLOCKS = TILES // T
    F_CHUNKS = D_FF // P
    N = T * P
    with ExitStack() as ctx:
        def sb(name, shape, dt=F32, slots=2):
            return [ctx.enter_context(nc.sbuf_tensor(f"f_{name}{i}", shape, dt)) for i in range(slots)]

        def sem(name):
            return ctx.enter_context(nc.semaphore(f"f_{name}"))

        fc2_full = sb("fc2_full", [P, F_CHUNKS, C], F32, 1)[0]
        qvk3_full = fc2_full[:].rearrange("p f n -> p (f n)")[:, 0:NC_ * 3 * C].rearrange("p (c n) -> p c n", c=NC_)
        stats = sb("stats", [P, T, 6])
        mean_var = sb("mean_var", [P, T, 2])
        rstd = sb("rstd", [P, T])
        x_hat = sb("x_hat", [P, T, C])
        x2 = sb("x2", [P, NC_, N], F32, 1)[0]
        x2_split = sb("x2_split", [P, 2, NC_, N], BF16)
        h = sb("h", [P, N], F32, 4)
        h_split = sb("h_split", [P, 2, F_CHUNKS, N], BF16)
        gain = sb("gain", [P, T, C])
        branch = sb("branch", [P, T, C])
        ps_t = ctx.enter_context(nc.psum_tensor("f_ps_t", [P, NC_, N], F32))
        ps_h = [ctx.enter_context(nc.psum_tensor(f"f_ps_h{i}", [P, N], F32)) for i in range(4)]
        ps_y = ctx.enter_context(nc.psum_tensor("f_ps_y", [P, T, C], F32))

        gain_here = [sem(f"gain_here{i}") for i in range(2)]
        fc2_here = sem("fc2_here")
        qvk3_here = sem("qvk3_here")
        qvk3_hi_made = sem("qvk3_hi_made")
        w_hi_made = sem("w_hi_made")
        w_lo_made = sem("w_lo_made")
        stats_made = sem("stats_made")
        mean_made = sem("mean_made")
        var_eps_made = sem("var_eps_made")
        rstd_made = sem("rstd_made")
        x_hat_made = sem("x_hat_made")
        x_turned = sem("x_turned")
        x_scaled = sem("x_scaled")
        x2_made = sem("x2_made")
        x2_hi_made = sem("x2_hi_made")
        x2_lo_made = sem("x2_lo_made")
        fc1_done = sem("fc1_done")
        h_made = sem("h_made")
        h_lo_even = sem("h_lo_even")
        h_lo_odd = sem("h_lo_odd")
        fc2_done = sem("fc2_done")
        branch_made = sem("branch_made")
        branch_gained = sem("branch_gained")
        last_branch_made = sem("last_branch_made")
        last_branch_gained = sem("last_branch_gained")
        x_updated = sem("x_updated")
        block = ctx.enter_context(nc.Block())
        gamma2 = m.gammas.rearrange("(b u s) n -> s b u n", s=SEQ, u=T)

        def rows(t):
            return m.x_all[:, bass.ds(t.n, 1)].rearrange("p b u n -> p (b u) n")

        def by_block(a, t):
            a = a[:].rearrange("p c (b s) -> p c b s", s=T * SEQ)[:, :, bass.ds(t.n, 1), :]
            return a.rearrange("p c b s -> p c (b s)")[:, :, :, None].to_broadcast([P, NC_, T * SEQ, L])

        def run(eng, stages):
            pipeline(eng, stages, BLOCKS, 2, 2)

        @block.sync
        def _(sp):
            sp.dma_start(fc2_full[:], fc2_w.rearrange(CHUNKED, p=P)).then_inc(fc2_here, 16)
            sp.dma_start(m.w_out3[:], out_w.rearrange(CHUNKED, p=P)).then_inc(m.linear_here, 16)
            sp.wait_ge(w_lo_made, 1)
            for k, source in enumerate((wq, wv, wk)):
                sp.dma_start(qvk3_full[:, :, k * C:(k + 1) * C], source.rearrange(CHUNKED, p=P)).then_inc(qvk3_here, 16)
            sp.wait_ge(m.linear_here, 16 * 4)

        @block.gpsimd
        def _(pool):
            def shift(t):
                pool.wait_ge(x_scaled, t.n + 1)
                pool.tensor_tensor(x2[:].rearrange("p c (s l) -> p c s l", l=L),
                                   x2[:].rearrange("p c (s l) -> p c s l", l=L), by_block(m.shift2, t), ALU.add
                                   ).then_inc(x2_made, 1)

            def rstd_of(t):
                a = t.slot(2)
                reuse(pool, x_hat_made, t, 2, T)
                pool.wait_ge(mean_made, (t.n + 1) * T)
                pool.tensor_tensor(rstd[a][:], mean_var[a][:, :, 1], m.eps_ln[:].to_broadcast([P, T]), ALU.add
                                   ).then_inc(var_eps_made, 1)
                pool.wait_ge(var_eps_made, t.n + 1)
                pool.tensor_tensor(rstd[a][:], rstd[a][:], m.minus_half[:], ALU.pow).then_inc(rstd_made, 1)

            def update(t):
                if isinstance(t.n, int) and t.n == BLOCKS - 1:
                    return
                a = t.slot(2)
                pool.wait_ge(branch_made, t.n + 1)
                pool.wait_ge(gain_here[a], (t.j + 1) * 16 * SEQ)
                pool.tensor_tensor(branch[a][:], branch[a][:], gain[a][:], ALU.mult).then_inc(branch_gained, 1)

            def add(t):
                if isinstance(t.n, int) and t.n == BLOCKS - 1:
                    return
                a = t.slot(2)
                pool.wait_ge(branch_gained, t.n + 1)
                pool.tensor_tensor(rows(t), rows(t), branch[a][:], ALU.add).then_inc(x_updated, 1)

            def split_fc2(t):
                if isinstance(t.n, int) and t.n == 0:
                    pool.wait_ge(w_hi_made, 1)
                    pool.tensor_tensor(m.w_fc2[:, LO], fc2_full[:], m.w_fc2[:, HI], ALU.subtract).then_inc(w_lo_made, 1)

            def split_qvk3(t):
                if isinstance(t.n, int) and t.n == BLOCKS - 1:
                    pool.wait_ge(qvk3_hi_made, 1)
                    pool.tensor_tensor(m.w_qvk3[:, LO], qvk3_full, m.w_qvk3[:, HI], ALU.subtract)

            def h_low_odd(t):
                a = t.slot(2)
                for f in range(1, F_CHUNKS, 2):
                    pool.wait_ge(h_made, t.n * F_CHUNKS + f + 1)
                    pool.tensor_tensor(h_split[a][:, LO, f], h[f % 4][:], h_split[a][:, HI, f], ALU.subtract
                                       ).then_inc(h_lo_odd, 1)

            run(pool, [(2, shift), (2, split_fc2), (0, rstd_of), (5, update), (5, add), (3, h_low_odd),
                       (3, split_qvk3)])

        @block.scalar
        def _(act):
            def load_gain(t):
                a = t.slot(2)
                reuse(act, branch_gained, t, 2)
                for s in range(SEQ):
                    source = gamma2[s:s + 1, bass.ds(t.n, 1), :, C:2 * C].rearrange("s b u n -> (s b) u n")
                    act.dma_start(gain[a][s * L:(s + 1) * L], source.to_broadcast([L, T, C])
                                  ).then_inc(gain_here[a], 16)

            def split_fc2(t):
                if isinstance(t.n, int) and t.n == 0:
                    act.wait_ge(fc2_here, 16)
                    act.activation(m.w_fc2[:, HI], fc2_full[:], ACT.Copy).then_inc(w_hi_made, 1)

            def split_qvk3(t):
                if isinstance(t.n, int) and t.n == BLOCKS - 1:
                    act.wait_ge(qvk3_here, 16 * 3)
                    act.activation(m.w_qvk3[:, HI], qvk3_full, ACT.Copy).then_inc(qvk3_hi_made, 1)

            def x2_high(t):
                a = t.slot(2)
                act.wait_ge(x2_made, t.n + 1)
                reuse(act, fc1_done, t, 2, F_CHUNKS)
                act.activation(x2_split[a][:, HI], x2[:], ACT.Copy).then_inc(x2_hi_made, 1)

            def gelus(t):
                a = t.slot(2)
                reuse(act, fc2_done, t, 2, 2)
                for f in range(F_CHUNKS):
                    act.wait_ge(fc1_done, t.n * F_CHUNKS + f + 1)
                    if f >= 4 or not isinstance(t.n, int) or t.n > 0:
                        half_way = t.n * (F_CHUNKS // 2) + f // 2 - 1
                        act.wait_ge(h_lo_odd if f % 2 else h_lo_even, half_way)
                    act.activation(h_split[a][:, HI, f], ps_h[f % 4][:], ACT.Gelu, bias=m.b_fc1[:, f:f + 1])
                    act.activation(h[f % 4][:], ps_h[f % 4][:], ACT.Gelu, bias=m.b_fc1[:, f:f + 1]).then_inc(h_made, 1)

            run(act, [(0, split_fc2), (4, load_gain), (2, x2_high), (3, gelus), (3, split_qvk3)])

        @block.tensor
        def _(pe):
            def fc2(t, tiles):
                a = t.slot(2)
                pe.wait_ge(h_lo_even, (t.n + 1) * (F_CHUNKS // 2))
                pe.wait_ge(h_lo_odd, (t.n + 1) * (F_CHUNKS // 2))
                if isinstance(t.n, int) and t.n == 0:
                    pe.wait_ge(w_lo_made, 1)
                reuse(pe, branch_made, t, 1)
                for i in tiles:
                    for f in range(F_CHUNKS):
                        for k, (hs, ws) in enumerate(SPLITS):
                            last = pe.matmul(ps_y[:, i], h_split[a][:, hs, f, i * P:(i + 1) * P], m.w_fc2[:, ws, f],
                                             start=(f == 0 and k == 0), stop=(f == F_CHUNKS - 1 and k == 2))
                last.then_inc(fc2_done, 1)

            def fc2_first(t):
                fc2(t, range(T // 2))

            def fc2_second(t):
                fc2(t, range(T // 2, T))

            def turn_x(t):
                a = t.slot(2)
                pe.wait_ge(x_hat_made, (t.n + 1) * T)
                reuse(pe, x_scaled, t, 1)
                for i in range(T):
                    for c in range(NC_):
                        last = pe.transpose(ps_t[:, c, i * P:(i + 1) * P], x_hat[a][:, i, c * P:(c + 1) * P], m.ident[:])
                last.then_inc(x_turned, 1)

            def fc1(t, chunks):
                a = t.slot(2)
                pe.wait_ge(x2_lo_made, t.n + 1)
                for f in chunks:
                    if f >= 4 or not isinstance(t.n, int) or t.n > 0:
                        pe.wait_ge(h_made, t.n * F_CHUNKS + f - 3)
                    for k, (ws, xs) in enumerate(SPLITS):
                        for c in range(NC_):
                            last = pe.matmul(ps_h[f % 4][:], m.w_fc1[:, ws, c, f * P:(f + 1) * P], x2_split[a][:, xs, c],
                                             start=(k == 0 and c == 0), stop=(k == 2 and c == NC_ - 1))
                    last.then_inc(fc1_done, 1)

            def fc1_first(t):
                fc1(t, range(F_CHUNKS // 2))

            def fc1_second(t):
                fc1(t, range(F_CHUNKS // 2, F_CHUNKS))

            run(pe, [(3, fc1_first), (4, fc2_first), (3, fc1_second), (1, turn_x), (4, fc2_second)])

        @block.vector
        def _(dve):
            def scale(t):
                dve.wait_ge(x_turned, t.n + 1)
                reuse(dve, x2_hi_made, t, 1)
                reuse(dve, x2_lo_made, t, 1)
                dve.tensor_tensor(x2[:].rearrange("p c (s l) -> p c s l", l=L),
                                  ps_t[:].rearrange("p c (s l) -> p c s l", l=L), by_block(m.scale2, t), ALU.mult
                                  ).then_inc(x_scaled, 1)

            def hat(t):
                a = t.slot(2)
                dve.wait_ge(rstd_made, t.n + 1)
                reuse(dve, x_turned, t, 2)
                for i in range(T):
                    dve.tensor_scalar(x_hat[a][:, i], rows(t)[:, i], mean_var[a][:, i, 0:1], rstd[a][:, i:i + 1],
                                      ALU.subtract, ALU.mult).then_inc(x_hat_made, 1)

            def statistics(t):
                a = t.slot(2)
                if not isinstance(t.n, int) or t.n:
                    dve.wait_ge(stats_made, t.n * T)
                reuse(dve, x_hat_made, t, 2, T)
                for i in range(T):
                    dve.bn_stats(stats[a][:, i], rows(t)[:, i]).then_inc(stats_made, 1)

            def aggregate(t):
                a = t.slot(2)
                if isinstance(t.n, int) and t.n == BLOCKS - 1:
                    dve.wait_ge(stats_made, BLOCKS * T)
                    dve.wait_ge(x_hat_made, (BLOCKS - 2) * T)
                for i in range(T):
                    dve.bn_aggr(mean_var[a][:, i], stats[a][:, i]).then_inc(mean_made, 1)

            def x2_low(t):
                a = t.slot(2)
                dve.wait_ge(x2_hi_made, t.n + 1)
                reuse(dve, fc1_done, t, 2, F_CHUNKS)
                dve.tensor_tensor(x2_split[a][:, LO], x2[:], x2_split[a][:, HI], ALU.subtract).then_inc(x2_lo_made, 1)

            def last_residual(t):
                if not (isinstance(t.n, int) and t.n == BLOCKS - 1):
                    return
                a = t.slot(2)
                reuse(dve, x_updated, t, 2)
                dve.wait_ge(gain_here[a], (t.j + 1) * 16 * SEQ)
                for k in range(2):
                    half = slice(k * T // 2, (k + 1) * T // 2)
                    dve.wait_ge(fc2_done, t.n * 2 + k + 1)
                    dve.tensor_tensor(branch[a][:, half], ps_y[:, half], m.b_fc2[:, None, :].to_broadcast([P, T // 2, C]),
                                      ALU.add).then_inc(last_branch_made, 1)
                    dve.wait_ge(last_branch_made, k + 1)
                    dve.tensor_tensor(branch[a][:, half], branch[a][:, half], gain[a][:, half], ALU.mult
                                      ).then_inc(last_branch_gained, 1)
                    dve.wait_ge(last_branch_gained, k + 1)
                    dve.tensor_tensor(rows(t)[:, half], rows(t)[:, half], branch[a][:, half], ALU.add)

            def residual(t):
                if isinstance(t.n, int) and t.n == BLOCKS - 1:
                    return
                a = t.slot(2)
                dve.wait_ge(fc2_done, (t.n + 1) * 2)
                reuse(dve, x_updated, t, 2)
                dve.tensor_tensor(branch[a][:], ps_y[:], m.b_fc2[:, None, :].to_broadcast([P, T, C]), ALU.add
                                  ).then_inc(branch_made, 1)

            def h_low_even(t):
                a = t.slot(2)
                reuse(dve, fc2_done, t, 2, 2)
                for f in range(0, F_CHUNKS, 2):
                    dve.wait_ge(h_made, t.n * F_CHUNKS + f + 1)
                    dve.tensor_tensor(h_split[a][:, LO, f], h[f % 4][:], h_split[a][:, HI, f], ALU.subtract
                                      ).then_inc(h_lo_even, 1)

            run(dve, [(2, scale), (1, hat), (-1, statistics), (0, aggregate), (2, x2_low), (3, h_low_even),
                      (4, residual), (4, last_residual)])


def linear_pass(nc, m, cond, out):
    Y_LAG = 8
    Y_GAP = Y_LAG + 1
    NK = NC_ * SEQ
    with ExitStack() as ctx:
        def sb(name, shape, dt=F32, slots=2):
            return [ctx.enter_context(nc.sbuf_tensor(f"l_{name}{i}", shape, dt)) for i in range(slots)]

        def ps(name, shape):
            return ctx.enter_context(nc.psum_tensor(f"l_{name}", shape, F32))

        def sem(name):
            return ctx.enter_context(nc.semaphore(f"l_{name}"))

        stats = sb("stats", [P, 6])
        mean_var = sb("mean_var", [P, 2, 2])
        rstd = sb("rstd", [P, 2])
        x_hat = sb("x_hat", [P, C])
        x3_t = sb("x3_t", [P, NC_, P])
        x3_split = sb("x3_split", [P, 2, NC_, P], BF16)
        kq = sb("kq", [P, 2 * C], F32, 4)
        k_tops = sb("k_tops", [P, NC_, SEQ])
        k_shift = sb("k_shift", [P, NC_, SEQ])
        q_tops = sb("q_tops", [P, H])
        sums = sb("sums", [P, NK + H], F32, 4)
        v_split = sb("v_split", [P, 2, C], BF16, 4)
        kq_t = sb("kq_t", [P, 2, 2 * C], BF16, 4)
        kv = sb("kv", [P, NC_, SEQ, P])
        kv_split = sb("kv_split", [P, 2, NC_, SEQ, P], BF16)
        y_stats = sb("y_stats", [P, 6])
        y_hat = sb("y_hat", [P, C])
        z_t = sb("z_t", [P, NC_, P])
        tanh = sb("tanh", [P, NC_, P])
        silu = sb("silu", [P, NC_, P])
        gate = sb("gate", [P, C], F32, 4)
        branch = sb("branch", [P, C])
        ps_xt = ps("ps_xt", [P, NC_, P])
        ps_qv = ps("ps_qv", [P, 2 * C])
        ps_k = ps("ps_k", [P, NC_, P])
        ps_kq = ps("ps_kq", [P, 2 * C])
        ps_kv = ps("ps_kv", [P, NC_, SEQ, P])
        ps_y = ps("ps_y", [P, C])
        ps_yt = ps("ps_yt", [P, NC_, P])
        ps_out = ps("ps_out", [P, C])

        gate_here = [sem(f"gate_here{i}") for i in range(4)]
        stats_made = sem("stats_made")
        mean_made = sem("mean_made")
        var_eps_made = sem("var_eps_made")
        rstd_made = sem("rstd_made")
        x_hat_made = sem("x_hat_made")
        x_turned = sem("x_turned")
        x3_made = sem("x3_made")
        x3_hi_made = sem("x3_hi_made")
        x3_lo_made = sem("x3_lo_made")
        k_done = sem("k_done")
        qv_done = sem("qv_done")
        k_top_found = sem("k_top_found")
        k_top_biased = sem("k_top_biased")
        k_shift_made = sem("k_shift_made")
        k_exp_made = sem("k_exp_made")
        v_hi_made = sem("v_hi_made")
        v_lo_made = sem("v_lo_made")
        tops_made = sem("tops_made")
        q_lowered = sem("q_lowered")
        q_exp_made = sem("q_exp_made")
        sums_made = sem("sums_made")
        sums_inverted = sem("sums_inverted")
        softmax_made = sem("softmax_made")
        kq_turned = sem("kq_turned")
        kq_hi_made = sem("kq_hi_made")
        kq_lo_made = sem("kq_lo_made")
        kv_first = sem("kv_first")
        kv_done = sem("kv_done")
        kv_masked = sem("kv_masked")
        kv_hi_made = sem("kv_hi_made")
        kv_lo_made = sem("kv_lo_made")
        y_done = sem("y_done")
        y_stats_made = sem("y_stats_made")
        y_mean_made = sem("y_mean_made")
        y_hat_made = sem("y_hat_made")
        y_turned = sem("y_turned")
        z_made = sem("z_made")
        tanh_made = sem("tanh_made")
        silu_product = sem("silu_product")
        silu_made = sem("silu_made")
        out_done = sem("out_done")
        branch_made = sem("branch_made")
        x_updated = sem("x_updated")
        stored = sem("stored")
        block = ctx.enter_context(nc.Block())
        gates = cond.rearrange("(j u s) n -> s j u n", s=SEQ, u=UNROLL)

        def k_of(a):
            return a[:, 0:C].rearrange("p (k l) -> p k l", l=L)

        def q_of(a):
            return a[:, C:2 * C].rearrange("p (h e) -> p h e", e=HD)

        def by_token(a):
            return a[:, :, None].to_broadcast([P, NK, L])

        def by_seq_over_tokens(a, t):
            a = a[:].rearrange("p c (j u s) -> p c j u s", u=UNROLL, s=SEQ)[:, :, bass.ds(t.j, 1), t.u, :]
            return a.rearrange("p c j s -> p c (j s)")[:, :, :, None].to_broadcast([P, NC_, SEQ, L])

        def tokens_by_seq(a):
            return a.rearrange("p c (s l) -> p c s l", l=L)

        @block.sync
        def _(sp):
            sp.wait_ge(stored, 16 * GROUPS)

        @block.gpsimd
        def _(pool):
            def add(t):
                a = t.slot(2)
                pool.wait_ge(branch_made, t.n + 1)
                pool.tensor_tensor(t.rows(m.x_all), t.rows(m.x_all), branch[a][:, None, :], ALU.add
                                   ).then_inc(x_updated, 1)

            def silus(t):
                a = t.slot(2)
                pool.wait_ge(tanh_made, t.n + 1)
                reuse(pool, out_done, t, 2)
                pool.tensor_tensor(silu[a][:], tanh[a][:], z_t[a][:], ALU.mult).then_inc(silu_product, 1)
                pool.wait_ge(silu_product, t.n + 1)
                pool.tensor_tensor(silu[a][:], silu[a][:], z_t[a][:], ALU.add).then_inc(silu_made, 1)

            def kv_low(t):
                a = t.slot(2)
                pool.wait_ge(kv_hi_made, t.n + 1)
                reuse(pool, y_done, t, 2)
                pool.tensor_tensor(kv_split[a][:, LO], kv[a][:], kv_split[a][:, HI], ALU.subtract
                                   ).then_inc(kv_lo_made, 1)

            def softmax(t):
                a = t.slot(2)
                pool.wait_ge(sums_inverted, t.n + 1)
                pool.tensor_tensor(k_of(kq[t.slot(4)]), k_of(kq[t.slot(4)]), by_token(sums[t.slot(4)][:, 0:NK]), ALU.mult
                                   ).then_inc(softmax_made, 1)
                pool.tensor_tensor(q_of(kq[t.slot(4)]), q_of(kq[t.slot(4)]), over_channels(sums[t.slot(4)][:, NK:]), ALU.mult
                                   ).then_inc(softmax_made, 1)

            def inverse_deviations(t):
                a = t.slot(2)
                first = isinstance(t.n, int) and t.n < Y_GAP
                pool.wait_ge(mean_made, t.n + 1)
                reuse(pool, x_hat_made, t, 2)
                if not first:
                    pool.wait_ge(y_mean_made, t.n + 1 - Y_GAP)
                power(a, slice(0, 1 if first else 2), t.n + 1)

            def last_inverse_deviations(t):
                if isinstance(t.n, int) and t.n + Y_GAP >= TILES:
                    pool.wait_ge(y_mean_made, t.n + 1)
                    reuse(pool, y_hat_made, t, 2)
                    power((t.n + Y_GAP) % 2, slice(1, 2), t.n + Y_GAP + 1)

            def power(a, which, nth):
                width = which.stop - which.start
                pool.tensor_tensor(rstd[a][:, which], mean_var[a][:, which, 1], m.eps_norm3[:].to_broadcast([P, width]),
                                   ALU.add).then_inc(var_eps_made, 1)
                pool.wait_ge(var_eps_made, nth)
                pool.tensor_tensor(rstd[a][:, which], rstd[a][:, which], m.minus_half[:, 0:width], ALU.pow
                                   ).then_inc(rstd_made, 1)

            pipeline(pool, [(5, softmax), (7, kv_low), (-1, inverse_deviations), (Y_LAG, last_inverse_deviations),
                            (10, silus), (12, add)])

        @block.scalar
        def _(act):
            def load_gate(t):
                reuse(act, branch_made, t, 4)
                for s in range(SEQ):
                    source = gates[s:s + 1, bass.ds(t.j, 1), t.u, :].rearrange("s j n -> (s j) n")
                    act.dma_start(gate[t.slot(4)][s * L:(s + 1) * L], source.to_broadcast([L, C])
                                  ).then_inc(gate_here[t.slot(4)], 16)

            def store(t):
                if t.u == UNROLL - 1:
                    act.wait_ge(x_updated, t.n + 1)
                    act.dma_start(x_tiles(out)[:, bass.ds(t.j, 1)], m.x_all[:, bass.ds(t.j, 1)]).then_inc(stored, 16)

            def modulate(t):
                a = t.slot(2)
                act.wait_ge(y_turned, t.n + 1)
                reuse(act, silu_made, t, 2)
                for c in range(NC_):
                    for s in range(SEQ):
                        act.activation(z_t[a][:, c, s * L:(s + 1) * L], ps_yt[:, c, s * L:(s + 1) * L], ACT.Identity,
                                       bias=by_seq(m.shift3, c, t, s), scale=by_seq(m.scale3, c, t, s)
                                       ).then_inc(z_made, 1)

            def tanhs(t):
                a = t.slot(2)
                act.wait_ge(z_made, (t.n + 1) * NK)
                act.activation(tanh[a][:], z_t[a][:], ACT.Tanh).then_inc(tanh_made, 1)

            def kv_high(t):
                a = t.slot(2)
                act.wait_ge(kv_masked, t.n + 1)
                reuse(act, y_done, t, 2)
                act.activation(kv_split[a][:, HI], kv[a][:], ACT.Copy).then_inc(kv_hi_made, 1)

            def kq_high(t):
                a = t.slot(2)
                act.wait_ge(kq_turned, t.n + 1)
                reuse(act, y_done, t, 4)
                act.activation(kq_t[t.slot(4)][:, HI], ps_kq[:], ACT.Copy).then_inc(kq_hi_made, 1)

            def q_exponentials(t):
                act.wait_ge(q_lowered, t.n + 1)
                act.activation(kq[t.slot(4)][:, C:2 * C], kq[t.slot(4)][:, C:2 * C], ACT.Exp).then_inc(q_exp_made, 1)

            def k_exponentials(t):
                a = t.slot(2)
                act.wait_ge(k_shift_made, t.n + 1)
                reuse(act, kq_turned, t, 4)
                for c in range(NC_):
                    for s in range(SEQ):
                        i = c * SEQ + s
                        act.activation(kq[t.slot(4)][:, i * L:(i + 1) * L], ps_k[:, c, s * L:(s + 1) * L], ACT.Exp,
                                       bias=k_shift[a][:, c, s:s + 1], accum_out=sums[t.slot(4)][:, i:i + 1]
                                       ).then_inc(k_exp_made, 1)

            def v_high(t):
                a = t.slot(2)
                act.wait_ge(qv_done, t.n + 1)
                reuse(act, kv_done, t, 4)
                act.activation(v_split[t.slot(4)][:, HI], ps_qv[:, C:2 * C], ACT.Copy).then_inc(v_hi_made, 1)

            def affine(t):
                a = t.slot(2)
                act.wait_ge(x_turned, t.n + 1)
                reuse(act, x3_lo_made, t, 2)
                for c in range(NC_):
                    act.activation(x3_t[a][:, c], ps_xt[:, c], ACT.Identity, bias=m.b_norm3[:, c:c + 1],
                                   scale=m.g_norm3[:, c:c + 1]).then_inc(x3_made, 1)

            def x3_high(t):
                a = t.slot(2)
                act.wait_ge(x3_made, (t.n + 1) * NC_)
                reuse(act, k_done, t, 2)
                act.activation(x3_split[a][:, HI], x3_t[a][:], ACT.Copy).then_inc(x3_hi_made, 1)

            pipeline(act, [(3, v_high), (1, affine), (9, load_gate), (1, x3_high), (5, kq_high),
                           (3, k_exponentials), (9, modulate), (3, q_exponentials), (6, kv_high), (13, store),
                           (9, tanhs)])

        @block.tensor
        def _(pe):
            def project(t):
                a = t.slot(2)
                pe.wait_ge(silu_made, t.n + 1)
                reuse(pe, branch_made, t, 1)
                pe.matmul(ps_out[:], m.ones[:], m.rows_out3, start=True, stop=False)
                for c in range(NC_):
                    last = pe.matmul(ps_out[:], silu[a][:, c], m.w_out3[:, c], start=False, stop=(c == NC_ - 1))
                last.then_inc(out_done, 1)

            def turn_y(t):
                a = t.slot(2)
                pe.wait_ge(y_hat_made, t.n + 1)
                reuse(pe, z_made, t, 1, NK)
                for c in range(NC_):
                    last = pe.transpose(ps_yt[:, c], y_hat[a][:, c * P:(c + 1) * P], m.ident[:])
                last.then_inc(y_turned, 1)

            def q_kv(t):
                a = t.slot(2)
                pe.wait_ge(kv_lo_made, t.n + 1)
                reuse(pe, y_hat_made, t, 1)
                for s in range(SEQ):
                    for c in range(NC_):
                        q_cols = C + c * P + s * L
                        for i, (q, w) in enumerate(SPLITS):
                            last = pe.matmul(ps_y[s * L:(s + 1) * L, c * P:(c + 1) * P],
                                             kq_t[t.slot(4)][:, q, q_cols:q_cols + L], kv_split[a][:, w, c, s],
                                             start=(i == 0), stop=(i == 2))
                last.then_inc(y_done, 1)

            def k_v(t):
                a = t.slot(2)
                pe.wait_ge(kq_lo_made, t.n + 1)
                pe.wait_ge(v_lo_made, t.n + 1)
                reuse(pe, kv_masked, t, 1)
                for s in range(SEQ):
                    own = slice(s * L, (s + 1) * L)
                    for c in range(NC_):
                        chans = slice(c * P, (c + 1) * P)
                        for i, (k, v) in enumerate(SPLITS):
                            last = pe.matmul(ps_kv[:, c, s], kq_t[t.slot(4)][own, k, chans], v_split[t.slot(4)][own, v, chans],
                                             start=(i == 0), stop=(i == 2))
                    if s < SEQ - 1:
                        last.then_inc(kv_first, 1)
                        pe.wait_ge(kv_first, t.n + 1)
                last.then_inc(kv_done, 1)

            def turn_kq(t):
                a = t.slot(2)
                pe.wait_ge(softmax_made, (t.n + 1) * 2)
                reuse(pe, kq_lo_made, t, 1)
                for k in range(2 * NC_):
                    last = pe.transpose(ps_kq[:, k * P:(k + 1) * P], kq[t.slot(4)][:, k * P:(k + 1) * P], m.ident[:])
                last.then_inc(kq_turned, 1)

            def qkv(t):
                a = t.slot(2)
                pe.wait_ge(x3_lo_made, t.n + 1)
                reuse(pe, v_lo_made, t, 1)
                pe.matmul(ps_qv[:], m.ones[:], m.rows_qv3, start=True, stop=False)
                for i, (xs, ws) in enumerate(SPLITS):
                    for c in range(NC_):
                        last = pe.matmul(ps_qv[:], x3_split[a][:, xs, c], m.w_qvk3[:, ws, c, 0:2 * C],
                                         start=False, stop=(i == 2 and c == NC_ - 1))
                last.then_inc(qv_done, 1)
                reuse(pe, k_exp_made, t, 1, NK)
                for to in range(NC_):
                    cols = slice(2 * C + to * P, 2 * C + (to + 1) * P)
                    for i, (ws, xs) in enumerate(SPLITS):
                        for c in range(NC_):
                            last = pe.matmul(ps_k[:, to], m.w_qvk3[:, ws, c, cols], x3_split[a][:, xs, c],
                                             start=(i == 0 and c == 0), stop=(i == 2 and c == NC_ - 1))
                last.then_inc(k_done, 1)

            def turn_x(t):
                a = t.slot(2)
                pe.wait_ge(x_hat_made, t.n + 1)
                reuse(pe, x3_made, t, 1, NC_)
                for c in range(NC_):
                    last = pe.transpose(ps_xt[:, c], x_hat[a][:, c * P:(c + 1) * P], m.ident[:])
                last.then_inc(x_turned, 1)

            pipeline(pe, [(6, k_v), (5, turn_kq), (0, turn_x), (11, project), (2, qkv), (7, q_kv),
                          (Y_LAG, turn_y)])

        @block.vector
        def _(dve):
            def residual(t):
                a = t.slot(2)
                dve.wait_ge(out_done, t.n + 1)
                reuse(dve, x_updated, t, 2)
                dve.wait_ge(gate_here[t.slot(4)], (t.j + 1) * 16 * SEQ)
                dve.tensor_tensor(branch[a][:], ps_out[:], gate[t.slot(4)][:], ALU.mult).then_inc(branch_made, 1)

            def y_statistics(t):
                a = t.slot(2)
                dve.wait_ge(y_done, t.n + 1)
                reuse(dve, y_hat_made, t, 2)
                dve.bn_stats(y_stats[a][:], ps_y[:]).then_inc(y_stats_made, 1)

            def y_aggregate(t):
                a = t.slot(2)
                if isinstance(t.n, int):
                    dve.wait_ge(y_stats_made, t.n + 1)
                dve.bn_aggr(mean_var[1 - a][:, 1], y_stats[a][:]).then_inc(y_mean_made, 1)

            def y_hats(t):
                a = t.slot(2)
                dve.wait_ge(rstd_made, t.n + Y_GAP + 1)
                reuse(dve, y_turned, t, 2)
                dve.tensor_scalar(y_hat[a][:], ps_y[:], mean_var[1 - a][:, 1, 0:1], rstd[1 - a][:, 1:2], ALU.subtract, ALU.mult
                                  ).then_inc(y_hat_made, 1)

            def mask(t):
                a = t.slot(2)
                dve.wait_ge(kv_done, t.n + 1)
                reuse(dve, kv_lo_made, t, 2)
                dve.tensor_tensor(kv[a][:].rearrange("p c s l -> p (c s) l"), ps_kv[:].rearrange("p c s l -> p (c s) l"),
                                  m.same_head[:, None, :].to_broadcast([P, NC_ * SEQ, P]), ALU.mult
                                  ).then_inc(kv_masked, 1)

            def kq_low(t):
                a = t.slot(2)
                dve.wait_ge(kq_hi_made, t.n + 1)
                dve.tensor_tensor(kq_t[t.slot(4)][:, LO], ps_kq[:], kq_t[t.slot(4)][:, HI], ALU.subtract).then_inc(kq_lo_made, 1)

            def total(t):
                dve.wait_ge(q_exp_made, t.n + 1)
                dve.wait_ge(k_exp_made, (t.n + 1) * NK)
                dve.tensor_reduce(sums[t.slot(4)][:, NK:], q_of(kq[t.slot(4)]), X_AXIS, ALU.add).then_inc(sums_made, 1)
                dve.wait_ge(sums_made, t.n + 1)
                dve.reciprocal(sums[t.slot(4)][:], sums[t.slot(4)][:]).then_inc(sums_inverted, 1)

            def k_maxima(t):
                a = t.slot(2)
                dve.wait_ge(k_done, t.n + 1)
                dve.tensor_reduce(k_tops[a][:].rearrange("p c s -> p (c s)"),
                                  ps_k[:].rearrange("p c (s l) -> p (c s) l", l=L), X_AXIS, ALU.max
                                  ).then_inc(k_top_found, 1)

            def k_top_bias(t):
                a = t.slot(2)
                dve.wait_ge(k_top_found, t.n + 1)
                dve.tensor_tensor(k_tops[a][:], k_tops[a][:], k_bias, ALU.add).then_inc(k_top_biased, 1)

            def k_shifts(t):
                a = t.slot(2)
                dve.wait_ge(k_top_biased, t.n + 1)
                reuse(dve, k_exp_made, t, 2, NK)
                if not isinstance(t.n, int):
                    dve.wait_ge(y_stats_made, t.n + 4 - Y_LAG)
                dve.tensor_tensor(k_shift[a][:], k_bias, k_tops[a][:], ALU.subtract).then_inc(k_shift_made, 1)

            def q_maxima(t):
                a = t.slot(2)
                dve.wait_ge(v_hi_made, t.n + 1)
                reuse(dve, q_lowered, t, 2)
                dve.tensor_reduce(q_tops[a][:], ps_qv[:, 0:C].rearrange("p (h e) -> p h e", e=HD), X_AXIS, ALU.max
                                  ).then_inc(tops_made, 1)

            def q_lower(t):
                a = t.slot(2)
                dve.wait_ge(tops_made, t.n + 1)
                reuse(dve, kq_turned, t, 4)
                dve.tensor_tensor(q_of(kq[t.slot(4)]), ps_qv[:, 0:C].rearrange("p (h e) -> p h e", e=HD),
                                  over_channels(q_tops[a][:]), ALU.subtract).then_inc(q_lowered, 1)

            def v_low(t):
                reuse(dve, kv_done, t, 4)
                dve.tensor_tensor(v_split[t.slot(4)][:, LO], ps_qv[:, C:2 * C], v_split[t.slot(4)][:, HI],
                                  ALU.subtract).then_inc(v_lo_made, 1)

            def statistics(t):
                a = t.slot(2)
                if not isinstance(t.n, int) or t.n:
                    dve.wait_ge(stats_made, t.n)
                reuse(dve, x_hat_made, t, 2)
                dve.bn_stats(stats[a][:], t.rows(m.x_all).rearrange("p j n -> p (j n)")).then_inc(stats_made, 1)

            def aggregate(t):
                a = t.slot(2)
                if isinstance(t.n, int) and t.n == TILES - 1:
                    dve.wait_ge(stats_made, TILES)
                    dve.wait_ge(x_hat_made, TILES - 2)
                dve.bn_aggr(mean_var[a][:, 0], stats[a][:]).then_inc(mean_made, 1)

            def hat(t):
                a = t.slot(2)
                dve.wait_ge(rstd_made, t.n + 1)
                reuse(dve, x_turned, t, 2)
                dve.tensor_scalar(x_hat[a][:, None, :], t.rows(m.x_all), mean_var[a][:, 0, 0:1], rstd[a][:, 0:1],
                                  ALU.subtract, ALU.mult).then_inc(x_hat_made, 1)

            k_bias = m.b_k3[:, :, None].to_broadcast([P, NC_, SEQ])
            def x3_low(t):
                a = t.slot(2)
                dve.wait_ge(x3_hi_made, t.n + 1)
                reuse(dve, k_done, t, 2)
                dve.tensor_tensor(x3_split[a][:, LO], x3_t[a][:], x3_split[a][:, HI], ALU.subtract).then_inc(x3_lo_made, 1)

            pipeline(dve, [(-2, statistics), (3, k_maxima), (Y_LAG, y_statistics), (3, q_maxima), (3, k_top_bias),
                           (-1, aggregate), (3, q_lower), (3, v_low), (3, k_shifts), (Y_LAG, y_aggregate),
                           (6, mask), (5, kq_low), (-1, hat), (4, total), (Y_LAG, y_hats), (1, x3_low),
                           (11, residual)])



_INS = ["x", "cond_1024", "L0_cond_mat_qkv_w", "L0_cond_q_bias", "L0_cond_v_bias", "L0_cond_scale_mul",
        "L0_cond_proj_w", "L0_cond_proj_b", "L0_cond_ada_w", "L0_cond_ada_b", "L0_cond_fc1_w", "L0_cond_fc1_b",
        "L0_cond_fc2_w", "L0_cond_fc2_b", "L1_cond_norm_g", "L1_cond_norm_b", "L1_cond_Wq", "L1_cond_bq",
        "L1_cond_Wk", "L1_cond_bk", "L1_cond_Wv", "L1_cond_bv", "L1_cond_emb_W", "L1_cond_emb_b",
        "L1_cond_sn_g", "L1_cond_sn_b", "L1_cond_out_W", "L1_cond_out_b"]
_TURNED = {"L0_cond_mat_qkv_w", "L0_cond_proj_w", "L0_cond_ada_w", "L0_cond_fc1_w", "L0_cond_fc2_w"}


def kernel(**inputs):
    import concourse.bacc as bacc
    from concourse.bass_utils import run_bass_kernel_spmd

    nc = bacc.Bacc("TRN2", target_bir_lowering=False, num_devices=1)
    arrays, args = {}, []
    for name in _INS:
        a = np.asarray(inputs[name])
        a = np.ascontiguousarray(a.T if name in _TURNED else a)
        arrays[f"in_{name}"] = a
        args.append(nc.dram_tensor(f"in_{name}", a.shape, mybir.dt.from_np(a.dtype), kind="ExternalInput").ap())
    args.append(nc.dram_tensor("out_0", (B, L, C), F32, kind="ExternalOutput").ap())
    condition_kernel(nc, *args)
    r = run_bass_kernel_spmd(nc, [arrays], core_ids=[0])
    return r.results[0]["out_0"]
```
